# Optimizing a Trainium2 kernel written in Bass

```python
import numpy as np
import jax
import jax.numpy as jnp

def _softmax(x, axis=-1):
    return jax.nn.softmax(x, axis=axis)

def _gelu(x):
    return jax.nn.gelu(x, approximate=True)

def _silu(x):
    return jax.nn.silu(x)

def _sigmoid(x):
    return jax.nn.sigmoid(x)

def _layernorm(x, axis=-1, eps=1e-05):
    m = jnp.mean(x, axis=axis, keepdims=True)
    v = jnp.var(x, axis=axis, keepdims=True)
    return (x - m) / jnp.sqrt(v + eps)

def _scatter_add(tgt, idx, src, axis=0):
    return tgt.at[idx].add(src)

def _segment_sum(src, seg, n):
    return jax.ops.segment_sum(src, seg, n)
kernel_name = 'mk_gps_d1_gnn_r8_99052b'

def setup_inputs(seed: int=0):
    np.random.seed(seed)
    _w = jnp.asarray

    def _rec_inputs():
        import jax
        import jax.numpy as jnp
        _gk = jax.random.key(seed)
        x = -7.329e-05 + 0.9999 * jax.random.normal(jax.random.fold_in(_gk, 1), (1250, 1024), jnp.float32)
        _s = jax.random.randint(jax.random.fold_in(_gk, 2), (20000,), 0, 1250, jnp.int32)
        _d = jax.random.randint(jax.random.fold_in(_gk, 3), (20000,), 0, 1250, jnp.int32)
        _loop = jnp.arange(1250, dtype=jnp.int32)
        src = jnp.concatenate([_s, _d, _loop])
        dst = jnp.concatenate([_d, _s, _loop])
        _o = jnp.argsort(dst, stable=True)
        src = src[_o]
        dst = dst[_o]
        edge_weight = -0.000130211 + 0.031236 * jax.random.normal(jax.random.fold_in(_gk, 12), (41250,), jnp.float32)
        return (x, src, dst, edge_weight)
    x, src, dst, edge_weight = _rec_inputs()

    def _L0_gnn_setup():
        import jax, jax.numpy as jnp
        import numpy as np
        INDIM = 1024
        OUTDIM = 1024
        NNZ = 8192
        N = 6250
        key = jax.random.key(seed)
        k1, k2, k3, k4, k5 = jax.random.split(key, 5)
        x = jax.random.normal(k1, (N, INDIM), dtype=jnp.float32)
        stdv = np.sqrt(6.0 / (INDIM + OUTDIM))
        nnz_weight = jax.random.uniform(k2, (NNZ,), dtype=jnp.float32, minval=-stdv, maxval=stdv)
        bias = jax.random.normal(k3, (OUTDIM,), dtype=jnp.float32) * 0.02
        row = jax.random.randint(k4, (NNZ,), 0, OUTDIM, dtype=jnp.int64)
        col = jax.random.randint(k5, (NNZ,), 0, INDIM, dtype=jnp.int64)
        edge_index = jnp.stack([row, col])
        return {'x': x, 'nnz_weight': nnz_weight, 'bias': bias, 'edge_index': edge_index}
    _L0_gnn_all = _L0_gnn_setup()
    _L0_gnn_in = {k: v for k, v in _L0_gnn_all.items() if k in ('bias',)}
    del _L0_gnn_all

    def _L0_mix_setup():
        import jax, jax.numpy as jnp
        import numpy as np
        DIM = 1024
        HEADS = 16
        DHEAD = DIM // HEADS
        EPS_NORM = 1e-06
        EPS_DEN = 1e-06

        def rmsnorm(x, w):
            xf = x.astype(jnp.float32)
            return (w * xf * jax.lax.rsqrt(jnp.mean(xf * xf, axis=-1, keepdims=True) + EPS_NORM)).astype(x.dtype)
        key = jax.random.key(seed)
        ks = jax.random.split(key, 6)
        b, n = (4, 512)
        x = jax.random.normal(ks[0], (b, n, DIM), dtype=jnp.float32)
        W_qkv = jax.random.normal(ks[1], (DIM, 3 * DIM), dtype=jnp.float32) * DIM ** (-0.5)
        qn_w = jnp.ones((DIM,), dtype=jnp.float32)
        kn_w = jnp.ones((DIM,), dtype=jnp.float32)
        W_out = jax.random.normal(ks[2], (DIM, DIM), dtype=jnp.float32) * DIM ** (-0.5)
        b_out = jnp.zeros((DIM,), dtype=jnp.float32)
        return {'x': x, 'W_qkv': W_qkv, 'qn_w': qn_w, 'kn_w': kn_w, 'W_out': W_out, 'b_out': b_out}
    _L0_mix_all = _L0_mix_setup()
    _L0_mix_in = {k: v for k, v in _L0_mix_all.items() if k in ('W_qkv', 'qn_w', 'kn_w', 'W_out', 'b_out')}
    del _L0_mix_all

    def _L0_ffn_setup():
        import jax, jax.numpy as jnp
        import numpy as np
        B, S, D = (1, 256, 1024)
        I = 256
        E = 8
        K = 2
        LIMIT = 7.0
        ALPHA = 1.702
        EPS = 1e-05

        def _swiglu(h):
            x_glu = jnp.minimum(h[..., ::2], LIMIT)
            x_lin = jnp.clip(h[..., 1::2], -LIMIT, LIMIT)
            return x_glu * jax.nn.sigmoid(ALPHA * x_glu) * (x_lin + 1.0)

        def _moe(t, gate_w, gate_b, mlp1_w, mlp1_b, mlp2_w, mlp2_b):
            T = t.shape[0]
            logits = t @ gate_w + gate_b
            top_v, top_i = jax.lax.top_k(logits, K)
            probs = jax.nn.softmax(top_v, axis=-1)
            w = jnp.zeros((T, E), t.dtype).at[jnp.arange(T)[:, None], top_i].set(probs)

            def body(acc, ew):
                w1, b1, w2, b2, we = ew
                h = _swiglu(t @ w1 + b1)
                y = h @ w2 + b2
                return (acc + we[:, None] * y, None)
            acc0 = jnp.zeros((T, t.shape[1]), t.dtype)
            acc, _ = jax.lax.scan(body, acc0, (mlp1_w, mlp1_b, mlp2_w, mlp2_b, w.T))
            return acc
        key = jax.random.key(seed)
        ks = jax.random.split(key, 4)
        s = 0.02
        return {'x': jax.random.normal(ks[0], (B, S, D), jnp.float32), 'norm_scale': jnp.ones((D,), jnp.float32), 'gate_w': jax.random.normal(ks[1], (D, E), jnp.float32) * s, 'gate_b': jnp.zeros((E,), jnp.float32), 'mlp1_w': jax.random.normal(ks[2], (E, D, 2 * I), jnp.float32) * s, 'mlp1_b': jnp.zeros((E, 2 * I), jnp.float32), 'mlp2_w': jax.random.normal(ks[3], (E, I, D), jnp.float32) * s, 'mlp2_b': jnp.zeros((E, D), jnp.float32)}
    _L0_ffn_all = _L0_ffn_setup()
    _L0_ffn_in = {k: v for k, v in _L0_ffn_all.items() if k in ('norm_scale', 'gate_w', 'gate_b', 'mlp1_w', 'mlp1_b', 'mlp2_w', 'mlp2_b')}
    del _L0_ffn_all
    return {'x': x, 'src': src, 'dst': dst, 'edge_weight': edge_weight, 'L0_gnn_bias': _L0_gnn_in['bias'], 'L0_mix_W_qkv': _L0_mix_in['W_qkv'], 'L0_mix_qn_w': _L0_mix_in['qn_w'], 'L0_mix_kn_w': _L0_mix_in['kn_w'], 'L0_mix_W_out': _L0_mix_in['W_out'], 'L0_mix_b_out': _L0_mix_in['b_out'], 'L0_ffn_norm_scale': _L0_ffn_in['norm_scale'], 'L0_ffn_gate_w': _L0_ffn_in['gate_w'], 'L0_ffn_gate_b': _L0_ffn_in['gate_b'], 'L0_ffn_mlp1_w': _L0_ffn_in['mlp1_w'], 'L0_ffn_mlp1_b': _L0_ffn_in['mlp1_b'], 'L0_ffn_mlp2_w': _L0_ffn_in['mlp2_w'], 'L0_ffn_mlp2_b': _L0_ffn_in['mlp2_b']}

def reference(x, src, dst, edge_weight, L0_gnn_bias, L0_mix_W_qkv, L0_mix_qn_w, L0_mix_kn_w, L0_mix_W_out, L0_mix_b_out, L0_ffn_norm_scale, L0_ffn_gate_w, L0_ffn_gate_b, L0_ffn_mlp1_w, L0_ffn_mlp1_b, L0_ffn_mlp2_w, L0_ffn_mlp2_b):
    import jax
    import jax.numpy as jnp

    def _L0_gnn_ref(x, nnz_weight, bias, edge_index):
        import jax, jax.numpy as jnp
        import numpy as np
        INDIM = 1024
        OUTDIM = 1024
        NNZ = 8192
        N = 6250
        row, col = (edge_index[0], edge_index[1])
        W = jnp.zeros((OUTDIM, INDIM), dtype=nnz_weight.dtype).at[row, col].add(nnz_weight)
        return x @ W.T + bias

    def _L0_mix_ref(x, W_qkv, qn_w, kn_w, W_out, b_out):
        import jax, jax.numpy as jnp
        import numpy as np
        DIM = 1024
        HEADS = 16
        DHEAD = DIM // HEADS
        EPS_NORM = 1e-06
        EPS_DEN = 1e-06

        def rmsnorm(x, w):
            xf = x.astype(jnp.float32)
            return (w * xf * jax.lax.rsqrt(jnp.mean(xf * xf, axis=-1, keepdims=True) + EPS_NORM)).astype(x.dtype)
        b, n, _ = x.shape
        qkv = x @ W_qkv
        q, k, v = jnp.split(qkv, 3, axis=-1)
        q = rmsnorm(q, qn_w)
        k = rmsnorm(k, kn_w)

        def split_heads(t):
            return t.reshape(b, n, HEADS, DHEAD).transpose(0, 2, 1, 3)
        q, k, v = map(split_heads, (q, k, v))
        q = jax.nn.relu(q).astype(jnp.float32)
        k = jax.nn.relu(k).astype(jnp.float32)
        v = v.astype(jnp.float32)
        kv = jnp.einsum('bhnd,bhne->bhde', k, v)
        out = jnp.einsum('bhnd,bhde->bhne', q, kv)
        k_sum = k.sum(axis=2)
        normalizer = jnp.einsum('bhnd,bhd->bhn', q, k_sum) + EPS_DEN
        out = out / normalizer[..., None]
        out = out.transpose(0, 2, 1, 3).reshape(b, n, DIM)
        return out @ W_out + b_out

    def _L0_ffn_ref(x, norm_scale, gate_w, gate_b, mlp1_w, mlp1_b, mlp2_w, mlp2_b):
        import jax, jax.numpy as jnp
        import numpy as np
        B, S, D = (1, 256, 1024)
        I = 256
        E = 8
        K = 2
        LIMIT = 7.0
        ALPHA = 1.702
        EPS = 1e-05

        def _swiglu(h):
            x_glu = jnp.minimum(h[..., ::2], LIMIT)
            x_lin = jnp.clip(h[..., 1::2], -LIMIT, LIMIT)
            return x_glu * jax.nn.sigmoid(ALPHA * x_glu) * (x_lin + 1.0)

        def _moe(t, gate_w, gate_b, mlp1_w, mlp1_b, mlp2_w, mlp2_b):
            T = t.shape[0]
            logits = t @ gate_w + gate_b
            top_v, top_i = jax.lax.top_k(logits, K)
            probs = jax.nn.softmax(top_v, axis=-1)
            w = jnp.zeros((T, E), t.dtype).at[jnp.arange(T)[:, None], top_i].set(probs)

            def body(acc, ew):
                w1, b1, w2, b2, we = ew
                h = _swiglu(t @ w1 + b1)
                y = h @ w2 + b2
                return (acc + we[:, None] * y, None)
            acc0 = jnp.zeros((T, t.shape[1]), t.dtype)
            acc, _ = jax.lax.scan(body, acc0, (mlp1_w, mlp1_b, mlp2_w, mlp2_b, w.T))
            return acc
        Bx, Sx, Dx = x.shape
        ms = jnp.mean(x * x, axis=-1, keepdims=True)
        t = (x * jax.lax.rsqrt(ms + EPS) * norm_scale).reshape(Bx * Sx, Dx)
        y = _moe(t, gate_w, gate_b, mlp1_w, mlp1_b, mlp2_w, mlp2_b)
        return x + y.reshape(Bx, Sx, Dx)
    edge_index = jnp.stack([src, dst])
    xn = _layernorm(x, axis=-1)
    x = x + _L0_gnn_ref(xn, edge_weight, L0_gnn_bias, edge_index) + _L0_mix_ref(xn[None], L0_mix_W_qkv, L0_mix_qn_w, L0_mix_kn_w, L0_mix_W_out, L0_mix_b_out)[0]
    x = x + _L0_ffn_ref(_layernorm(x, axis=-1)[None], L0_ffn_norm_scale, L0_ffn_gate_w, L0_ffn_gate_b, L0_ffn_mlp1_w, L0_ffn_mlp1_b, L0_ffn_mlp2_w, L0_ffn_mlp2_b)[0]
    return x

_drawn_inputs = setup_inputs


def setup_inputs(seed=0):
    import zlib

    import numpy as np

    out = dict(_drawn_inputs(seed))
    spreads = {'L0_mix_qn_w': (1.0, 0.6),
     'L0_mix_kn_w': (1.0, 0.6),
     'L0_mix_b_out': (0.0, 0.1),
     'L0_ffn_norm_scale': (1.0, 0.546),
     'L0_ffn_gate_b': (0.0, 0.317),
     'L0_ffn_mlp1_b': (0.0, 0.798),
     'L0_ffn_mlp2_b': (0.0, 0.1)}
    factors = {'L0_gnn_bias': 2.721}
    for name, (base, spread) in spreads.items():
        noise = np.random.default_rng([zlib.crc32(name.encode()), seed]).standard_normal(out[name].shape)
        drawn = base * np.exp(spread * noise) if base else spread * noise
        out[name] = jnp.asarray(drawn.astype(out[name].dtype))
    for name, factor in factors.items():
        out[name] = (out[name] * factor).astype(out[name].dtype)
    return out
```

```python
from contextlib import ExitStack

import concourse.bass as bass
from concourse import mybir

F32 = mybir.dt.float32
F16 = mybir.dt.float16
I32 = mybir.dt.int32
U32 = mybir.dt.uint32
ALU = mybir.AluOpType
ACT = mybir.ActivationFunctionType
AX = mybir.AxisListType
ENG = mybir.EngineType

P = 128
N, D = 1250, 1024
TT = 125
NT = N // TT
KT = D // P
HEADS = 16
PAIRS = HEADS // 2
E, HID = 8, 256
NE = 41250
CHUNKS = -(-NE // P)
LAST_ROWS = CHUNKS - 2 * P
WIN = 16
WINDOWS = D // WIN
G = 8
KV_GROUPS, Q_GROUPS = 3 * NT, 3 * KT
GROUPS = KV_GROUPS + Q_GROUPS
STEPS = (GROUPS + 2) * G
assert GROUPS * G >= CHUNKS + WINDOWS - 1
GRP = [(0, 418), (418, 416), (834, 416)]
GW = 418
PIECE = 2048
N_PIECE_Q, N_PIECE_O, N_PIECE_1, N_PIECE_2 = 4, 4, 16, 8
PIECES = 32
BLOCKS = (2 * N + E * (P - 1)) // P
SLOTS = BLOCKS * P

SX = 32.0
SW = 256.0
ST = 16.0
EPS_LN, EPS_Q, EPS_T = 1e-5, 1e-6, 1e-5

XNT_AT = 0
A_AT = 40000
B_AT = A_AT + 65536
C_AT = B_AT + 32768
S_AT = C_AT + 32768
TOP = 212800


def build_gps_layer(nc, x, src, dst, edge_weight, gnn_bias, w_qkv, qn_w, kn_w, w_flat, b_out,
                    norm_scale, gate_w, gate_b, mlp1_b, mlp2_b, out):
    scratch = lambda name, shape, dt: nc.dram_tensor(name, shape, dt, kind="Internal").ap()
    split_dram = scratch("split_dram", [2, PIECES, P, PIECE], F16)
    wg_dram = scratch("wg_dram", [2, D * D], F16)
    t_dram = scratch("t_dram", [N, D], F32)
    base_dram = scratch("base_dram", [N, D], F32)
    slot_token_dram = scratch("slot_token_dram", [SLOTS, 1], I32)
    y_dram = scratch("y_dram", [SLOTS, D], F32)

    with ExitStack() as ctx:
        arena = ctx.enter_context(nc.sbuf_tensor("arena", [P, TOP // 4], F32))
        bank = [ctx.enter_context(nc.psum_tensor(f"bank{b}", [P, 512], F32)) for b in range(8)]
        sem = lambda name: ctx.enter_context(nc.semaphore(name))

        def view(at, shape, dt=F32):
            size = 2 if dt == F16 else 4
            n = 1
            for s in shape:
                n *= s
            assert at % 4 == 0 and at + n * size <= TOP, (at, shape)
            v = arena[:, at // 4:at // 4 + -(-n * size // 4)]
            if dt != F32:
                v = v.bitcast(dt)
            v = v[:, 0:n]
            if len(shape) == 2:
                v = v.rearrange("p (a b) -> p a b", a=shape[0])
            if len(shape) == 3:
                v = v.rearrange("p (a b c) -> p a b c", a=shape[0], b=shape[1])
            return v

        class Place:
            def __init__(self, at, end):
                self.at, self.end = at, end

            def __call__(self, shape, dt=F32):
                n = 2 if dt == F16 else 4
                for s in shape:
                    n *= s
                v = view(self.at, shape, dt)
                self.at += -(-n // 32) * 32
                assert self.at <= self.end, (self.at, self.end)
                return v

        S = Place(S_AT, TOP)
        ident = S([P])
        ones = S([P])
        upper = S([P])
        zeros = S([P], F16)
        col_iota = S([P, G], F16)
        eps_x = S([1]); eps_k = S([1]); eps_den = S([1]); eps_b = S([1]); eps_t = S([1])
        qnw = S([KT])
        logits = S([NT, E]); top_v = S([NT, E]); top_i = S([NT, E], U32)
        gate_hl = S([2, KT * E], F16)
        gate_bias = S([E])
        ln_st = S([2, 12]); ln_mv = S([2, 2]); ln_sd = S([2, 1]); ln_rs = S([2, 1]); tiny = S([8])
        table_at = S.at
        key16 = S([STEPS], F16); lo16 = S([STEPS], F16); whi = S([STEPS], F16); wlo = S([STEPS], F16)
        win_at = S([STEPS], I32)
        one_hot = [S([3, P, G], F16) for _ in range(2)]
        key_hot = S([P, G], F16)
        stage_at = S.at
        stage = [S([PIECE]) for _ in range(2)]

        xt = view(XNT_AT, [2, KT, N], F16)
        wkv = view(A_AT, [2, KT, 2048], F16)
        ut = view(A_AT, [2, KT, N], F16)
        tail = Place(A_AT + 40000, A_AT + 65536)
        kvb = [tail([PAIRS, P], F16) for _ in range(2)]
        ksb = [tail([PAIRS, P], F16) for _ in range(2)]
        wq = [tail([2, KT, P], F16) for _ in range(2)]
        w_acc = view(C_AT, [WINDOWS * P])

        C = Place(C_AT, S_AT)
        src_i = C([3, P], I32); dst_i = C([3, P], I32)
        ew = C([3, P])
        key_c = C([3, P]); lo_c = C([3, P]); hi_i = C([3, P], I32)
        hi_f = C([3, P]); big = C([3, P])
        w_first = C([3]); w_last = C([3]); ends_i = C([3, 2], I32); n_win = C([3]); first = C([3])
        past = C([3]); shift = C([3])
        pick = C([3, STEPS])
        step_iota = C([STEPS])
        shift_b = C([3, P])
        win_f = C([STEPS])
        wsc = C([STEPS])

        B = Place(B_AT, C_AT)
        part = [B([2, PIECE], F16) for _ in range(2)]
        b_work = B.at
        xs = [B([D]) for _ in range(2)]
        xn = [B([D]) for _ in range(2)]
        B.at = b_work
        knw = B([D])
        kw = B([512])
        kt_ = [B([D], F16) for _ in range(2)]
        vt_ = [B([PAIRS, 130], F16) for _ in range(2)]
        junk = B([512], F16)
        B.at = b_work
        u32 = [B([GW]) for _ in range(2)]
        usq = [B([GW]) for _ in range(2)]
        qss = B([3, GW])
        ksf = B([PAIRS])
        head_mask = B([P])
        wo = view(B_AT, [2, KT, D], F16)

        T = Place(table_at, TOP)
        den = [T([GW]) for _ in range(2)]
        rec = [T([GW]) for _ in range(2)]
        att = [T([GW]) for _ in range(2)]
        eps_row = T([3, GW])
        acc_part = [T([2, D], F16) for _ in range(2)]

        T = Place(table_at, TOP)
        xm = [T([D]) for _ in range(2)]
        xn2 = T([D])
        tm = [T([D]) for _ in range(2)]
        tt = T([2, KT, TT], F16)
        bias_b = T([D]); scale_b = T([D])
        gate_f = T([KT * E])
        wg = view(C_AT, [2, KT, D], F16)

        slot_off = [A_AT + 40000, XNT_AT, B_AT]
        eslot = [(view(o, [2, KT * 512], F16), view(o + 16384, [2, 2 * D], F16)) for o in slot_off]
        arena16 = arena[:, :].bitcast(F16)
        b2_b = view(A_AT, [E * D])
        b1_b = view(C_AT, [E * 2 * HID])
        T = Place(C_AT + 16384, S_AT)
        hb = T([2 * HID]); glu = T([HID]); lin = T([HID]); sg = T([HID]); act = T([HID])
        actT = T([2, 2, P], F16)
        blk_i = T([BLOCKS], I32); exp_i = T([BLOCKS], I32); base_i = T([E + 1], I32)
        T2 = Place(table_at, TOP)
        rows = [T2([D]) for _ in range(2)]
        row_idx = [T2([1], I32) for _ in range(2)]
        rowT = [T2([2, KT, P], F16) for _ in range(2)]
        ysb = [T2([D]) for _ in range(2)]
        R = Place(24576, A_AT)
        oh = [R([NT, E]) for _ in range(2)]
        both = R([NT, E]); rank = R([NT, E]); tot = R([NT, E]); pre = R([NT, E])
        cnt = R([E]); cnt_i = R([E], I32); nblk = R([E]); cum = R([E + 1])
        e_iota = R([NT, E]); b_iota = R([BLOCKS]); expf = R([BLOCKS]); offf = R([BLOCKS]); ge = R([BLOCKS])
        slot_f = R([2, NT]); slot_i = [R([NT], I32) for _ in range(2)]
        token_i = R([NT], I32); zero_i = R([BLOCKS], I32); tok_of = R([BLOCKS], I32)
        prob = R([2, NT]); pe_ = R([NT]); pden = R([NT]); idx_f = R([NT, E])
        T3 = Place(C_AT, S_AT)
        cy = [[T3([D]) for _ in range(2)] for _ in range(2)]
        cb = [T3([D]) for _ in range(2)]

        passed = sem("passed"); edges_in = sem("edges_in"); table_in = sem("table_in"); consts = sem("consts")
        x_in = [sem(f"x_in{h}") for h in range(2)]
        xn_ready = sem("xn_ready"); stat_ready = sem("stat_ready"); sd_ready = sem("sd_ready")
        xt_psum = sem("xt_psum"); xt_hi = sem("xt_hi"); xt_done = sem("xt_done")
        stage_in = [sem(f"stage_in{h}") for h in range(2)]
        part_hi = sem("part_hi"); part_lo = sem("part_lo")
        part_out = [sem(f"part_out{h}") for h in range(2)]
        table_mm = sem("table_mm"); table_step = sem("table_step"); table_done = sem("table_done")
        knw_in = sem("knw_in"); qn_in = sem("qn_in"); qn_ready = sem("qn_ready"); acc_zero = sem("acc_zero")
        gate_w_ready = sem("gate_w_ready"); t_whole = sem("t_whole"); slots_zero = sem("slots_zero")
        kv_mm = sem("kv_mm"); k_sq = sem("k_sq"); kw_ready = sem("kw_ready"); k_hi = sem("k_hi")
        k_ss = sem("k_ss"); k_sd = sem("k_sd"); k_rs = sem("k_rs"); v_hi = sem("v_hi")
        v_lo = sem("v_lo"); kv_used = sem("kv_used")
        hot_ready = sem("hot_ready"); hot_key = sem("hot_key"); step_mm = sem("step_mm"); acc_done = sem("acc_done")
        dve_step = sem("dve_step"); act_step = sem("act_step"); pool_step = sem("pool_step")
        kvb_zero = sem("kvb_zero"); kvb_ready = sem("kvb_ready"); kvf_hi = sem("kvf_hi")
        wq_in = [sem(f"wq_in{h}") for h in range(2)]
        q_mm = sem("q_mm"); q_evac = sem("q_evac"); q_split = sem("q_split")
        eps_mm = sem("eps_mm"); eps_ready = sem("eps_ready")
        at_mm = sem("at_mm"); at_f = sem("at_f"); at_hi = sem("at_hi"); at_done = sem("at_done")
        acc_hi = sem("acc_hi"); acc_lo = sem("acc_lo")
        acc_out = [sem(f"acc_out{h}") for h in range(2)]
        wg_in = sem("wg_in"); wo_in = sem("wo_in"); mixc_in = sem("mixc_in"); mixc_ready = sem("mixc_ready")
        xm_in = [sem(f"xm_in{h}") for h in range(2)]
        xb_ready = sem("xb_ready"); mix_mm = sem("mix_mm"); x1_ready = sem("x1_ready")
        xn2_ready = sem("xn2_ready"); base_ready = sem("base_ready")
        base_out = [sem(f"base_out{h}") for h in range(2)]
        sd2_ready = sem("sd2_ready"); stat2_ready = sem("stat2_ready")
        t_ready = sem("t_ready")
        t_out = [sem(f"t_out{h}") for h in range(2)]
        tt_psum = sem("tt_psum"); tt_hi = sem("tt_hi"); tt_done = sem("tt_done")
        gate_mm = sem("gate_mm"); gate_done = sem("gate_done")
        route_iota = sem("route_iota"); zero_out = sem("zero_out"); route_mm = sem("route_mm")
        count_in = sem("count_in"); route_exp = sem("route_exp"); pexp_in = sem("pexp_in")
        slots_ready = sem("slots_ready"); tokens_out = sem("tokens_out"); tokens_in = sem("tokens_in")
        bias_in = sem("bias_in"); w_slot_in = sem("w_slot_in"); expert_ready = sem("expert_ready")
        row_in = [sem(f"row_in{h}") for h in range(2)]; idx_ready = sem("idx_ready")
        rt_psum = sem("rt_psum"); rt_hi = sem("rt_hi"); rt_done = sem("rt_done")
        h_mm = sem("h_mm"); h_evac = sem("h_evac"); glu_ready = sem("glu_ready"); sg_ready = sem("sg_ready")
        act_ready = sem("act_ready"); at_psum = sem("at_psum"); a_hi = sem("a_hi"); a_done = sem("a_done")
        y_mm = sem("y_mm"); y_ready = sem("y_ready")
        y_out = [sem(f"y_out{h}") for h in range(2)]
        c_in = [sem(f"c_in{h}") for h in range(2)]
        c_base_in = [sem(f"c_base_in{h}") for h in range(2)]
        c_done = sem("c_done"); stored = [sem(f"stored{h}") for h in range(2)]

        START = 1

        class Steps:
            def __init__(self, eng, s):
                self.eng, self.s, self.base, self.n = eng, s, 0, 0

            def done(self, ins):
                self.n += 1
                ins.then_inc(self.s, 1)
                self.eng.wait_ge(self.s, self.base + self.n)

            def enter(self, i, per):
                self.start = self.base + self.n if not hasattr(self, "start") else self.start
                self.base, self.n, self.per = self.start + i * per, 0, per

            def leave(self, iters):
                assert self.n == self.per, (self.n, self.per)
                self.base, self.n = self.start + iters * self.per, 0
                del self.start

        def apart(eng):
            eng.sem_inc(passed, 1)

        def tok(i, n=TT):
            return bass.ds(i * TT, n)

        x_rows = x.rearrange("(i p) d -> i p d", p=TT)
        out_rows = out.rearrange("(i p) d -> i p d", p=TT)
        t_rows = t_dram.rearrange("(i p) d -> i p d", p=TT)
        base_rows = base_dram.rearrange("(i p) d -> i p d", p=TT)
        wkv_rows = w_qkv.rearrange("(k p) c -> k p c", p=P)

        def tile_dma(eng, to, frm, s):
            for a, b in ((0, 112), (112, TT)):
                eng.dma_start(to[a:b], frm[a:b]).then_inc(s, 16)

        def row_of(rows3, i):
            return rows3[bass.ds(i, 1)].rearrange("o p d -> (o p) d")

        block = ctx.enter_context(nc.Block())

        @block.sync
        def _(sp):
            sp.wait_ge(edges_in, 1)
            for t_i, a in ((src_i, src), (dst_i, dst), (ew, edge_weight)):
                full = (CHUNKS - 1) * P
                sp.dma_start(t_i[:, 0:2, :], a[0:2 * P * P].rearrange("(r c e) -> c r e", r=2, e=P)).then_inc(table_in, 16)
                sp.dma_start(t_i[0:LAST_ROWS - 1, 2, :], a[2 * P * P:full].rearrange("(c e) -> c e", e=P)).then_inc(table_in, 16)
                sp.dma_start(t_i[LAST_ROWS - 1:LAST_ROWS, 2, 0:NE - full],
                             a[full:NE].rearrange("(c e) -> c e", c=1)).then_inc(table_in, 16)
            for i in range(2):
                tile_dma(sp, xs[i], x_rows[i], x_in[i])
            with sp.Fori(1, NT // 2) as t:
                for h in range(2):
                    sp.wait_ge(xn_ready, 2 * t + h - 1)
                    tile_dma(sp, xs[h], row_of(x_rows, 2 * t + h), x_in[h])
            sp.dma_start(qnw, qn_w).then_inc(qn_in, 16)
            for m in range(KT):
                if m >= 2:
                    sp.wait_ge(part_lo, m - 1)
                sp.dma_start(stage[m % 2], wkv_rows[m, :, D:3 * D]).then_inc(stage_in[m % 2], 16)
            def ask(m, h):
                sp.wait_ge(part_lo, KT - 1 + m)
                sp.dma_start(stage[h], w_flat[bass.ds(m, 1)].rearrange("o p c -> (o p) c")).then_inc(stage_in[h], 16)

            def store(m, h):
                sp.wait_ge(part_lo, KT + 1 + m)
                for hl in range(2):
                    sp.dma_start(split_dram[hl, bass.ds(m, 1)].rearrange("o p c -> (o p) c"), part[h][:, hl, :]).then_inc(part_out[h], 16)
            ask(0, 0)
            ask(1, 1)
            with sp.Fori(0, N_PIECE_Q // 2 - 1) as t:
                for h in range(2):
                    store(2 * t + h, h)
                    ask(2 * t + h + 2, h)
            sp.wait_ge(xt_done, 2 + NT)
            sp.dma_start(knw, kn_w.partition_broadcast(P)).then_inc(knw_in, 16)
            m0 = N_PIECE_Q - 2
            with sp.Fori(0, (PIECES - N_PIECE_Q) // 2 - KT // 2) as t:
                for h in range(2):
                    store(m0 + 2 * t + h, h)
                    ask(m0 + 2 * t + h + 2, h)
            m1 = m0 + (PIECES - N_PIECE_Q) - KT
            for h in range(2):
                sp.wait_ge(part_out[h], 32 * N_PIECE_Q // 2)

            def load_wq(t, h):
                for hl in range(2):
                    sp.dma_start(wq[h][:, hl, :, :], split_dram[hl, bass.ds(t, 1), :, h * D:(h + 1) * D].rearrange("o p (k c) -> (o p) k c", c=P)).then_inc(wq_in[h], 16)
            sp.wait_ge(kv_used, START + NT)
            for h in range(2):
                load_wq(0, h)
            with sp.Fori(0, KT // 2 - 1) as t:
                for h in range(2):
                    store(m1 + 2 * t + h, h)
                    ask(m1 + 2 * t + h + 2, h)
                for h in range(2):
                    sp.wait_ge(q_mm, 6 * t + 3 * h + 3)
                    load_wq(t + 1, h)
            for h in range(2):
                store(PIECES - 4 + h, h)
                ask(PIECES - 2 + h, h)
            for h in range(2):
                store(PIECES - 2 + h, h)
            for h in range(2):
                sp.wait_ge(part_out[h], 32 * PIECES // 2)
            sp.wait_ge(eps_mm, 3)
            for hl in range(2):
                for m in range(N_PIECE_O):
                    sp.dma_start(wo[:, hl, 2 * m:2 * m + 2, :], split_dram[hl, N_PIECE_Q + m].rearrange("p (k c) -> p k c", c=D)).then_inc(wo_in, 16)
            wg_win = wg_dram.rearrange("l (w m c) -> l m w c", m=P, c=P)
            for b in range(8):
                sp.wait_ge(acc_lo, b + 1)
                for hl in range(2):
                    sp.dma_start(wg_win[hl, :, 8 * b:8 * b + 8, :], acc_part[b % 2][:, hl, :].rearrange("p (w c) -> p w c", c=P)).then_inc(acc_out[b % 2], 16)
            for h in range(2):
                sp.wait_ge(acc_out[h], 4 * 32)
            for hl in range(2):
                sp.dma_start(wg[:, hl, :, :], wg_dram[hl].rearrange("(k p c) -> p k c", p=P, c=D)).then_inc(wg_in, 16)
            sp.wait_ge(at_done, START + 3 * KT)
            sp.dma_start(bias_b, gnn_bias.partition_broadcast(P)).then_inc(mixc_in, 16)
            sp.dma_start(tm[1], b_out.partition_broadcast(P)).then_inc(mixc_in, 16)
            sp.dma_start(scale_b, norm_scale.partition_broadcast(P)).then_inc(mixc_in, 16)
            sp.dma_start(gate_bias, gate_b.partition_broadcast(P)).then_inc(mixc_in, 16)
            sp.dma_start(gate_f, gate_w).then_inc(mixc_in, 16)

            def load_expert(e, s):
                w1, w2 = eslot[e % 3]
                for hl in range(2):
                    for m in range(2):
                        sp.dma_start(w1[:, hl, m * PIECE:(m + 1) * PIECE], split_dram[hl, N_PIECE_Q + N_PIECE_O + 2 * e + m]).then_inc(s, 16)
                    sp.dma_start(w2[:, hl, :], split_dram[hl, N_PIECE_Q + N_PIECE_O + N_PIECE_1 + e]).then_inc(s, 16)
            tile_dma(sp, xm[0], x_rows[0], xm_in[0])
            tile_dma(sp, xm[1], x_rows[1], xm_in[1])
            load_expert(0, w_slot_in)

            def store_mixed(i, h):
                sp.wait_ge(t_ready, i + 1)
                tile_dma(sp, row_of(t_rows, i), tm[h], t_out[h])
                sp.wait_ge(base_ready, i + 1)
                tile_dma(sp, row_of(base_rows, i), xm[h], base_out[h])
            with sp.Fori(0, NT // 2 - 1) as t:
                for h in range(2):
                    store_mixed(2 * t + h, h)
                    sp.wait_ge(base_out[h], 32 * (t + 1))
                    tile_dma(sp, xm[h], row_of(x_rows, 2 * t + h + 2), xm_in[h])
            for h in range(2):
                store_mixed(NT - 2 + h, h)
            for h in range(2):
                sp.wait_ge(base_out[h], 16 * NT)
                sp.wait_ge(t_out[h], 16 * NT)
            sp.sem_inc(t_whole, 1)
            sp.wait_ge(gate_done, START + NT)
            sp.dma_start(b1_b, mlp1_b.partition_broadcast(P)).then_inc(bias_in, 16)
            sp.dma_start(b2_b, mlp2_b.partition_broadcast(P)).then_inc(bias_in, 16)
            sp.wait_ge(w_slot_in, 96)
            sp.sem_inc(expert_ready, 1)
            sp.wait_ge(count_in, 1)
            for e in range(1, E):
                if e >= 3:
                    done = sp.value_load(base_i[0:1, e - 2:e - 1], min_val=1, max_val=BLOCKS)
                    sp.wait_ge(y_mm, done)
                load_expert(e, w_slot_in)
                sp.wait_ge(w_slot_in, 96 * (e + 1))
                sp.sem_inc(expert_ready, 1)
            for i in range(NT):
                sp.wait_ge(c_done, i + 1)
                tile_dma(sp, out_rows[i], cb[i % 2], stored[i % 2])
            for h in range(2):
                sp.wait_ge(stored[h], 16 * NT)

        @block.gpsimd
        def _(pool):
            st = Steps(pool, pool_step)
            for s in (q_split, at_done):
                pool.sem_inc(s, START)
            pool.memset(dst_i[:, 2, :], 2047).then_inc(pool_step, 1)
            pool.memset(src_i[:, 2, :], 0).then_inc(pool_step, 1)
            pool.memset(ew[:, 2, :], 0.0).then_inc(pool_step, 1)
            st.n = 3
            pool.wait_ge(pool_step, 3)
            pool.sem_inc(edges_in, 1)
            st.done(pool.memset(ident, 0.0))
            pool.affine_select(out=ident, in_=ident, pattern=[[-1, P]], compare_op=ALU.not_equal, fill=1.0,
                               base=0, channel_multiplier=1).then_inc(consts, 1)
            pool.memset(ones, 1.0).then_inc(consts, 1)
            st.done(pool.memset(upper, 1.0))
            pool.affine_select(out=upper, in_=upper, pattern=[[1, P]], compare_op=ALU.is_gt, fill=0.0,
                               base=0, channel_multiplier=-1).then_inc(consts, 1)
            pool.iota(step_iota, [[1, STEPS]], base=0, channel_multiplier=0,
                      allow_small_or_imprecise_dtypes=True).then_inc(consts, 1)
            pool.iota(col_iota, [[1, P], [0, G]], base=0, channel_multiplier=0,
                      allow_small_or_imprecise_dtypes=True).then_inc(consts, 1)
            pool.memset(zeros, 0.0).then_inc(consts, 1)
            for tile_, v in ((eps_x, EPS_LN / (SX * SX)), (eps_k, EPS_Q * 65536.0), (eps_den, 64e-12 * EPS_Q),
                             (eps_b, EPS_LN), (eps_t, EPS_T / (ST * ST))):
                pool.memset(tile_, v).then_inc(consts, 1)

            pool.wait_ge(consts, 11)
            pool.wait_ge(table_done, 1)
            pool.memset(w_acc, 0.0).then_inc(acc_zero, 1)
            pool.wait_ge(kv_used, START + NT)
            for t_ in kvb:
                pool.memset(t_, 0.0).then_inc(kvb_zero, 1)
            st.done(pool.memset(head_mask, 0.0))
            for a in (0, 64):
                pool.memset(head_mask[a:a + 64, a:a + 64], 1.0).then_inc(kvb_zero, 1)
            pool.wait_ge(kvb_zero, 4)
            st.done(pool.memset(qss, 0.0))
            with pool.Fori(0, KT // 2) as t:
                for u in range(6):
                    h, g = divmod(u, 3)
                    a, n = GRP[g]
                    pool.wait_ge(q_evac, START + 6 * t + u + 1)
                    pool.tensor_copy(ut[:, 0, bass.ds(2 * t + h, 1), a:a + n].rearrange("p o n -> p (o n)"),
                                     u32[u % 2][:, 0:n]).then_inc(q_split, 1)
                    pool.wait_ge(q_split, START + 3 * (6 * t + u) + 1)
                    pool.tensor_tensor(ut[:, 1, bass.ds(2 * t + h, 1), a:a + n].rearrange("p o n -> p (o n)"),
                                       u32[u % 2][:, 0:n],
                                       ut[:, 0, bass.ds(2 * t + h, 1), a:a + n].rearrange("p o n -> p (o n)"),
                                       ALU.subtract).then_inc(q_split, 1)
                    pool.tensor_tensor(qss[:, g, 0:n], qss[:, g, 0:n], usq[u % 2][:, 0:n], ALU.add).then_inc(q_split, 1)
                    pool.wait_ge(q_split, START + 3 * (6 * t + u) + 3)

            with pool.Fori(0, KT // 2) as t:
                for u in range(6):
                    h, g = divmod(u, 3)
                    a, n = GRP[g]
                    pool.wait_ge(at_hi, 6 * t + u + 1)
                    pool.tensor_tensor(ut[:, 1, bass.ds(2 * t + h, 1), a:a + n].rearrange("p o n -> p (o n)"),
                                       att[u % 2][:, 0:n],
                                       ut[:, 0, bass.ds(2 * t + h, 1), a:a + n].rearrange("p o n -> p (o n)"),
                                       ALU.subtract).then_inc(at_done, 1)

            pool.wait_ge(mixc_in, 80)
            pool.tensor_tensor(bias_b, bias_b, tm[1], ALU.add).then_inc(mixc_ready, 1)
            pool.wait_ge(mixc_ready, 1)

            def mix_in(i, h, t):
                pool.wait_ge(xm_in[h], 32 * (t + 1))
                pool.tensor_tensor(xm[h][0:TT], xm[h][0:TT], bias_b[0:TT], ALU.add).then_inc(xb_ready, 1)

            def mix_out(i, h):
                pool.wait_ge(xn2_ready, i + 1)
                pool.tensor_tensor(xm[h][0:TT], xm[h][0:TT], xn2[0:TT], ALU.add).then_inc(base_ready, 1)
            mix_in(0, 0, 0)
            mix_in(1, 1, 0)
            with pool.Fori(0, NT // 2 - 1) as t:
                for h in range(2):
                    mix_out(2 * t + h, h)
                    mix_in(2 * t + h + 2, h, t + 1)
            mix_out(NT - 2, 0)
            mix_out(NT - 1, 1)

            pool.wait_ge(gate_done, START + NT)
            pool.iota(e_iota, [[0, NT], [1, E]], base=0, channel_multiplier=0,
                      allow_small_or_imprecise_dtypes=True).then_inc(route_iota, 1)
            pool.iota(b_iota, [[1, BLOCKS]], base=0, channel_multiplier=0,
                      allow_small_or_imprecise_dtypes=True).then_inc(route_iota, 1)
            pool.iota(token_i, [[TT, NT]], base=0, channel_multiplier=1).then_inc(route_iota, 1)
            pool.memset(zero_i, 0).then_inc(route_iota, 1)
            pool.wait_ge(route_iota, 4)
            pool.dma_start(slot_token_dram.rearrange("(p b) o -> p (b o)", p=P), zero_i).then_inc(zero_out, 16)
            pool.wait_ge(zero_out, 16)
            pool.wait_ge(slots_ready, 1)
            for c in range(2):
                for i in range(NT):
                    pool.indirect_dma_start(
                        out=slot_token_dram, out_offset=bass.IndirectOffsetOnAxis(ap=slot_i[c][0:TT, i:i + 1], axis=0),
                        in_=token_i[0:TT, i:i + 1], in_offset=None).then_inc(tokens_in, 16)
            pool.wait_ge(tokens_in, 16 * 2 * NT)
            with nc.allow_non_contiguous_dma(reason="one int32 per slot"):
                pool.dma_start(tok_of, slot_token_dram.rearrange("(b p) o -> p (b o)", p=P)).then_inc(tokens_in, 16)
            pool.wait_ge(tokens_in, 16 * (2 * NT + 1))
            pool.wait_ge(t_whole, 1)

            def gather(b, s):
                pool.tensor_copy(row_idx[s], tok_of[:, bass.ds(b, 1)]).then_inc(idx_ready, 1)
                pool.wait_ge(idx_ready, b + 1)
                apart(pool)
                pool.indirect_dma_start(out=rows[s], out_offset=None, in_=t_dram,
                                        in_offset=bass.IndirectOffsetOnAxis(ap=row_idx[s], axis=0)).then_inc(row_in[s], 16)
            gather(0, 0)
            gather(1, 1)
            with pool.Fori(0, (BLOCKS - 3) // 2) as t:
                for h in range(2):
                    pool.wait_ge(rt_psum, 2 * t + h + 1)
                    gather(2 * t + h + 2, h)
            pool.wait_ge(rt_psum, BLOCKS - 2)
            gather(BLOCKS - 1, (BLOCKS - 1) % 2)
            for h in range(2):
                pool.wait_ge(y_out[h], START + 16 * ((BLOCKS + 1 - h) // 2))
            pool.wait_ge(y_ready, START + BLOCKS)
            for i in range(NT):
                if i >= 2:
                    pool.wait_ge(c_done, i - 1)
                    pool.wait_ge(stored[i % 2], 32 * (i // 2))
                for c in range(2):
                    pool.indirect_dma_start(
                        out=cy[i % 2][c][0:TT], out_offset=None, in_=y_dram,
                        in_offset=bass.IndirectOffsetOnAxis(ap=slot_i[c][0:TT, i:i + 1], axis=0)).then_inc(c_in[i % 2], 16)
                tile_dma(pool, cb[i % 2], base_rows[i], c_base_in[i % 2])

        @block.tensor
        def _(pe):
            for s in (kv_used, gate_mm):
                pe.sem_inc(s, START)
            pe.wait_ge(consts, 11)
            pe.wait_ge(table_step, 1)
            rows_of = [P, P, LAST_ROWS]
            for r in range(3):
                for q in range(r):
                    pe.matmul(bank[0][:, r:r + 1], ones[0:rows_of[q], :], n_win[0:rows_of[q], q:q + 1], start=(q == 0), stop=False)
                mm = pe.matmul(bank[0][:, r:r + 1], upper[0:rows_of[r], :], n_win[0:rows_of[r], r:r + 1], start=(r == 0), stop=True)
            mm.then_inc(table_mm, 1)
            pe.wait_ge(table_step, 2)
            for b, cols in enumerate((key_c, lo_c, ew, shift_b, None)):
                for r in range(3):
                    lhs = ones[0:rows_of[r], :] if cols is None else cols[0:rows_of[r], r, :]
                    mm = pe.matmul(bank[1 + b][:, 0:STEPS], lhs, pick[0:rows_of[r], r, :], start=(r == 0), stop=(r == 2))
            mm.then_inc(table_mm, 1)
            pe.wait_ge(table_done, 1)

            with pe.Fori(0, NT // 2) as t:
                for h in range(2):
                    pe.wait_ge(xn_ready, 2 * t + h + 1)
                    pe.wait_ge(xt_done, 2 * t + h + 1)
                    for k in range(KT):
                        mm = pe.transpose(bank[2 * h + k // 4][:, (k % 4) * TT:(k % 4 + 1) * TT], xn[h][0:TT, k * P:(k + 1) * P], ident[0:TT, 0:TT])
                    mm.then_inc(xt_psum, 1)
            pe.wait_ge(xt_done, 2 + NT)
            pe.wait_ge(part_lo, KT)
            for b in range(3):
                pe.matmul(bank[3 + b][:, :], zeros, wkv[:, 0, 0, 0:512], start=True, stop=False, skip_group_check=True)

            def kv_unit(i, b, c0):
                for k in range(KT):
                    for n, (l, r) in enumerate(((0, 0), (0, 1), (1, 0))):
                        mm = pe.matmul(bank[b][0:TT, :], xt[:, l, k, tok(i)], wkv[:, r, k, c0:c0 + 512],
                                       start=(k == 0 and n == 0), stop=(k == KT - 1 and n == 2))
                mm.then_inc(kv_mm, 1)

            def kv_sums():
                for p in range(PAIRS):
                    for l, r in ((0, 0), (0, 1), (1, 0)):
                        mm = pe.matmul(bank[3 + p // 3][:, (p % 3) * 130:(p % 3) * 130 + 129], kt_[l][0:TT, p * P:(p + 1) * P],
                                       vt_[r][0:TT, p, 0:129], start=False, stop=False, skip_group_check=True)
                mm.then_inc(kv_used, 1)

            def steps(n, h):
                pe.wait_ge(hot_ready, n + 1)
                pe.wait_ge(acc_done, START + G * n)
                for j in range(G):
                    o = bank[6 + j // 4][:, (j % 4) * P:(j % 4 + 1) * P]
                    pe.matmul(o, one_hot[h][:, 1, :, j], one_hot[h][:, 0, :, j], start=True, stop=False)
                    mm = pe.matmul(o, one_hot[h][:, 2, :, j], one_hot[h][:, 0, :, j], start=False, stop=True)
                    if j % 4 == 3:
                        mm.then_inc(step_mm, 1)

            def kv_tile(i, s, first=False):
                if not first:
                    pe.wait_ge(v_lo, 2 * i)
                kv_unit(i, 0, 0)
                if not first:
                    kv_sums()
                kv_unit(i, 1, 512)
                steps(3 * i, s % 2)
                kv_unit(i, 2, 1024)
                steps(3 * i + 1, (s + 1) % 2)
                pe.wait_ge(kw_ready, 2 * i + 1)
                kv_unit(i, 0, 1536)
                steps(3 * i + 2, (s + 2) % 2)
            kv_tile(0, 0, True)
            kv_tile(1, 3)
            with pe.Fori(1, NT // 2) as t:
                for h in range(2):
                    kv_tile(2 * t + h, 3 * h)
            pe.wait_ge(v_lo, 2 * NT)
            kv_sums()

            with pe.Fori(0, KT // 2) as t:
                for u in range(6):
                    h, g = divmod(u, 3)
                    a, n = GRP[g]
                    if g == 0:
                        pe.wait_ge(wq_in[h], 32 * (t + 1))
                    pe.wait_ge(q_evac, START + 6 * t + max(u - 2, 0))
                    for k in range(KT):
                        for c, (l, r) in enumerate(((0, 0), (1, 0), (0, 1))):
                            mm = pe.matmul(bank[u % 3][:, 0:n], wq[h][:, l, k, :], xt[:, r, k, a:a + n],
                                           start=(k == 0 and c == 0), stop=(k == KT - 1 and c == 2))
                    mm.then_inc(q_mm, 1)
                    steps(KV_GROUPS + 6 * t + u, u % 2)
            pe.wait_ge(q_split, START + 9 * KT)
            pe.wait_ge(q_evac, START + 3 * KT)
            pe.wait_ge(kvb_ready, 1)
            for g in range(3):
                pe.matmul(bank[g][:, 0:GRP[g][1]], ones, qss[:, g, 0:GRP[g][1]], start=True, stop=True).then_inc(eps_mm, 1)
            pe.wait_ge(eps_ready, 3)
            with pe.Fori(0, KT // 2) as t:
                for u in range(6):
                    h, g = divmod(u, 3)
                    a, n = GRP[g]
                    pe.wait_ge(at_f, START + 6 * t + max(u - 2, 0))
                    for b, w in ((2 * (u % 3), kvb), (2 * (u % 3) + 1, ksb)):
                        for c, (l, r) in enumerate(((0, 0), (1, 0), (0, 1))):
                            mm = pe.matmul(bank[b][:, 0:n], w[l][:, bass.ds(2 * t + h, 1), :].rearrange("p o n -> p (o n)"),
                                           ut[:, r, bass.ds(2 * t + h, 1), a:a + n].rearrange("p o n -> p (o n)"), start=(c == 0), stop=(c == 2))
                    mm.then_inc(at_mm, 1)

            pe.wait_ge(at_done, START + 3 * KT)
            pe.wait_ge(wo_in, 16 * 2 * N_PIECE_O)
            pe.wait_ge(wg_in, 32)
            pe.wait_ge(gate_w_ready, 1)

            def mix_tile(i, h):
                for half in range(2):
                    c0 = half * 512
                    for m, (a_, w_) in enumerate(((ut, wo), (xt, wg))):
                        for k in range(KT):
                            for c, (l, r) in enumerate(((0, 0), (0, 1), (1, 0))):
                                mm = pe.matmul(bank[2 * h + half][0:TT, :], a_[:, l, k, tok(i)], w_[:, r, k, c0:c0 + 512],
                                               start=(m == 0 and k == 0 and c == 0), stop=(m == 1 and k == KT - 1 and c == 2))
                mm.then_inc(mix_mm, 1)

            def gate_tile(i, h):
                pe.wait_ge(t_ready, i + 1)
                for k in range(KT):
                    mm = pe.transpose(bank[4 + k // 4][:, (k % 4) * TT:(k % 4 + 1) * TT], tm[h][0:TT, k * P:(k + 1) * P], ident[0:TT, 0:TT])
                mm.then_inc(tt_psum, 1)

            def gate_logits(i):
                pe.wait_ge(tt_done, i + 1)
                pe.wait_ge(gate_done, START + i)
                for k in range(KT):
                    for c, (l, r) in enumerate(((0, 0), (0, 1), (1, 0))):
                        mm = pe.matmul(bank[6][0:TT, 0:E], tt[:, l, k, :], gate_hl[:, r, k * E:(k + 1) * E],
                                       start=(k == 0 and c == 0), stop=(k == KT - 1 and c == 2))
                mm.then_inc(gate_mm, 1)
            mix_tile(0, 0)
            mix_tile(1, 1)
            gate_tile(0, 0)
            with pe.Fori(1, NT // 2) as t:
                for h in range(2):
                    i = 2 * t + h
                    pe.wait_ge(x1_ready, i - 1)
                    mix_tile(i, h)
                    gate_logits(i - 2)
                    gate_tile(i - 1, 1 - h)
            gate_logits(NT - 2)
            gate_tile(NT - 1, 1)
            gate_logits(NT - 1)
            pe.wait_ge(route_mm, 1)
            pe.matmul(bank[0][0:TT, 0:NT * E], upper[0:TT, 0:TT], both[0:TT].rearrange("p a b -> p (a b)"), start=True, stop=True)
            pe.matmul(bank[1][:, 0:NT * E], ones[0:TT, :], both[0:TT].rearrange("p a b -> p (a b)"), start=True, stop=True).then_inc(route_mm, 1)
            def row_T(b, s, q):
                pe.wait_ge(row_in[s], 16 * (q + 1))
                for k in range(KT):
                    mm = pe.transpose(bank[2 + 2 * s + k // 4][:, (k % 4) * P:(k % 4 + 1) * P], rows[s][:, k * P:(k + 1) * P], ident)
                mm.then_inc(rt_psum, 1)

            def up(b, s, off, half):
                if half == 0:
                    pe.wait_ge(rt_done, b + 1)
                    pe.wait_ge(h_evac, b)
                for k in range(4 * half, 4 * half + 4):
                    for c, (l, r) in enumerate(((0, 0), (0, 1), (1, 0))):
                        mm = pe.matmul(bank[6][:, :], rowT[s][:, l, k, :], arena16[:, bass.ds(off + (r * KT + k) * 512, 512)],
                                       start=(k == 0 and c == 0), stop=(k == KT - 1 and c == 2))
                if half == 1:
                    mm.then_inc(h_mm, 1)

            def act_T(b):
                pe.wait_ge(act_ready, b + 1)
                for k in range(2):
                    mm = pe.transpose(bank[7][:, k * P:(k + 1) * P], act[:, k * P:(k + 1) * P], ident)
                mm.then_inc(at_psum, 1)

            def down(b):
                off = pe.value_load(blk_i[0:1, bass.ds(b, 1)], min_val=0, max_val=TOP // 2 - 12288)
                pe.wait_ge(a_done, b + 1)
                pe.wait_ge(y_ready, START + b)
                for half in range(2):
                    for k in range(2):
                        for c, (l, r) in enumerate(((0, 0), (0, 1), (1, 0))):
                            mm = pe.matmul(bank[half][:, :], actT[:, l, k, :], arena16[:, bass.ds(off + 8192 + r * 2048 + k * D + half * 512, 512)],
                                           start=(k == 0 and c == 0), stop=(k == 1 and c == 2))
                mm.then_inc(y_mm, 1)

            def expert_block(b, s, q, first=False, last=False):
                off = pe.value_load(blk_i[0:1, bass.ds(b, 1)], min_val=0, max_val=TOP // 2 - 12288)
                need = pe.value_load(exp_i[0:1, bass.ds(b, 1)], min_val=0, max_val=E)
                if not last:
                    row_T(b + 1, 1 - s, q + s)
                pe.wait_ge(expert_ready, need + 1)
                up(b, s, off, 0)
                if not first:
                    act_T(b - 1)
                up(b, s, off, 1)
                if not first:
                    down(b - 1)
            pe.wait_ge(count_in, 1)
            row_T(0, 0, 0)
            expert_block(0, 0, 0, first=True)
            with pe.Fori(0, (BLOCKS - 3) // 2) as t:
                expert_block(2 * t + 1, 1, t)
                expert_block(2 * t + 2, 0, t + 1)
            expert_block(BLOCKS - 2, 1, (BLOCKS - 2) // 2)
            expert_block(BLOCKS - 1, 0, (BLOCKS - 1) // 2, last=True)
            act_T(BLOCKS - 1)
            down(BLOCKS - 1)

        @block.scalar
        def _(act_e):
            a_ = act_e
            st = Steps(a_, act_step)
            for s in (q_evac, y_out[0], y_out[1]):
                a_.sem_inc(s, START)
            a_.wait_ge(consts, 11)

            def xt_copy(i, h):
                a_.wait_ge(xt_psum, i + 1)
                apart(a_)
                for b in range(2):
                    a_.activation(xt[:, 0, 4 * b:4 * b + 4, tok(i)], bank[2 * h + b][:, 0:4 * TT].rearrange("p (k n) -> p k n", n=TT), ACT.Copy).then_inc(xt_hi, 1)

            def ln_sqrt(i, h):
                a_.wait_ge(stat_ready, i + 1)
                a_.activation(ln_sd[0:TT, h, :], ln_mv[0:TT, h, 1:2], ACT.Sqrt, bias=eps_x[0:TT], scale=1.0 / (SX * SX)).then_inc(sd_ready, 1)
            ln_sqrt(0, 0)
            ln_sqrt(1, 1)
            xt_copy(0, 0)
            with a_.Fori(1, NT // 2) as t:
                for h in range(2):
                    ln_sqrt(2 * t + h, h)
                    xt_copy(2 * t + h - 1, 1 - h)
            xt_copy(NT - 1, 1)

            def split_hi(m, h, to, seen, first=False):
                a_.wait_ge(stage_in[h], 16 * (seen + 1))
                a_.activation(to, stage[h], ACT.Copy, scale=SW).then_inc(part_hi, 1)
            for m in range(KT):
                split_hi(m, m % 2, wkv[:, 0, m, :], m // 2)

            def piece_hi(t, h):
                a_.wait_ge(part_out[h], 32 * t)
                split_hi(2 * t + h, h, part[h][:, 0, :], KT // 2 + t)
            for t in range(N_PIECE_Q // 2):
                for h in range(2):
                    piece_hi(t, h)

            def k_half(i, c):
                a_.wait_ge(kv_mm, 4 * i + c + 1)
                a_.activation(junk[0:TT], bank[c][0:TT, :], ACT.Square, accum_out=tiny[0:TT, c:c + 1]).then_inc(k_sq, 1)
                a_.wait_ge(kw_ready, 2 * i + c + 1)
                a_.activation(kt_[0][0:TT, c * 512:(c + 1) * 512], kw[0:TT], ACT.Relu).then_inc(k_hi, 1)

            def v_half(i, c):
                a_.wait_ge(kv_mm, 4 * i + 3 + c)
                a_.activation(vt_[0][0:TT, 4 * c:4 * c + 4, 0:P], bank[2 if c == 0 else 0][0:TT, :].rearrange("p (a b) -> p a b", b=P),
                              ACT.Copy, scale=tiny[0:TT, 4:5]).then_inc(v_hi, 1)

            def kv_tile(i, t, h):
                k_half(i, 0)
                k_half(i, 1)
                a_.wait_ge(k_ss, i + 1)
                a_.activation(tiny[0:TT, 3:4], tiny[0:TT, 2:3], ACT.Sqrt, bias=eps_k[0:TT], scale=2.0 ** -20).then_inc(k_sd, 1)
                piece_hi(2 + 2 * t + h, 0)
                a_.wait_ge(k_rs, i + 1)
                v_half(i, 0)
                piece_hi(2 + 2 * t + h, 1)
                v_half(i, 1)
            with a_.Fori(0, NT // 2) as t:
                for h in range(2):
                    kv_tile(2 * t + h, t, h)
            a_.wait_ge(kv_used, START + NT)
            a_.wait_ge(kvb_zero, 4)
            for p in range(PAIRS):
                for r0 in (0, 64):
                    c0 = (p % 3) * 130 + r0
                    ins = a_.activation(kvb[0][r0:r0 + 64, p, r0:r0 + 64], bank[3 + p // 3][r0:r0 + 64, c0:c0 + 64], ACT.Copy, scale=2.0 ** -12)
            ins.then_inc(kvf_hi, 1)

            a_.wait_ge(qn_ready, 1)
            with a_.Fori(0, KT // 2) as t:
                for u in range(6):
                    h, g = divmod(u, 3)
                    n = GRP[g][1]
                    a_.wait_ge(q_mm, 6 * t + u + 1)
                    a_.wait_ge(q_split, START + 3 * (6 * t + max(u - 1, 0)))
                    a_.activation(usq[u % 2][:, 0:n], bank[u % 3][:, 0:n], ACT.Square, scale=1.0 / (SX * SW)).then_inc(act_step, 1)
                    a_.activation(u32[u % 2][:, 0:n], bank[u % 3][:, 0:n], ACT.Relu, scale=qnw[:, bass.ds(2 * t + h, 1)]).then_inc(q_evac, 1)
                    if u == 2:
                        piece_hi(12 + t, 0)
                    if u == 5:
                        piece_hi(12 + t, 1)
            a_.wait_ge(hot_ready, GROUPS + 2)
            for g in range(3):
                a_.wait_ge(eps_mm, g + 1)
                a_.activation(eps_row[:, g, 0:GRP[g][1]], bank[g][:, 0:GRP[g][1]], ACT.Sqrt, bias=eps_den, scale=64e-12 / D).then_inc(eps_ready, 1)
            for b in range(8):
                if b >= 2:
                    a_.wait_ge(acc_out[b % 2], 32 * (b // 2))
                a_.activation(acc_part[b % 2][:, 0, :], w_acc[:, b * D:(b + 1) * D], ACT.Copy).then_inc(acc_hi, 1)
            with a_.Fori(0, KT // 2) as t:
                for u in range(6):
                    h, g = divmod(u, 3)
                    a, n = GRP[g]
                    a_.wait_ge(at_f, START + 6 * t + u + 1)
                    apart(a_)
                    a_.activation(ut[:, 0, bass.ds(2 * t + h, 1), a:a + n].rearrange("p o n -> p (o n)"), att[u % 2][:, 0:n], ACT.Copy).then_inc(at_hi, 1)
            def mix_sqrt(i, h):
                a_.wait_ge(stat2_ready, 2 * i + 1)
                a_.activation(ln_sd[0:TT, h, :], ln_mv[0:TT, h, 1:2], ACT.Sqrt, bias=eps_b[0:TT]).then_inc(sd2_ready, 1)
                a_.wait_ge(stat2_ready, 2 * i + 2)
                a_.activation(tiny[0:TT, 1:2], tiny[0:TT, 0:1], ACT.Sqrt, bias=eps_t[0:TT], scale=1.0 / (ST * ST)).then_inc(sd2_ready, 1)

            def tt_copy(i):
                a_.wait_ge(tt_psum, i + 1)
                a_.wait_ge(gate_mm, START + i)
                for b in range(2):
                    a_.activation(tt[:, 0, 4 * b:4 * b + 4, :], bank[4 + b][:, 0:4 * TT].rearrange("p (k n) -> p k n", n=TT), ACT.Copy).then_inc(tt_hi, 1)
            with a_.Fori(0, NT // 2) as t:
                for h in range(2):
                    mix_sqrt(2 * t + h, h)
                    tt_copy(2 * t + h)
            a_.wait_ge(route_exp, 1)
            a_.activation(pe_[0:TT], pe_[0:TT], ACT.Exp).then_inc(pexp_in, 1)
            def row_hi(b, s, first=False):
                a_.wait_ge(rt_psum, b + 1)
                if not first:
                    a_.wait_ge(h_mm, b - 1)
                for q in range(2):
                    a_.activation(rowT[s][:, 0, 4 * q:4 * q + 4, :], bank[2 + 2 * s + q][:, :].rearrange("p (k n) -> p k n", n=P), ACT.Copy).then_inc(rt_hi, 1)

            def act_hi(b):
                a_.wait_ge(at_psum, b + 1)
                a_.wait_ge(y_mm, b)
                a_.activation(actT[:, 0, :, :], bank[7][:, 0:2 * P].rearrange("p (k n) -> p k n", n=P), ACT.Copy).then_inc(a_hi, 1)

            def sigmoid(b):
                a_.wait_ge(glu_ready, b + 1)
                a_.wait_ge(act_ready, b)
                a_.activation(sg, glu, ACT.Sigmoid, scale=1.702).then_inc(sg_ready, 1)

            def store_y(b, s):
                a_.wait_ge(y_ready, START + b + 1)
                a_.dma_start(y_dram[bass.ds(b * P, P), :], ysb[s]).then_inc(y_out[s], 16)
            row_hi(0, 0, first=True)
            row_hi(1, 1, first=True)
            sigmoid(0)
            row_hi(2, 0)
            act_hi(0)
            sigmoid(1)
            with a_.Fori(0, (BLOCKS - 3) // 2) as t:
                for h in range(2):
                    b = 2 * t + h + 2
                    row_hi(b + 1, 1 - h)
                    act_hi(b - 1)
                    store_y(b - 2, h)
                    sigmoid(b)
            act_hi(BLOCKS - 2)
            store_y(BLOCKS - 3, (BLOCKS - 3) % 2)
            sigmoid(BLOCKS - 1)
            act_hi(BLOCKS - 1)
            store_y(BLOCKS - 2, (BLOCKS - 2) % 2)
            store_y(BLOCKS - 1, (BLOCKS - 1) % 2)

        @block.vector
        def _(v):
            st = Steps(v, dve_step)
            v.sem_inc(xt_done, 2)
            for s in (at_f, gate_done, y_ready, acc_done):
                v.sem_inc(s, START)
            v.wait_ge(consts, 11)
            v.wait_ge(table_in, 16 * 9)
            flat = lambda a: a.rearrange("p a b -> p (a b)")
            st.done(v.tensor_scalar(flat(hi_i), flat(src_i), 7, None, ALU.logical_shift_right))
            st.done(v.tensor_copy(flat(hi_f), flat(hi_i)))
            st.done(v.tensor_scalar(flat(hi_i), flat(src_i), P - 1, None, ALU.bitwise_and))
            v.tensor_copy(flat(lo_c), flat(hi_i))
            v.tensor_scalar(flat(big), flat(hi_f), float(D // P), 16384.0, ALU.is_ge, ALU.mult)
            st.done(v.tensor_copy(flat(key_c), flat(dst_i)))
            st.done(v.scalar_tensor_tensor(flat(key_c), flat(key_c), float(D // P), flat(hi_f), ALU.mult, ALU.add))
            st.done(v.tensor_tensor(flat(key_c), flat(key_c), flat(big), ALU.add))
            for c, col in ((0, 0), (1, P - 1)):
                ins = v.tensor_scalar(ends_i[:, :, c], dst_i[:, :, col], 4, None, ALU.logical_shift_right)
            st.done(ins)
            v.tensor_scalar(w_first, ends_i[:, :, 0], float(WINDOWS - 1), None, ALU.min)
            st.done(v.tensor_scalar(w_last, ends_i[:, :, 1], float(WINDOWS - 1), None, ALU.min))
            v.scalar_tensor_tensor(n_win, w_last, 1.0, w_first, ALU.add, ALU.subtract).then_inc(table_step, 1)
            v.wait_ge(table_mm, 1)
            st.done(v.tensor_copy(first, bank[0][:, 0:3]))
            v.tensor_tensor(past, first, n_win, ALU.add)
            st.done(v.tensor_tensor(shift, w_first, first, ALU.subtract))
            for r in range(3):
                v.tensor_scalar(shift_b[:, r, :], ones, shift[:, r:r + 1], None, ALU.mult)
                st.done(v.tensor_scalar(pick[:, r, :], step_iota, first[:, r:r + 1], None, ALU.is_ge))
                ins = v.scalar_tensor_tensor(pick[:, r, :], step_iota, past[:, r:r + 1], pick[:, r, :], ALU.is_lt, ALU.mult)
            ins.then_inc(table_step, 1)
            v.wait_ge(table_mm, 2)
            st.done(v.tensor_tensor(win_f, bank[5][:, 0:STEPS], step_iota, ALU.mult))
            st.done(v.tensor_tensor(win_f, bank[4][:, 0:STEPS], win_f, ALU.add))
            v.scalar_tensor_tensor(key16, win_f, -float(P), bank[1][:, 0:STEPS], ALU.mult, ALU.add)
            v.tensor_copy(lo16, bank[2][:, 0:STEPS])
            st.done(v.tensor_scalar(wsc, bank[3][:, 0:STEPS], SW, None, ALU.mult))
            st.done(v.tensor_copy(whi, wsc))
            v.tensor_tensor(wlo, wsc, whi, ALU.subtract)
            v.tensor_scalar(win_at, win_f, float(P), None, ALU.mult).then_inc(table_done, 1)
            v.wait_ge(table_done, 1)

            def stats(i, h, t):
                v.wait_ge(x_in[h], 32 * (t + 1))
                v.bn_stats(ln_st[0:TT, h, 0:6], xs[h][0:TT, 0:512])
                st.done(v.bn_stats(ln_st[0:TT, h, 6:12], xs[h][0:TT, 512:1024]))
                apart(v)
                v.bn_aggr(ln_mv[0:TT, h, :], ln_st[0:TT, h, :]).then_inc(stat_ready, 1)

            def norm(i, h):
                v.wait_ge(sd_ready, i + 1)
                st.done(v.reciprocal(ln_rs[0:TT, h, :], ln_sd[0:TT, h, :]))
                v.tensor_scalar(xn[h][0:TT], xs[h][0:TT], ln_mv[0:TT, h, 0:1], ln_rs[0:TT, h, :], ALU.subtract, ALU.mult).then_inc(xn_ready, 1)

            def xt_lo(i, h):
                for b in range(2):
                    v.wait_ge(xt_hi, 2 * i + b + 1)
                    ins = v.tensor_tensor(xt[:, 1, 4 * b:4 * b + 4, tok(i)], bank[2 * h + b][:, 0:4 * TT].rearrange("p (k n) -> p k n", n=TT),
                                          xt[:, 0, 4 * b:4 * b + 4, tok(i)], ALU.subtract)
                ins.then_inc(xt_done, 1)
            stats(0, 0, 0)
            norm(0, 0)
            stats(1, 1, 0)
            xt_lo(0, 0)
            norm(1, 1)
            with v.Fori(1, NT // 2) as t:
                st.enter(t - 1, 4)
                for h in range(2):
                    stats(2 * t + h, h, t)
                    xt_lo(2 * t + h - 1, 1 - h)
                    norm(2 * t + h, h)
            st.leave(NT // 2 - 1)
            xt_lo(NT - 1, 1)
            v.wait_ge(qn_in, 16)
            v.tensor_scalar(qnw, qnw, 1.0 / SW, None, ALU.mult).then_inc(qn_ready, 1)

            for m in range(KT):
                v.wait_ge(part_hi, m + 1)
                v.scalar_tensor_tensor(wkv[:, 1, m, :], stage[m % 2], SW, wkv[:, 0, m, :], ALU.mult, ALU.subtract).then_inc(part_lo, 1)

            def piece_lo(pair, h, j, slices):
                w = PIECE // slices
                if j == 0:
                    v.wait_ge(part_hi, KT + 2 * pair + h + 1)
                ins = v.scalar_tensor_tensor(part[h][:, 1, j * w:(j + 1) * w], stage[h][:, j * w:(j + 1) * w], SW,
                                             part[h][:, 0, j * w:(j + 1) * w], ALU.mult, ALU.subtract)
                if j == slices - 1:
                    ins.then_inc(part_lo, 1)
            for pair in range(N_PIECE_Q // 2):
                for h in range(2):
                    piece_lo(pair, h, 0, 1)

            def make(n, s, k):
                cols = lambda a: a[:, bass.ds(n * G, G)].unsqueeze(1).to_broadcast([P, P, G])
                if k == 0:
                    v.tensor_tensor(one_hot[s][:, 0], col_iota, cols(lo16), ALU.is_equal)
                elif k == 1:
                    v.wait_ge(hot_ready, n)
                    v.tensor_tensor(key_hot, col_iota, cols(key16), ALU.is_equal).then_inc(hot_key, 1)
                elif k == 2:
                    v.wait_ge(hot_key, n + 1)
                    v.tensor_tensor(one_hot[s][:, 1], key_hot, cols(whi), ALU.mult)
                else:
                    v.tensor_tensor(one_hot[s][:, 2], key_hot, cols(wlo), ALU.mult).then_inc(hot_ready, 1)

            def accumulate(n, s, pair=None, h=None):
                _, at = nc.values_load_multi_w_load_instructions(
                    win_at[0:1, bass.ds(n * G, G)], engines=(ENG.DVE,), min_val=0, max_val=(WINDOWS - 1) * P,
                    skip_runtime_bounds_check_because="the table clips windows to WINDOWS - 1")
                for j in range(G):
                    v.wait_ge(step_mm, 2 * n + j // 4 + 1)
                    v.wait_ge(acc_done, START + G * n + j)
                    v.tensor_tensor(w_acc[:, bass.ds(at[j], P)], bank[6 + j // 4][:, (j % 4) * P:(j % 4 + 1) * P],
                                    w_acc[:, bass.ds(at[j], P)], ALU.add).then_inc(acc_done, 1)
                    if j >= 4:
                        make(n + 2, s, j - 4)
                    elif pair is not None:
                        piece_lo(pair, h, j, 4)
            for n in range(2):
                for k in range(4):
                    make(n, n, k)

            def k_half(i, c):
                v.wait_ge(k_sq, 2 * i + c + 1)
                v.scalar_tensor_tensor(kw[0:TT], bank[c][0:TT, :], 1.0 / SW, knw[0:TT, c * 512:(c + 1) * 512], ALU.mult, ALU.mult).then_inc(kw_ready, 1)
                v.wait_ge(k_hi, 2 * i + c + 1)
                st.done(v.scalar_tensor_tensor(kt_[1][0:TT, c * 512:(c + 1) * 512], kw[0:TT], 0.0, kt_[0][0:TT, c * 512:(c + 1) * 512], ALU.max, ALU.subtract))

            def v_half(i, c):
                v.wait_ge(v_hi, 2 * i + c + 1)
                v.scalar_tensor_tensor(vt_[1][0:TT, 4 * c:4 * c + 4, 0:P], bank[2 if c == 0 else 0][0:TT, :].rearrange("p (a b) -> p a b", b=P),
                                       tiny[0:TT, 4:5], vt_[0][0:TT, 4 * c:4 * c + 4, 0:P], ALU.mult, ALU.subtract).then_inc(v_lo, 1)

            def kv_tile(i, s):
                v.wait_ge(kv_used, START + i)
                k_half(i, 0)
                k_half(i, 1)
                v.tensor_tensor(tiny[0:TT, 2:3], tiny[0:TT, 0:1], tiny[0:TT, 1:2], ALU.add).then_inc(k_ss, 1)
                v.wait_ge(k_sd, i + 1)
                st.done(v.reciprocal(tiny[0:TT, 4:5], tiny[0:TT, 3:4]))
                st.done(v.tensor_scalar(tiny[0:TT, 5:6], tiny[0:TT, 4:5], SX * SW, None, ALU.mult))
                st.done(v.tensor_scalar(vt_[0][0:TT, :, P], ones[0:TT, 0:PAIRS], tiny[0:TT, 5:6], None, ALU.mult))
                v.scalar_tensor_tensor(vt_[1][0:TT, :, P], ones[0:TT, 0:PAIRS], tiny[0:TT, 5:6], vt_[0][0:TT, :, P], ALU.mult, ALU.subtract).then_inc(k_rs, 1)
                accumulate(3 * i, s % 2, 2 + i, 0)
                v_half(i, 0)
                accumulate(3 * i + 1, (s + 1) % 2, 2 + i, 1)
                v_half(i, 1)
                accumulate(3 * i + 2, (s + 2) % 2)
            v.wait_ge(acc_zero, 1)
            v.wait_ge(knw_in, 16)
            with v.Fori(0, NT // 2) as t:
                st.enter(t, 10)
                for h in range(2):
                    kv_tile(2 * t + h, 3 * h)
            st.leave(NT // 2)
            v.wait_ge(kvf_hi, 1)
            for p in range(PAIRS):
                for r0 in (0, 64):
                    c0 = (p % 3) * 130 + r0
                    v.scalar_tensor_tensor(kvb[1][r0:r0 + 64, p, r0:r0 + 64], bank[3 + p // 3][r0:r0 + 64, c0:c0 + 64], 2.0 ** -12,
                                           kvb[0][r0:r0 + 64, p, r0:r0 + 64], ALU.mult, ALU.subtract)
            for b in range(3):
                n = min(3, PAIRS - 3 * b)
                ins = v.tensor_scalar(ksf[:, 3 * b:3 * b + n], bank[3 + b][:, 0:390].rearrange("p (a b) -> p a b", b=130)[:, 0:n, P], 2.0 ** -12, None, ALU.mult)
            st.done(ins)
            for p in range(PAIRS):
                ins = v.tensor_scalar(ksb[0][:, p, :], head_mask, ksf[:, p:p + 1], None, ALU.mult)
            st.done(ins)
            for p in range(PAIRS):
                ins = v.scalar_tensor_tensor(ksb[1][:, p, :], head_mask, ksf[:, p:p + 1], ksb[0][:, p, :], ALU.mult, ALU.subtract)
            ins.then_inc(kvb_ready, 1)
            with v.Fori(0, KT // 2) as t:
                for u in range(6):
                    if u in (2, 5):
                        accumulate(KV_GROUPS + 6 * t + u, u % 2, 12 + t, u // 3)
                    else:
                        accumulate(KV_GROUPS + 6 * t + u, u % 2)
            for b in range(8):
                v.wait_ge(acc_hi, b + 1)
                v.tensor_tensor(acc_part[b % 2][:, 1, :], w_acc[:, b * D:(b + 1) * D], acc_part[b % 2][:, 0, :], ALU.subtract).then_inc(acc_lo, 1)
            v.wait_ge(eps_ready, 3)
            with v.Fori(0, KT // 2) as t:
                st.enter(t, 12)
                for u in range(6):
                    n = GRP[u % 3][1]
                    v.wait_ge(at_mm, 6 * t + u + 1)
                    st.done(v.tensor_tensor(den[u % 2][:, 0:n], bank[2 * (u % 3) + 1][:, 0:n], eps_row[:, u % 3, 0:n], ALU.add))
                    st.done(v.reciprocal(rec[u % 2][:, 0:n], den[u % 2][:, 0:n]))
                    v.wait_ge(at_done, START + 6 * t + max(u - 1, 0))
                    v.scalar_tensor_tensor(att[u % 2][:, 0:n], bank[2 * (u % 3)][:, 0:n], SX, rec[u % 2][:, 0:n], ALU.mult, ALU.mult).then_inc(at_f, 1)
            st.leave(KT // 2)

            v.wait_ge(mixc_in, 80)
            st.done(v.tensor_scalar(gate_hl[:, 0, :], gate_f, SW, None, ALU.mult))
            v.scalar_tensor_tensor(gate_hl[:, 1, :], gate_f, SW, gate_hl[:, 0, :], ALU.mult, ALU.subtract).then_inc(gate_w_ready, 1)

            def mix_tile(i, t, h):
                v.wait_ge(xb_ready, i + 1)
                v.wait_ge(mix_mm, i + 1)
                for half in range(2):
                    c = slice(half * 512, half * 512 + 512)
                    ins = v.scalar_tensor_tensor(xm[h][0:TT, c], bank[2 * h + half][0:TT, :], 1.0 / (SX * SW), xm[h][0:TT, c], ALU.mult, ALU.add)
                ins.then_inc(x1_ready, 1)
                v.wait_ge(x1_ready, i + 1)
                v.bn_stats(ln_st[0:TT, h, 0:6], xm[h][0:TT, 0:512])
                st.done(v.bn_stats(ln_st[0:TT, h, 6:12], xm[h][0:TT, 512:1024]))
                apart(v)
                v.bn_aggr(ln_mv[0:TT, h, :], ln_st[0:TT, h, :]).then_inc(stat2_ready, 1)
                v.wait_ge(sd2_ready, 2 * i + 1)
                st.done(v.reciprocal(ln_rs[0:TT, h, :], ln_sd[0:TT, h, :]))
                v.tensor_scalar(tiny[0:TT, 0:1], ln_mv[0:TT, h, 1:2], ln_rs[0:TT, h, :], ln_rs[0:TT, h, :], ALU.mult, ALU.mult).then_inc(stat2_ready, 1)
                v.wait_ge(base_ready, i)
                v.tensor_scalar(xn2[0:TT], xm[h][0:TT], ln_mv[0:TT, h, 0:1], ln_rs[0:TT, h, :], ALU.subtract, ALU.mult).then_inc(xn2_ready, 1)
                v.wait_ge(sd2_ready, 2 * i + 2)
                st.done(v.reciprocal(tiny[0:TT, 2:3], tiny[0:TT, 1:2]))
                v.wait_ge(t_out[h], 32 * t)
                v.wait_ge(xn2_ready, i + 1)
                v.scalar_tensor_tensor(tm[h][0:TT], xn2[0:TT], tiny[0:TT, 2:3], scale_b[0:TT], ALU.mult, ALU.mult).then_inc(t_ready, 1)

            def tt_lo(i):
                for b in range(2):
                    v.wait_ge(tt_hi, 2 * i + b + 1)
                    ins = v.tensor_tensor(tt[:, 1, 4 * b:4 * b + 4, :], bank[4 + b][:, 0:4 * TT].rearrange("p (k n) -> p k n", n=TT),
                                          tt[:, 0, 4 * b:4 * b + 4, :], ALU.subtract)
                ins.then_inc(tt_done, 1)

            def gate(i):
                v.wait_ge(gate_mm, START + i + 1)
                v.scalar_tensor_tensor(logits[0:TT, bass.ds(i, 1), :].rearrange("p a b -> p (a b)"), bank[6][0:TT, 0:E], 1.0 / (ST * SW), gate_bias[0:TT],
                                       ALU.mult, ALU.add).then_inc(gate_done, 1)
            mix_tile(0, 0, 0)
            tt_lo(0)
            mix_tile(1, 0, 1)
            gate(0)
            tt_lo(1)
            with v.Fori(1, NT // 2) as t:
                st.enter(t - 1, 6)
                for h in range(2):
                    mix_tile(2 * t + h, t, h)
                    gate(2 * t + h - 1)
                    tt_lo(2 * t + h)
            st.leave(NT // 2 - 1)
            gate(NT - 1)

            v.wait_ge(gate_done, START + NT)
            v.wait_ge(route_iota, 4)
            for i in range(NT):
                ins = v.max(top_v[0:TT, i, :], logits[0:TT, i, :])
            st.done(ins)
            for i in range(NT):
                ins = v.max_index(top_i[0:TT, i, :], top_v[0:TT, i, :], logits[0:TT, i, :])
            st.done(ins)
            v.tensor_tensor(pe_[0:TT], top_v[0:TT, :, 1], top_v[0:TT, :, 0], ALU.subtract).then_inc(route_exp, 1)
            st.done(v.tensor_copy(flat(idx_f[0:TT]), flat(top_i[0:TT])))
            for c in range(2):
                ins = v.tensor_tensor(oh[c][0:TT], e_iota[0:TT], idx_f[0:TT, :, c:c + 1].to_broadcast([TT, NT, E]), ALU.is_equal)
            st.done(ins)
            v.tensor_tensor(flat(both[0:TT]), flat(oh[0][0:TT]), flat(oh[1][0:TT]), ALU.add).then_inc(route_mm, 1)
            v.wait_ge(route_mm, 2)
            v.memset(pre[:, 0, :], 0.0)
            st.done(v.tensor_copy(flat(tot), bank[1][:, 0:NT * E]))
            for i in range(1, NT):
                st.done(v.tensor_tensor(pre[:, i, :], pre[:, i - 1, :], tot[:, i - 1, :], ALU.add))
            st.done(v.tensor_tensor(cnt, pre[:, NT - 1, :], tot[:, NT - 1, :], ALU.add))
            st.done(v.tensor_scalar(cnt_i, cnt, float(P - 1), None, ALU.add))
            st.done(v.tensor_scalar(cnt_i, cnt_i, 7, None, ALU.logical_shift_right))
            v.memset(cum[:, 0:1], 0.0)
            st.done(v.tensor_scalar(nblk, cnt_i, 1.0, None, ALU.max))
            for e in range(E):
                st.done(v.tensor_tensor(cum[:, e + 1:e + 2], cum[:, e:e + 1], nblk[:, e:e + 1], ALU.add))
            v.tensor_copy(base_i, cum)
            v.memset(expf, 0.0)
            st.done(v.memset(offf, float(slot_off[0] // 2)))
            for e in range(E - 1):
                move = (slot_off[(e + 1) % 3] - slot_off[e % 3]) // 2
                st.done(v.tensor_scalar(ge, b_iota, cum[:, e + 1:e + 2], None, ALU.is_ge))
                v.tensor_tensor(expf, expf, ge, ALU.add)
                st.done(v.scalar_tensor_tensor(offf, ge, float(move), offf, ALU.mult, ALU.add))
            v.tensor_copy(exp_i, expf)
            v.tensor_copy(blk_i, offf).then_inc(count_in, 1)
            st.done(v.tensor_tensor(flat(rank[0:TT]), bank[0][0:TT, 0:NT * E], flat(pre[0:TT]), ALU.add))
            st.done(v.scalar_tensor_tensor(rank[0:TT], cum[0:TT, 0:E].unsqueeze(1).to_broadcast([TT, NT, E]), float(P), rank[0:TT], ALU.mult, ALU.add))
            for c in range(2):
                st.done(v.tensor_tensor(flat(oh[c][0:TT]), flat(oh[c][0:TT]), flat(rank[0:TT]), ALU.mult))
                st.done(v.tensor_reduce(slot_f[0:TT, c, :], oh[c][0:TT], AX.X, ALU.add))
                ins = v.tensor_copy(slot_i[c][0:TT], slot_f[0:TT, c, :])
            ins.then_inc(slots_ready, 1)
            v.wait_ge(pexp_in, 1)
            st.done(v.tensor_scalar(pden[0:TT], pe_[0:TT], 1.0, None, ALU.add))
            st.done(v.reciprocal(prob[0:TT, 0, :], pden[0:TT]))
            st.done(v.tensor_tensor(prob[0:TT, 1, :], pe_[0:TT], prob[0:TT, 0, :], ALU.mult))

            def row_lo(b, s):
                for q in range(2):
                    v.wait_ge(rt_hi, 2 * b + q + 1)
                    ins = v.tensor_tensor(rowT[s][:, 1, 4 * q:4 * q + 4, :], bank[2 + 2 * s + q][:, :].rearrange("p (k n) -> p k n", n=P),
                                          rowT[s][:, 0, 4 * q:4 * q + 4, :], ALU.subtract)
                ins.then_inc(rt_done, 1)

            def swiglu(b):
                e = v.value_load(exp_i[0:1, bass.ds(b, 1)], min_val=0, max_val=E - 1)
                v.wait_ge(h_mm, b + 1)
                v.scalar_tensor_tensor(hb, bank[6][:, :], 1.0 / (ST * SW), b1_b[:, bass.ds(e * (2 * HID), 2 * HID)], ALU.mult, ALU.add).then_inc(h_evac, 1)
                v.wait_ge(h_evac, b + 1)
                pairs = hb.rearrange("p (j c) -> p j c", c=2)
                v.tensor_scalar(glu, pairs[:, :, 0], 7.0, None, ALU.min).then_inc(glu_ready, 1)
                st.done(v.tensor_scalar(lin, pairs[:, :, 1], -7.0, 7.0, ALU.max, ALU.min))
                st.done(v.scalar_tensor_tensor(lin, lin, 1.0, glu, ALU.add, ALU.mult))
                v.wait_ge(sg_ready, b + 1)
                v.wait_ge(at_psum, b)
                v.scalar_tensor_tensor(act, lin, SX, sg, ALU.mult, ALU.mult).then_inc(act_ready, 1)

            def act_lo(b):
                v.wait_ge(a_hi, b + 1)
                v.tensor_tensor(actT[:, 1, :, :], bank[7][:, 0:2 * P].rearrange("p (k n) -> p k n", n=P), actT[:, 0, :, :], ALU.subtract).then_inc(a_done, 1)

            def evac_y(b, s, q):
                e = v.value_load(exp_i[0:1, bass.ds(b, 1)], min_val=0, max_val=E - 1)
                v.wait_ge(y_mm, b + 1)
                v.wait_ge(y_out[s], START + 16 * q)
                for half in range(2):
                    ins = v.scalar_tensor_tensor(ysb[s][:, half * 512:half * 512 + 512], bank[half][:, :], 1.0 / (SX * SW),
                                                 b2_b[:, bass.ds(e * D + half * 512, 512)], ALU.mult, ALU.add)
                ins.then_inc(y_ready, 1)
            v.wait_ge(bias_in, 32)
            row_lo(0, 0)
            row_lo(1, 1)
            swiglu(0)
            with v.Fori(0, (BLOCKS - 3) // 2) as t:
                st.enter(t, 4)
                for h in range(2):
                    b = 2 * t + h + 1
                    row_lo(b + 1, h)
                    act_lo(b - 1)
                    swiglu(b)
                    evac_y(b - 1, h, t)
            st.leave((BLOCKS - 3) // 2)
            for b in range(BLOCKS - 2, BLOCKS):
                if b + 1 < BLOCKS:
                    row_lo(b + 1, (b + 1) % 2)
                act_lo(b - 1)
                swiglu(b)
                evac_y(b - 1, (b - 1) % 2, (b - 1) // 2)
            act_lo(BLOCKS - 1)
            evac_y(BLOCKS - 1, (BLOCKS - 1) % 2, (BLOCKS - 1) // 2)
            for i in range(NT):
                v.wait_ge(c_in[i % 2], 32 * (i // 2 + 1))
                v.wait_ge(c_base_in[i % 2], 32 * (i // 2 + 1))
                o = cb[i % 2][0:TT]
                st.done(v.scalar_tensor_tensor(o, cy[i % 2][0][0:TT], prob[0:TT, 0, i:i + 1], o, ALU.mult, ALU.add))
                v.scalar_tensor_tensor(o, cy[i % 2][1][0:TT], prob[0:TT, 1, i:i + 1], o, ALU.mult, ALU.add).then_inc(c_done, 1)


_OUT = (N, D)


def kernel(**inputs):
    import numpy as np
    import concourse.bacc as bacc
    from concourse.bass_utils import run_bass_kernel_spmd

    a = {k: np.ascontiguousarray(v) for k, v in inputs.items()}
    w_qkv = a["L0_mix_W_qkv"]
    wq = w_qkv[:, 0:D].reshape(KT, P, KT, P).transpose(2, 1, 0, 3)
    wq = wq.reshape(KT // 2, 2, P, D).transpose(0, 2, 1, 3).reshape(N_PIECE_Q, P, PIECE)
    wo = a["L0_mix_W_out"].reshape(N_PIECE_O, 2, P, D).transpose(0, 2, 1, 3).reshape(N_PIECE_O, P, PIECE)
    w1 = a["L0_ffn_mlp1_w"].reshape(E, 2, 4, P, 2 * HID).transpose(0, 1, 3, 2, 4).reshape(N_PIECE_1, P, PIECE)
    w2 = a["L0_ffn_mlp2_w"].reshape(E, 2, P, D).transpose(0, 2, 1, 3).reshape(N_PIECE_2, P, PIECE)
    arrays = {
        "x": a["x"], "src": a["src"], "dst": a["dst"], "edge_weight": a["edge_weight"],
        "gnn_bias": a["L0_gnn_bias"], "w_qkv": w_qkv,
        "qn_w": np.ascontiguousarray(a["L0_mix_qn_w"].reshape(KT, P).T), "kn_w": a["L0_mix_kn_w"],
        "w_flat": np.ascontiguousarray(np.concatenate([wq, wo, w1, w2])), "b_out": a["L0_mix_b_out"],
        "norm_scale": a["L0_ffn_norm_scale"],
        "gate_w": np.ascontiguousarray(a["L0_ffn_gate_w"].reshape(KT, P, E).transpose(1, 0, 2).reshape(P, KT * E)),
        "gate_b": a["L0_ffn_gate_b"], "mlp1_b": a["L0_ffn_mlp1_b"].reshape(-1), "mlp2_b": a["L0_ffn_mlp2_b"].reshape(-1),
    }
    nc = bacc.Bacc("TRN2", target_bir_lowering=False, num_devices=1)
    args = {k: nc.dram_tensor(f"in_{k}", v.shape, mybir.dt.from_np(v.dtype), kind="ExternalInput").ap() for k, v in arrays.items()}
    out = nc.dram_tensor("out_x", _OUT, F32, kind="ExternalOutput").ap()
    build_gps_layer(nc, **args, out=out)
    r = run_bass_kernel_spmd(nc, [{f"in_{k}": v for k, v in arrays.items()}], core_ids=[0])
    return r.results[0]["out_x"]
```

```python
from contextlib import ExitStack

import concourse.bass as bass
from concourse import mybir

F32 = mybir.dt.float32
F16 = mybir.dt.float16
I32 = mybir.dt.int32
U32 = mybir.dt.uint32
ALU = mybir.AluOpType
ACT = mybir.ActivationFunctionType
AX = mybir.AxisListType
ENG = mybir.EngineType

P = 128
N, D = 1250, 1024
TT = 125
NT = N // TT
KT = D // P
HEADS = 16
PAIRS = HEADS // 2
AT_UNITS = PAIRS * NT // 2
E, HID = 8, 256
NE = 41250
CHUNKS = -(-NE // P)
LAST_ROWS = CHUNKS - 2 * P
WIN = 16
WINDOWS = D // WIN
G = 8
KV_GROUPS, Q_GROUPS = 3 * NT, 3 * KT
GROUPS = KV_GROUPS + Q_GROUPS
STEPS = (GROUPS + 2) * G
assert GROUPS * G >= CHUNKS + WINDOWS - 1
GRP = [(0, 418), (418, 416), (834, 416)]
GW = 418
AW = 2 * TT
PIECE = 2048
N_PIECE_Q, N_PIECE_O, N_PIECE_1, N_PIECE_2 = 4, 4, 16, 8
PIECES = 32
BLOCKS = (2 * N + E * (P - 1)) // P
SLOTS = BLOCKS * P

SX = 32.0
SW = 256.0
ST = 16.0
EPS_LN, EPS_Q, EPS_T = 1e-5, 1e-6, 1e-5

XNT_AT = 0
A_AT = 40000
B_AT = A_AT + 65536
C_AT = B_AT + 32768
S_AT = C_AT + 32768
TOP = 212800


def build_gps_layer(nc, x, src, dst, edge_weight, gnn_bias, w_qkv, qn_w, kn_w, w_flat, b_out,
                    norm_scale, gate_w, gate_b, mlp1_b, mlp2_b, out):
    scratch = lambda name, shape, dt: nc.dram_tensor(name, shape, dt, kind="Internal").ap()
    split_dram = scratch("split_dram", [2, PIECES, P, PIECE], F16)
    wg_dram = scratch("wg_dram", [2, D * D], F16)
    t_dram = scratch("t_dram", [N, D], F32)
    base_dram = scratch("base_dram", [N, D], F32)
    slot_token_dram = scratch("slot_token_dram", [SLOTS, 1], I32)
    y_dram = scratch("y_dram", [SLOTS, D], F32)

    with ExitStack() as ctx:
        arena = ctx.enter_context(nc.sbuf_tensor("arena", [P, TOP // 4], F32))
        bank = [ctx.enter_context(nc.psum_tensor(f"bank{b}", [P, 512], F32)) for b in range(8)]
        sem = lambda name: ctx.enter_context(nc.semaphore(name))

        def view(at, shape, dt=F32):
            size = 2 if dt == F16 else 4
            n = 1
            for s in shape:
                n *= s
            assert at % 4 == 0 and at + n * size <= TOP, (at, shape)
            v = arena[:, at // 4:at // 4 + -(-n * size // 4)]
            if dt != F32:
                v = v.bitcast(dt)
            v = v[:, 0:n]
            if len(shape) == 2:
                v = v.rearrange("p (a b) -> p a b", a=shape[0])
            if len(shape) == 3:
                v = v.rearrange("p (a b c) -> p a b c", a=shape[0], b=shape[1])
            return v

        class Place:
            def __init__(self, at, end):
                self.at, self.end = at, end

            def __call__(self, shape, dt=F32):
                n = 2 if dt == F16 else 4
                for s in shape:
                    n *= s
                v = view(self.at, shape, dt)
                self.at += -(-n // 32) * 32
                assert self.at <= self.end, (self.at, self.end)
                return v

        S = Place(S_AT, TOP)
        ident = S([P])
        ones = S([P])
        upper = S([P])
        zeros = S([P], F16)
        col_iota = S([P, G], F16)
        eps_x = S([1]); eps_k = S([1]); eps_den = S([1]); eps_b = S([1]); eps_t = S([1])
        qnw = S([KT])
        logits = S([NT, E]); top_v = S([NT, E]); top_i = S([NT, E], U32)
        gate_hl = S([2, KT * E], F16)
        gate_bias = S([E])
        ln_st = S([2, 12]); ln_mv = S([2, 2]); ln_sd = S([2, 1]); ln_rs = S([2, 1]); tiny = S([8])
        table_at = S.at
        key16 = S([STEPS], F16); lo16 = S([STEPS], F16); whi = S([STEPS], F16); wlo = S([STEPS], F16)
        win_at = S([STEPS], I32)
        one_hot = [S([3, P, G], F16) for _ in range(2)]
        key_hot = S([P, G], F16)
        stage_at = S.at
        stage = [S([PIECE]) for _ in range(2)]

        xt = view(XNT_AT, [2, KT, N], F16)
        wkv = view(A_AT, [2, KT, 2048], F16)
        ut = view(A_AT, [2, KT, N], F16)
        tail = Place(A_AT + 40000, A_AT + 65536)
        kvb = [tail([PAIRS, P], F16) for _ in range(2)]
        ksb = [tail([PAIRS, P], F16) for _ in range(2)]
        after_q = tail.at
        wq = [tail([2, KT, P], F16) for _ in range(2)]
        tail.at = after_q
        eps_row = tail([N])
        att = [tail([AW]) for _ in range(2)]
        w_acc = view(C_AT, [WINDOWS * P])

        C = Place(C_AT, S_AT)
        src_i = C([3, P], I32); dst_i = C([3, P], I32)
        ew = C([3, P])
        key_c = C([3, P]); lo_c = C([3, P]); hi_i = C([3, P], I32)
        hi_f = C([3, P]); big = C([3, P])
        w_first = C([3]); w_last = C([3]); ends_i = C([3, 2], I32); n_win = C([3]); first = C([3])
        past = C([3]); shift = C([3])
        pick = C([3, STEPS])
        step_iota = C([STEPS])
        win_pick = C([3, STEPS])
        win_f = C([STEPS])
        wsc = C([STEPS])

        B = Place(B_AT, C_AT)
        part = [B([2, PIECE], F16) for _ in range(2)]
        b_work = B.at
        xs = [B([D]) for _ in range(2)]
        xn = [B([D]) for _ in range(2)]
        B.at = b_work
        knw = B([D])
        kw = B([512])
        kt_ = [B([D], F16) for _ in range(2)]
        vt_ = [B([PAIRS, 130], F16) for _ in range(2)]
        junk = B([512], F16)
        B.at = b_work
        u32 = [B([GW]) for _ in range(2)]
        usq = [B([GW]) for _ in range(2)]
        qss = B([3, GW])
        ksf = B([PAIRS])
        head_mask = B([P])
        wo = view(B_AT, [2, KT, D], F16)

        acc_part = view(table_at, [2, WINDOWS // 8, 8 * P], F16)

        T = Place(table_at, TOP)
        xm = [T([D]) for _ in range(2)]
        xn2 = T([D])
        tm = [T([D]) for _ in range(2)]
        tt = T([2, KT, TT], F16)
        bias_b = T([D]); scale_b = T([D])
        gate_f = T([KT * E])
        wg = view(C_AT, [2, KT, D], F16)

        slot_off = [A_AT + 40000, XNT_AT, B_AT]
        eslot = [(view(o, [2, KT * 512], F16), view(o + 16384, [2, 2 * D], F16)) for o in slot_off]
        arena16 = arena[:, :].bitcast(F16)
        b2_b = view(A_AT, [E * D])
        b1_b = view(C_AT, [E * 2 * HID])
        T = Place(C_AT + 16384, S_AT)
        hb = T([2 * HID]); glu = T([HID]); lin = T([HID]); sg = T([HID]); act = T([HID])
        actT = T([2, 2, P], F16)
        blk_i = T([BLOCKS], I32); exp_i = T([BLOCKS], I32); base_i = T([E + 1], I32)
        T2 = Place(table_at, TOP)
        rows = [T2([D]) for _ in range(2)]
        row_idx = [T2([1], I32) for _ in range(2)]
        rowT = [T2([2, KT, P], F16) for _ in range(2)]
        ysb = [T2([D]) for _ in range(2)]
        R = Place(24576, A_AT)
        oh = [R([NT, E]) for _ in range(2)]
        both = R([NT, E]); rank = R([NT, E]); tot = R([NT, E]); pre = R([NT, E])
        cnt = R([E]); cnt_i = R([E], I32); nblk = R([E]); cum = R([E + 1])
        e_iota = R([NT, E]); b_iota = R([BLOCKS]); expf = R([BLOCKS]); offf = R([BLOCKS]); ge = R([BLOCKS])
        slot_f = R([2, NT]); slot_i = [R([NT], I32) for _ in range(2)]
        token_i = R([NT], I32); zero_i = R([BLOCKS], I32); tok_of = R([BLOCKS], I32)
        prob = R([2, NT]); pe_ = R([NT]); pden = R([NT]); idx_f = R([NT, E])
        T3 = Place(C_AT, S_AT)
        cy = [[T3([D]) for _ in range(2)] for _ in range(2)]
        cb = [T3([D]) for _ in range(2)]

        passed = sem("passed"); edges_in = sem("edges_in"); table_in = sem("table_in"); consts = sem("consts")
        x_in = [sem(f"x_in{h}") for h in range(2)]
        xn_ready = sem("xn_ready"); stat_ready = sem("stat_ready"); sd_ready = sem("sd_ready")
        xt_psum = sem("xt_psum"); xt_hi = sem("xt_hi"); xt_done = sem("xt_done")
        stage_in = [sem(f"stage_in{h}") for h in range(2)]
        part_hi = sem("part_hi"); part_lo = sem("part_lo"); piece_scaled = sem("piece_scaled"); piece_done = sem("piece_done")
        part_out = [sem(f"part_out{h}") for h in range(2)]
        table_mm = sem("table_mm"); table_step = sem("table_step"); table_done = sem("table_done")
        knw_in = sem("knw_in"); qn_in = sem("qn_in"); qn_ready = sem("qn_ready"); acc_zero = sem("acc_zero")
        gate_w_ready = sem("gate_w_ready"); t_whole = sem("t_whole"); slots_zero = sem("slots_zero")
        kv_mm = sem("kv_mm"); k_sq = sem("k_sq"); kw_ready = sem("kw_ready"); k_hi = sem("k_hi")
        k_ss = sem("k_ss"); k_sd = sem("k_sd"); k_rs = sem("k_rs"); v_hi = sem("v_hi")
        v_lo = sem("v_lo"); kv_used = sem("kv_used")
        hot_ready = sem("hot_ready"); hot_key = sem("hot_key"); step_mm = sem("step_mm"); acc_done = sem("acc_done")
        dve_step = sem("dve_step"); act_step = sem("act_step"); pool_step = sem("pool_step")
        kvb_zero = sem("kvb_zero"); kvb_ready = sem("kvb_ready"); kvf_hi = sem("kvf_hi")
        wq_in = [sem(f"wq_in{h}") for h in range(2)]
        q_mm = sem("q_mm"); q_evac = sem("q_evac"); q_split = sem("q_split")
        eps_mm = sem("eps_mm"); eps_ready = sem("eps_ready")
        at_mm = sem("at_mm"); at_f = sem("at_f"); at_hi = sem("at_hi"); at_done = sem("at_done")
        acc_hi = sem("acc_hi"); acc_lo = sem("acc_lo")
        acc_out = sem("acc_out")
        wg_in = sem("wg_in"); wo_in = sem("wo_in"); mixc_in = sem("mixc_in"); mixc_ready = sem("mixc_ready")
        xm_in = [sem(f"xm_in{h}") for h in range(2)]
        xb_ready = sem("xb_ready"); mix_mm = sem("mix_mm"); x1_ready = sem("x1_ready"); x1_half = sem("x1_half")
        xn2_ready = sem("xn2_ready"); base_ready = sem("base_ready")
        base_out = [sem(f"base_out{h}") for h in range(2)]
        sd2_ready = sem("sd2_ready"); stat2_ready = sem("stat2_ready")
        t_ready = sem("t_ready")
        t_out = [sem(f"t_out{h}") for h in range(2)]
        tt_psum = sem("tt_psum"); tt_hi = sem("tt_hi"); tt_done = sem("tt_done")
        gate_mm = sem("gate_mm"); gate_done = sem("gate_done")
        route_iota = sem("route_iota"); zero_out = sem("zero_out"); route_mm = sem("route_mm")
        count_in = sem("count_in"); route_exp = sem("route_exp"); pexp_in = sem("pexp_in")
        slots_ready = sem("slots_ready"); tokens_out = sem("tokens_out"); tokens_in = sem("tokens_in")
        bias_in = sem("bias_in"); w_slot_in = sem("w_slot_in"); expert_ready = sem("expert_ready")
        row_in = [sem(f"row_in{h}") for h in range(2)]; idx_ready = sem("idx_ready")
        rt_psum = sem("rt_psum"); rt_hi = sem("rt_hi"); rt_done = sem("rt_done")
        h_mm = sem("h_mm"); h_evac = sem("h_evac"); glu_ready = sem("glu_ready"); sg_ready = sem("sg_ready")
        act_ready = sem("act_ready"); at_psum = sem("at_psum"); a_hi = sem("a_hi"); a_done = sem("a_done")
        y_mm = sem("y_mm"); y_ready = sem("y_ready")
        y_out = [sem(f"y_out{h}") for h in range(2)]
        c_in = [sem(f"c_in{h}") for h in range(2)]
        c_base_in = [sem(f"c_base_in{h}") for h in range(2)]
        c_done = sem("c_done"); stored = [sem(f"stored{h}") for h in range(2)]

        START = 1

        class Steps:
            def __init__(self, eng, s):
                self.eng, self.s, self.base, self.n = eng, s, 0, 0

            def done(self, ins):
                self.n += 1
                ins.then_inc(self.s, 1)
                self.eng.wait_ge(self.s, self.base + self.n)

            def enter(self, i, per):
                self.start = self.base + self.n if not hasattr(self, "start") else self.start
                self.base, self.n, self.per = self.start + i * per, 0, per

            def leave(self, iters):
                assert self.n == self.per, (self.n, self.per)
                self.base, self.n = self.start + iters * self.per, 0
                del self.start

        def apart(eng):
            eng.sem_inc(passed, 1)

        def tok(i, n=TT):
            return bass.ds(i * TT, n)

        x_rows = x.rearrange("(i p) d -> i p d", p=TT)
        out_rows = out.rearrange("(i p) d -> i p d", p=TT)
        t_rows = t_dram.rearrange("(i p) d -> i p d", p=TT)
        base_rows = base_dram.rearrange("(i p) d -> i p d", p=TT)
        wkv_rows = w_qkv.rearrange("(k p) c -> k p c", p=P)

        def tile_dma(eng, to, frm, s):
            for a, b in ((0, 112), (112, TT)):
                eng.dma_start(to[a:b], frm[a:b]).then_inc(s, 16)

        def row_of(rows3, i):
            return rows3[bass.ds(i, 1)].rearrange("o p d -> (o p) d")

        block = ctx.enter_context(nc.Block())

        @block.sync
        def _(sp):
            for i in range(2):
                tile_dma(sp, xs[i], x_rows[i], x_in[i])
            sp.wait_ge(edges_in, 1)
            for t_i, a in ((src_i, src), (dst_i, dst), (ew, edge_weight)):
                full = (CHUNKS - 1) * P
                sp.dma_start(t_i[:, 0:2, :], a[0:2 * P * P].rearrange("(r c e) -> c r e", r=2, e=P)).then_inc(table_in, 16)
                sp.dma_start(t_i[0:LAST_ROWS - 1, 2, :], a[2 * P * P:full].rearrange("(c e) -> c e", e=P)).then_inc(table_in, 16)
                sp.dma_start(t_i[LAST_ROWS - 1:LAST_ROWS, 2, 0:NE - full],
                             a[full:NE].rearrange("(c e) -> c e", c=1)).then_inc(table_in, 16)

            def load_x(i, h):
                sp.wait_ge(xn_ready, i - 1)
                tile_dma(sp, xs[h], row_of(x_rows, i), x_in[h])

            def load_wkv(m, h):
                if not (isinstance(m, int) and m < 2):
                    sp.wait_ge(part_lo, m - 1)
                sp.dma_start(stage[h], wkv_rows[bass.ds(m, 1), :, D:3 * D].rearrange("o p c -> (o p) c")).then_inc(stage_in[h], 16)
            load_wkv(0, 0)
            load_wkv(1, 1)
            load_x(2, 0)
            load_x(3, 1)
            load_wkv(2, 0)
            with sp.Fori(2, NT // 2 - 1) as t:
                for h in range(2):
                    load_x(2 * t + h, h)
                    load_wkv(2 * t + h - 1, 1 - h)
            load_x(NT - 2, 0)
            load_wkv(KT - 1, 1)
            load_x(NT - 1, 1)
            sp.dma_start(qnw, qn_w).then_inc(qn_in, 16)
            def ask(m, h):
                if isinstance(m, int) and m < 2:
                    sp.wait_ge(part_lo, KT - 1 + m)
                else:
                    sp.wait_ge(piece_done, m - 1)
                sp.dma_start(stage[h], w_flat[bass.ds(m, 1)].rearrange("o p c -> (o p) c")).then_inc(stage_in[h], 16)

            def store(m, h):
                sp.wait_ge(piece_done, m + 1)
                for hl in range(2):
                    sp.dma_start(split_dram[hl, bass.ds(m, 1)].rearrange("o p c -> (o p) c"), part[h][:, hl, :]).then_inc(part_out[h], 16)
            ask(0, 0)
            sp.wait_ge(xt_done, 2 + NT)
            sp.dma_start(knw, kn_w.partition_broadcast(P)).then_inc(knw_in, 16)
            ask(1, 1)
            with sp.Fori(0, N_PIECE_Q // 2 - 1) as t:
                for h in range(2):
                    store(2 * t + h, h)
                    ask(2 * t + h + 2, h)
            m0 = N_PIECE_Q - 2
            with sp.Fori(0, (PIECES - N_PIECE_Q) // 2 - KT // 2) as t:
                for h in range(2):
                    store(m0 + 2 * t + h, h)
                    ask(m0 + 2 * t + h + 2, h)
            m1 = m0 + (PIECES - N_PIECE_Q) - KT
            for h in range(2):
                sp.wait_ge(part_out[h], 32 * N_PIECE_Q // 2)

            def load_wq(t, h):
                for hl in range(2):
                    sp.dma_start(wq[h][:, hl, :, :], split_dram[hl, bass.ds(t, 1), :, h * D:(h + 1) * D].rearrange("o p (k c) -> (o p) k c", c=P)).then_inc(wq_in[h], 16)
            sp.wait_ge(kv_used, START + NT)
            for h in range(2):
                load_wq(0, h)
            with sp.Fori(0, KT // 2 - 1) as t:
                for h in range(2):
                    store(m1 + 2 * t + h, h)
                    ask(m1 + 2 * t + h + 2, h)
                for h in range(2):
                    sp.wait_ge(q_mm, 6 * t + 3 * h + 3)
                    load_wq(t + 1, h)
            for h in range(2):
                store(PIECES - 4 + h, h)
                ask(PIECES - 2 + h, h)
            for h in range(2):
                store(PIECES - 2 + h, h)
            for h in range(2):
                sp.wait_ge(part_out[h], 32 * PIECES // 2)
            sp.wait_ge(eps_mm, 3)
            for hl in range(2):
                for m in range(N_PIECE_O):
                    sp.dma_start(wo[:, hl, 2 * m:2 * m + 2, :], split_dram[hl, N_PIECE_Q + m].rearrange("p (k c) -> p k c", c=D)).then_inc(wo_in, 16)
            wg_win = wg_dram.rearrange("l (w m c) -> l m w c", m=P, c=P)
            for k in range(KT):
                sp.wait_ge(acc_lo, k + 1)
                for hl in range(2):
                    sp.dma_start(wg_win[hl, :, 8 * k:8 * k + 8, :], acc_part[:, hl, k, :].rearrange("p (w c) -> p w c", c=P)).then_inc(acc_out, 16)
            sp.wait_ge(acc_out, 16 * 2 * KT)
            for hl in range(2):
                sp.dma_start(wg[:, hl, :, :], wg_dram[hl].rearrange("(k p c) -> p k c", p=P, c=D)).then_inc(wg_in, 16)
            sp.dma_start(bias_b, gnn_bias.partition_broadcast(P)).then_inc(mixc_in, 16)
            sp.dma_start(tm[1], b_out.partition_broadcast(P)).then_inc(mixc_in, 16)
            sp.dma_start(scale_b, norm_scale.partition_broadcast(P)).then_inc(mixc_in, 16)
            sp.dma_start(gate_bias, gate_b.partition_broadcast(P)).then_inc(mixc_in, 16)
            sp.dma_start(gate_f, gate_w).then_inc(mixc_in, 16)

            def load_expert(e, s):
                w1, w2 = eslot[e % 3]
                for hl in range(2):
                    for m in range(2):
                        sp.dma_start(w1[:, hl, m * PIECE:(m + 1) * PIECE], split_dram[hl, N_PIECE_Q + N_PIECE_O + 2 * e + m]).then_inc(s, 16)
                    sp.dma_start(w2[:, hl, :], split_dram[hl, N_PIECE_Q + N_PIECE_O + N_PIECE_1 + e]).then_inc(s, 16)
            tile_dma(sp, xm[0], x_rows[0], xm_in[0])
            tile_dma(sp, xm[1], x_rows[1], xm_in[1])

            def store_mixed(i, h):
                sp.wait_ge(t_ready, i + 1)
                tile_dma(sp, row_of(t_rows, i), tm[h], t_out[h])
                sp.wait_ge(base_ready, i + 1)
                tile_dma(sp, row_of(base_rows, i), xm[h], base_out[h])
            with sp.Fori(0, NT // 2 - 1) as t:
                for h in range(2):
                    store_mixed(2 * t + h, h)
                    sp.wait_ge(base_out[h], 32 * (t + 1))
                    tile_dma(sp, xm[h], row_of(x_rows, 2 * t + h + 2), xm_in[h])
            sp.wait_ge(at_done, START + AT_UNITS)
            load_expert(0, w_slot_in)
            for h in range(2):
                store_mixed(NT - 2 + h, h)
            for h in range(2):
                sp.wait_ge(base_out[h], 16 * NT)
                sp.wait_ge(t_out[h], 16 * NT)
            sp.sem_inc(t_whole, 1)
            sp.wait_ge(gate_done, START + NT)
            sp.dma_start(b1_b, mlp1_b.partition_broadcast(P)).then_inc(bias_in, 16)
            sp.dma_start(b2_b, mlp2_b.partition_broadcast(P)).then_inc(bias_in, 16)
            sp.wait_ge(w_slot_in, 96)
            sp.sem_inc(expert_ready, 1)
            sp.wait_ge(count_in, 1)
            for e in range(1, E):
                if e >= 3:
                    done = sp.value_load(base_i[0:1, e - 2:e - 1], min_val=1, max_val=BLOCKS)
                    sp.wait_ge(y_mm, done)
                load_expert(e, w_slot_in)
                sp.wait_ge(w_slot_in, 96 * (e + 1))
                sp.sem_inc(expert_ready, 1)
            for i in range(NT):
                sp.wait_ge(c_done, i + 1)
                tile_dma(sp, out_rows[i], cb[i % 2], stored[i % 2])
            for h in range(2):
                sp.wait_ge(stored[h], 16 * NT)

        @block.gpsimd
        def _(pool):
            st = Steps(pool, pool_step)
            for s in (q_split, at_done):
                pool.sem_inc(s, START)
            pool.memset(dst_i[:, 2, :], 2047).then_inc(pool_step, 1)
            pool.memset(src_i[:, 2, :], 0).then_inc(pool_step, 1)
            pool.memset(ew[:, 2, :], 0.0).then_inc(pool_step, 1)
            st.n = 3
            pool.wait_ge(pool_step, 3)
            pool.sem_inc(edges_in, 1)
            st.done(pool.memset(ident, 0.0))
            pool.affine_select(out=ident, in_=ident, pattern=[[-1, P]], compare_op=ALU.not_equal, fill=1.0,
                               base=0, channel_multiplier=1).then_inc(consts, 1)
            pool.memset(ones, 1.0).then_inc(consts, 1)
            st.done(pool.memset(upper, 1.0))
            pool.affine_select(out=upper, in_=upper, pattern=[[1, P]], compare_op=ALU.is_gt, fill=0.0,
                               base=0, channel_multiplier=-1).then_inc(consts, 1)
            pool.iota(step_iota, [[1, STEPS]], base=0, channel_multiplier=0,
                      allow_small_or_imprecise_dtypes=True).then_inc(consts, 1)
            pool.iota(col_iota, [[1, P], [0, G]], base=0, channel_multiplier=0,
                      allow_small_or_imprecise_dtypes=True).then_inc(consts, 1)
            pool.memset(zeros, 0.0).then_inc(consts, 1)
            for tile_, v in ((eps_x, EPS_LN / (SX * SX)), (eps_k, EPS_Q * 65536.0), (eps_den, 64e-12 * EPS_Q),
                             (eps_b, EPS_LN), (eps_t, EPS_T / (ST * ST))):
                pool.memset(tile_, v).then_inc(consts, 1)

            pool.wait_ge(consts, 11)
            pool.wait_ge(table_done, 1)
            pool.memset(w_acc, 0.0).then_inc(acc_zero, 1)

            def piece_lo(t, h, a=0, b=PIECE):
                if a == 0:
                    pool.wait_ge(part_hi, KT + 2 * t + h + 1)
                ins = pool.tensor_tensor(part[h][:, 1, a:b], stage[h][:, a:b], part[h][:, 0, a:b], ALU.subtract)
                if b == PIECE:
                    ins.then_inc(piece_done, 1)
            for h in range(2):
                piece_lo(0, h)
            with pool.Fori(0, NT) as t:
                for h in range(2):
                    piece_lo(1 + t, h)
            pool.wait_ge(kv_used, START + NT)
            for t_ in kvb:
                pool.memset(t_, 0.0).then_inc(kvb_zero, 1)
            st.done(pool.memset(head_mask, 0.0))
            for a in (0, 64):
                pool.memset(head_mask[a:a + 64, a:a + 64], 1.0).then_inc(kvb_zero, 1)
            pool.wait_ge(kvb_zero, 4)
            st.done(pool.memset(qss, 0.0))
            for h in range(2):
                piece_lo(NT + 1, h)
            with pool.Fori(0, KT // 2) as t:
                for u in range(6):
                    h, g = divmod(u, 3)
                    a, n = GRP[g]
                    pool.wait_ge(q_evac, START + 6 * t + u + 1)
                    pool.tensor_copy(ut[:, 0, bass.ds(2 * t + h, 1), a:a + n].rearrange("p o n -> p (o n)"),
                                     u32[u % 2][:, 0:n]).then_inc(q_split, 1)
                    pool.wait_ge(q_split, START + 3 * (6 * t + u) + 1)
                    pool.tensor_tensor(ut[:, 1, bass.ds(2 * t + h, 1), a:a + n].rearrange("p o n -> p (o n)"),
                                       u32[u % 2][:, 0:n],
                                       ut[:, 0, bass.ds(2 * t + h, 1), a:a + n].rearrange("p o n -> p (o n)"),
                                       ALU.subtract).then_inc(q_split, 1)
                    pool.tensor_tensor(qss[:, g, 0:n], qss[:, g, 0:n], usq[u % 2][:, 0:n], ALU.add).then_inc(q_split, 1)
                    pool.wait_ge(q_split, START + 3 * (6 * t + u) + 3)
                    if g > 0:
                        piece_lo(12 + t, h, (g - 1) * PIECE // 2, g * PIECE // 2)

            def attend_lo(j, g, unit):
                pool.wait_ge(at_hi, unit + 1)
                pool.tensor_tensor(ut[:, 1, j, bass.ds(g * AW, AW)], att[j % 2], ut[:, 0, j, bass.ds(g * AW, AW)],
                                   ALU.subtract).then_inc(at_done, 1)
            for j in range(PAIRS):
                attend_lo(j, 0, j)

            pool.wait_ge(mixc_in, 80)
            pool.tensor_tensor(bias_b, bias_b, tm[1], ALU.add).then_inc(mixc_ready, 1)
            pool.wait_ge(mixc_ready, 1)

            def mix_in(i, h, t):
                pool.wait_ge(xm_in[h], 32 * (t + 1))
                pool.tensor_tensor(xm[h][0:TT], xm[h][0:TT], bias_b[0:TT], ALU.add).then_inc(xb_ready, 1)

            def mix_out(i, h):
                pool.wait_ge(xn2_ready, i + 1)
                pool.tensor_tensor(xm[h][0:TT], xm[h][0:TT], xn2[0:TT], ALU.add).then_inc(base_ready, 1)
            mix_in(0, 0, 0)
            mix_in(1, 1, 0)
            with pool.Fori(0, NT // 2 - 1) as t:
                for h in range(2):
                    for j in range(4 * h, 4 * h + 4):
                        attend_lo(j, t + 1, PAIRS * (t + 1) + j)
                    mix_out(2 * t + h, h)
                    mix_in(2 * t + h + 2, h, t + 1)
            mix_out(NT - 2, 0)
            mix_out(NT - 1, 1)

            pool.wait_ge(gate_done, START + NT)
            pool.iota(e_iota, [[0, NT], [1, E]], base=0, channel_multiplier=0,
                      allow_small_or_imprecise_dtypes=True).then_inc(route_iota, 1)
            pool.iota(b_iota, [[1, BLOCKS]], base=0, channel_multiplier=0,
                      allow_small_or_imprecise_dtypes=True).then_inc(route_iota, 1)
            pool.iota(token_i, [[TT, NT]], base=0, channel_multiplier=1).then_inc(route_iota, 1)
            pool.memset(zero_i, 0).then_inc(route_iota, 1)
            pool.wait_ge(route_iota, 4)
            pool.dma_start(slot_token_dram.rearrange("(p b) o -> p (b o)", p=P), zero_i).then_inc(zero_out, 16)
            pool.wait_ge(zero_out, 16)
            pool.wait_ge(slots_ready, 1)
            for c in range(2):
                for i in range(NT):
                    pool.indirect_dma_start(
                        out=slot_token_dram, out_offset=bass.IndirectOffsetOnAxis(ap=slot_i[c][0:TT, i:i + 1], axis=0),
                        in_=token_i[0:TT, i:i + 1], in_offset=None).then_inc(tokens_in, 16)
            pool.wait_ge(tokens_in, 16 * 2 * NT)
            with nc.allow_non_contiguous_dma(reason="one int32 per slot"):
                pool.dma_start(tok_of, slot_token_dram.rearrange("(b p) o -> p (b o)", p=P)).then_inc(tokens_in, 16)
            pool.wait_ge(tokens_in, 16 * (2 * NT + 1))
            pool.wait_ge(t_whole, 1)

            def gather(b, s):
                pool.tensor_copy(row_idx[s], tok_of[:, bass.ds(b, 1)]).then_inc(idx_ready, 1)
                pool.wait_ge(idx_ready, b + 1)
                apart(pool)
                pool.indirect_dma_start(out=rows[s], out_offset=None, in_=t_dram,
                                        in_offset=bass.IndirectOffsetOnAxis(ap=row_idx[s], axis=0)).then_inc(row_in[s], 16)
            gather(0, 0)
            gather(1, 1)
            with pool.Fori(0, (BLOCKS - 3) // 2) as t:
                for h in range(2):
                    pool.wait_ge(rt_psum, 2 * t + h + 1)
                    gather(2 * t + h + 2, h)
            pool.wait_ge(rt_psum, BLOCKS - 2)
            gather(BLOCKS - 1, (BLOCKS - 1) % 2)
            for h in range(2):
                pool.wait_ge(y_out[h], START + 16 * ((BLOCKS + 1 - h) // 2))
            pool.wait_ge(y_ready, START + BLOCKS)
            for i in range(NT):
                if i >= 2:
                    pool.wait_ge(c_done, i - 1)
                    pool.wait_ge(stored[i % 2], 32 * (i // 2))
                for c in range(2):
                    pool.indirect_dma_start(
                        out=cy[i % 2][c][0:TT], out_offset=None, in_=y_dram,
                        in_offset=bass.IndirectOffsetOnAxis(ap=slot_i[c][0:TT, i:i + 1], axis=0)).then_inc(c_in[i % 2], 16)
                tile_dma(pool, cb[i % 2], base_rows[i], c_base_in[i % 2])

        @block.tensor
        def _(pe):
            for s in (kv_used, gate_mm):
                pe.sem_inc(s, START)
            pe.wait_ge(consts, 11)
            pe.wait_ge(table_step, 1)
            rows_of = [P, P, LAST_ROWS]
            for r in range(3):
                for q in range(r):
                    pe.matmul(bank[0][:, r:r + 1], ones[0:rows_of[q], :], n_win[0:rows_of[q], q:q + 1], start=(q == 0), stop=False)
                mm = pe.matmul(bank[0][:, r:r + 1], upper[0:rows_of[r], :], n_win[0:rows_of[r], r:r + 1], start=(r == 0), stop=True)
            mm.then_inc(table_mm, 1)
            pe.wait_ge(table_step, 2)

            def table_column(c):
                for r in range(3):
                    n = rows_of[r]
                    lhs, rhs = (ones[0:n, :], win_pick) if c == 3 else ((key_c, lo_c, ew)[c][0:n, r, :], pick)
                    mm = pe.matmul(bank[4 + c][:, 0:STEPS], lhs, rhs[0:n, r, :], start=(r == 0), stop=(r == 2))
                mm.then_inc(table_mm, 1)

            def xt_tile(i, h):
                pe.wait_ge(xn_ready, i + 1)
                pe.wait_ge(xt_done, i + 1)
                for k in range(KT):
                    mm = pe.transpose(bank[2 * h + k // 4][:, (k % 4) * TT:(k % 4 + 1) * TT], xn[h][0:TT, k * P:(k + 1) * P], ident[0:TT, 0:TT])
                mm.then_inc(xt_psum, 1)
            table_column(0)
            xt_tile(0, 0)
            table_column(1)
            xt_tile(1, 1)
            table_column(2)
            table_column(3)
            with pe.Fori(1, NT // 2) as t:
                for h in range(2):
                    xt_tile(2 * t + h, h)
            pe.wait_ge(table_done, 1)
            pe.wait_ge(xt_done, 2 + NT)
            pe.wait_ge(part_lo, KT)
            for b in range(3):
                pe.matmul(bank[3 + b][:, :], zeros, wkv[:, 0, 0, 0:512], start=True, stop=False, skip_group_check=True)

            def kv_unit(i, b, c0):
                for k in range(KT):
                    for n, (l, r) in enumerate(((0, 0), (0, 1), (1, 0))):
                        mm = pe.matmul(bank[b][0:TT, :], xt[:, l, k, tok(i)], wkv[:, r, k, c0:c0 + 512],
                                       start=(k == 0 and n == 0), stop=(k == KT - 1 and n == 2))
                mm.then_inc(kv_mm, 1)

            def kv_sums():
                for p in range(PAIRS):
                    for l, r in ((0, 0), (0, 1), (1, 0)):
                        mm = pe.matmul(bank[3 + p // 3][:, (p % 3) * 130:(p % 3) * 130 + 129], kt_[l][0:TT, p * P:(p + 1) * P],
                                       vt_[r][0:TT, p, 0:129], start=False, stop=False, skip_group_check=True)
                mm.then_inc(kv_used, 1)

            def steps(n, h):
                pe.wait_ge(hot_ready, n + 1)
                pe.wait_ge(acc_done, START + G * n)
                for j in range(G):
                    o = bank[6 + j // 4][:, (j % 4) * P:(j % 4 + 1) * P]
                    pe.matmul(o, one_hot[h][:, 1, :, j], one_hot[h][:, 0, :, j], start=True, stop=False)
                    mm = pe.matmul(o, one_hot[h][:, 2, :, j], one_hot[h][:, 0, :, j], start=False, stop=True)
                    if j % 4 == 3:
                        mm.then_inc(step_mm, 1)

            def kv_tile(i, s, first=False):
                kv_unit(i, 0, 0)
                if not first:
                    pe.wait_ge(v_lo, 2 * i)
                    kv_sums()
                steps(3 * i, s % 2)
                kv_unit(i, 1, 512)
                kv_unit(i, 2, 1024)
                steps(3 * i + 1, (s + 1) % 2)
                pe.wait_ge(kw_ready, 2 * i + 2)
                kv_unit(i, 1, 1536)
                steps(3 * i + 2, (s + 2) % 2)
            kv_tile(0, 0, True)
            kv_tile(1, 3)
            with pe.Fori(1, NT // 2) as t:
                for h in range(2):
                    kv_tile(2 * t + h, 3 * h)
            pe.wait_ge(v_lo, 2 * NT)
            kv_sums()

            with pe.Fori(0, KT // 2) as t:
                for u in range(6):
                    h, g = divmod(u, 3)
                    a, n = GRP[g]
                    if g == 0:
                        pe.wait_ge(wq_in[h], 32 * (t + 1))
                    pe.wait_ge(q_evac, START + 6 * t + max(u - 2, 0))
                    for k in range(KT):
                        for c, (l, r) in enumerate(((0, 0), (1, 0), (0, 1))):
                            mm = pe.matmul(bank[u % 3][:, 0:n], wq[h][:, l, k, :], xt[:, r, k, a:a + n],
                                           start=(k == 0 and c == 0), stop=(k == KT - 1 and c == 2))
                    mm.then_inc(q_mm, 1)
                    steps(KV_GROUPS + 6 * t + u, u % 2)
            pe.wait_ge(q_split, START + 9 * KT)
            pe.wait_ge(q_evac, START + 3 * KT)
            pe.wait_ge(kvb_ready, 1)
            for g in range(3):
                pe.matmul(bank[g][:, 0:GRP[g][1]], ones, qss[:, g, 0:GRP[g][1]], start=True, stop=True).then_inc(eps_mm, 1)
            def attend_unit(j, g, unit):
                o = bank[2 + j % 2]
                pe.wait_ge(at_f, START + (max(unit - 1, 0) if isinstance(unit, int) else unit - 1))
                for at, w in ((0, kvb), (256, ksb)):
                    for c, (l, r) in enumerate(((0, 0), (1, 0), (0, 1))):
                        mm = pe.matmul(o[:, at:at + AW], w[l][:, j, :], ut[:, r, j, bass.ds(g * AW, AW)], start=(c == 0), stop=(c == 2))
                mm.then_inc(at_mm, 1)
            pe.wait_ge(eps_ready, 3)
            for j in range(PAIRS):
                attend_unit(j, 0, j)

            pe.wait_ge(wo_in, 16 * 2 * N_PIECE_O)

            def mix_tile(i, h, t, attend=True):
                if h == 0:
                    pe.wait_ge(at_done, START + PAIRS * (t + 1))
                for half in range(2):
                    c0 = half * 512
                    if not (isinstance(i, int) and i == 0):
                        pe.wait_ge(x1_half, 2 * i - 1 + half)
                    for m, (a_, w_) in enumerate(((ut, wo), (xt, wg))):
                        if m == 1 and isinstance(i, int) and i == 0 and half == 0:
                            pe.wait_ge(wg_in, 32)
                        for k in range(KT):
                            for c, (l, r) in enumerate(((0, 0), (0, 1), (1, 0))):
                                mm = pe.matmul(bank[half][0:TT, :], a_[:, l, k, tok(i)], w_[:, r, k, c0:c0 + 512],
                                               start=(m == 0 and k == 0 and c == 0), stop=(m == 1 and k == KT - 1 and c == 2))
                        if m == 1:
                            mm.then_inc(mix_mm, 1)
                        if attend:
                            j = 4 * h + 2 * half + m
                            attend_unit(j, t + 1, PAIRS * (t + 1) + j)

            def gate_tile(i, h):
                pe.wait_ge(t_ready, i + 1)
                for k in range(KT):
                    mm = pe.transpose(bank[4 + k // 4][:, (k % 4) * TT:(k % 4 + 1) * TT], tm[h][0:TT, k * P:(k + 1) * P], ident[0:TT, 0:TT])
                mm.then_inc(tt_psum, 1)

            def gate_logits(i):
                pe.wait_ge(tt_done, i + 1)
                pe.wait_ge(gate_done, START + i)
                for k in range(KT):
                    for c, (l, r) in enumerate(((0, 0), (0, 1), (1, 0))):
                        mm = pe.matmul(bank[6][0:TT, 0:E], tt[:, l, k, :], gate_hl[:, r, k * E:(k + 1) * E],
                                       start=(k == 0 and c == 0), stop=(k == KT - 1 and c == 2))
                mm.then_inc(gate_mm, 1)
            mix_tile(0, 0, 0)
            mix_tile(1, 1, 0)
            gate_tile(0, 0)
            pe.wait_ge(gate_w_ready, 1)
            with pe.Fori(1, NT // 2 - 1) as t:
                for h in range(2):
                    i = 2 * t + h
                    mix_tile(i, h, t)
                    gate_logits(i - 2)
                    gate_tile(i - 1, 1 - h)
            for h in range(2):
                i = NT - 2 + h
                mix_tile(i, h, NT // 2 - 1, attend=False)
                gate_logits(i - 2)
                gate_tile(i - 1, 1 - h)
            gate_logits(NT - 2)
            gate_tile(NT - 1, 1)
            gate_logits(NT - 1)
            pe.wait_ge(route_mm, 1)
            pe.matmul(bank[0][0:TT, 0:NT * E], upper[0:TT, 0:TT], both[0:TT].rearrange("p a b -> p (a b)"), start=True, stop=True)
            pe.matmul(bank[1][:, 0:NT * E], ones[0:TT, :], both[0:TT].rearrange("p a b -> p (a b)"), start=True, stop=True).then_inc(route_mm, 1)
            def row_T(b, s, q):
                pe.wait_ge(row_in[s], 16 * (q + 1))
                for k in range(KT):
                    mm = pe.transpose(bank[2 + 2 * s + k // 4][:, (k % 4) * P:(k % 4 + 1) * P], rows[s][:, k * P:(k + 1) * P], ident)
                mm.then_inc(rt_psum, 1)

            def up(b, s, off, half):
                if half == 0:
                    pe.wait_ge(rt_done, b + 1)
                    pe.wait_ge(h_evac, b)
                for k in range(4 * half, 4 * half + 4):
                    for c, (l, r) in enumerate(((0, 0), (0, 1), (1, 0))):
                        mm = pe.matmul(bank[6][:, :], rowT[s][:, l, k, :], arena16[:, bass.ds(off + (r * KT + k) * 512, 512)],
                                       start=(k == 0 and c == 0), stop=(k == KT - 1 and c == 2))
                if half == 1:
                    mm.then_inc(h_mm, 1)

            def act_T(b):
                pe.wait_ge(act_ready, b + 1)
                for k in range(2):
                    mm = pe.transpose(bank[7][:, k * P:(k + 1) * P], act[:, k * P:(k + 1) * P], ident)
                mm.then_inc(at_psum, 1)

            def down(b):
                off = pe.value_load(blk_i[0:1, bass.ds(b, 1)], min_val=0, max_val=TOP // 2 - 12288)
                pe.wait_ge(a_done, b + 1)
                pe.wait_ge(y_ready, START + b)
                for half in range(2):
                    for k in range(2):
                        for c, (l, r) in enumerate(((0, 0), (0, 1), (1, 0))):
                            mm = pe.matmul(bank[half][:, :], actT[:, l, k, :], arena16[:, bass.ds(off + 8192 + r * 2048 + k * D + half * 512, 512)],
                                           start=(k == 0 and c == 0), stop=(k == 1 and c == 2))
                mm.then_inc(y_mm, 1)

            def expert_block(b, s, q, first=False, last=False):
                off = pe.value_load(blk_i[0:1, bass.ds(b, 1)], min_val=0, max_val=TOP // 2 - 12288)
                need = pe.value_load(exp_i[0:1, bass.ds(b, 1)], min_val=0, max_val=E)
                if not last:
                    row_T(b + 1, 1 - s, q + s)
                pe.wait_ge(expert_ready, need + 1)
                up(b, s, off, 0)
                if not first:
                    act_T(b - 1)
                up(b, s, off, 1)
                if not first:
                    down(b - 1)
            pe.wait_ge(count_in, 1)
            row_T(0, 0, 0)
            expert_block(0, 0, 0, first=True)
            with pe.Fori(0, (BLOCKS - 3) // 2) as t:
                expert_block(2 * t + 1, 1, t)
                expert_block(2 * t + 2, 0, t + 1)
            expert_block(BLOCKS - 2, 1, (BLOCKS - 2) // 2)
            expert_block(BLOCKS - 1, 0, (BLOCKS - 1) // 2, last=True)
            act_T(BLOCKS - 1)
            down(BLOCKS - 1)

        @block.scalar
        def _(act_e):
            a_ = act_e
            st = Steps(a_, act_step)
            for s in (q_evac, y_out[0], y_out[1]):
                a_.sem_inc(s, START)
            a_.wait_ge(consts, 11)

            def xt_copy(i, h):
                a_.wait_ge(xt_psum, i + 1)
                apart(a_)
                for b in range(2):
                    a_.activation(xt[:, 0, 4 * b:4 * b + 4, tok(i)], bank[2 * h + b][:, 0:4 * TT].rearrange("p (k n) -> p k n", n=TT), ACT.Copy).then_inc(xt_hi, 1)

            def ln_sqrt(i, h):
                a_.wait_ge(stat_ready, i + 1)
                a_.activation(ln_sd[0:TT, h, :], ln_mv[0:TT, h, 1:2], ACT.Sqrt, bias=eps_x[0:TT], scale=1.0 / (SX * SX)).then_inc(sd_ready, 1)
            def wkv_hi(m, h, t):
                a_.wait_ge(stage_in[h], 16 * (t + 1))
                apart(a_)
                a_.activation(wkv[:, 0, bass.ds(m, 1), :].rearrange("p o c -> p (o c)"), stage[h], ACT.Copy, scale=SW).then_inc(part_hi, 1)
            ln_sqrt(0, 0)
            ln_sqrt(1, 1)
            with a_.Fori(1, NT // 2) as t:
                for h in range(2):
                    ln_sqrt(2 * t + h, h)
                    xt_copy(2 * t + h - 2, h)
                    wkv_hi(2 * t + h - 2, h, t - 1)
            xt_copy(NT - 2, 0)
            xt_copy(NT - 1, 1)

            def piece_hi(t, h):
                a_.wait_ge(stage_in[h], 16 * (KT // 2 + t + 1))
                a_.activation(stage[h], stage[h], ACT.Copy, scale=SW).then_inc(piece_scaled, 1)
                a_.wait_ge(piece_scaled, 2 * t + h + 1)
                if not (isinstance(t, int) and t == 0):
                    a_.wait_ge(part_out[h], 32 * t)
                a_.activation(part[h][:, 0, :], stage[h], ACT.Copy).then_inc(part_hi, 1)
            for h in range(2):
                piece_hi(0, h)

            def k_half(i, c):
                a_.wait_ge(kv_mm, 4 * i + c + 1)
                a_.activation(junk[0:TT], bank[c][0:TT, :], ACT.Square, accum_out=tiny[0:TT, c:c + 1]).then_inc(k_sq, 1)
                a_.wait_ge(kw_ready, 2 * i + c + 1)
                a_.activation(kt_[0][0:TT, c * 512:(c + 1) * 512], kw[0:TT], ACT.Relu).then_inc(k_hi, 1)

            def v_half(i, c):
                a_.wait_ge(kv_mm, 4 * i + 3 + c)
                a_.activation(vt_[0][0:TT, 4 * c:4 * c + 4, 0:P], bank[2 - c][0:TT, :].rearrange("p (a b) -> p a b", b=P),
                              ACT.Copy, scale=tiny[0:TT, 4:5]).then_inc(v_hi, 1)

            def kv_tile(i, t, h):
                k_half(i, 0)
                piece_hi(1 + 2 * t + h, 0)
                k_half(i, 1)
                a_.wait_ge(k_ss, i + 1)
                a_.activation(tiny[0:TT, 3:4], tiny[0:TT, 2:3], ACT.Sqrt, bias=eps_k[0:TT], scale=2.0 ** -20).then_inc(k_sd, 1)
                a_.wait_ge(k_rs, i + 1)
                v_half(i, 0)
                piece_hi(1 + 2 * t + h, 1)
                v_half(i, 1)
            with a_.Fori(0, NT // 2) as t:
                for h in range(2):
                    kv_tile(2 * t + h, t, h)
            a_.wait_ge(kv_used, START + NT)
            a_.wait_ge(kvb_zero, 4)
            for p in range(PAIRS):
                for r0 in (0, 64):
                    c0 = (p % 3) * 130 + r0
                    ins = a_.activation(kvb[0][r0:r0 + 64, p, r0:r0 + 64], bank[3 + p // 3][r0:r0 + 64, c0:c0 + 64], ACT.Copy, scale=2.0 ** -12)
            ins.then_inc(kvf_hi, 1)
            for h in range(2):
                piece_hi(NT + 1, h)

            a_.wait_ge(qn_ready, 1)
            with a_.Fori(0, KT // 2) as t:
                for u in range(6):
                    h, g = divmod(u, 3)
                    n = GRP[g][1]
                    a_.wait_ge(q_mm, 6 * t + u + 1)
                    a_.wait_ge(q_split, START + 3 * (6 * t + max(u - 1, 0)))
                    a_.activation(usq[u % 2][:, 0:n], bank[u % 3][:, 0:n], ACT.Square, scale=1.0 / (SX * SW)).then_inc(act_step, 1)
                    a_.activation(u32[u % 2][:, 0:n], bank[u % 3][:, 0:n], ACT.Relu, scale=qnw[:, bass.ds(2 * t + h, 1)]).then_inc(q_evac, 1)
                    if u % 3 == 0:
                        piece_hi(12 + t, u // 3)
            a_.wait_ge(hot_ready, GROUPS + 2)
            for g in range(3):
                a_.wait_ge(eps_mm, g + 1)
                a_.activation(eps_row[:, GRP[g][0]:sum(GRP[g])], bank[g][:, 0:GRP[g][1]], ACT.Sqrt, bias=eps_den, scale=64e-12 / D).then_inc(eps_ready, 1)
            a_.wait_ge(piece_done, PIECES)
            for k in range(8):
                a_.activation(acc_part[:, 0, k, :], w_acc[:, k * D:(k + 1) * D], ACT.Copy).then_inc(acc_hi, 1)

            def attend_hi(j, g, unit):
                a_.wait_ge(at_f, START + unit + 1)
                apart(a_)
                a_.activation(ut[:, 0, j, bass.ds(g * AW, AW)], att[j % 2], ACT.Copy).then_inc(at_hi, 1)

            def mix_sqrt(i, h):
                a_.wait_ge(stat2_ready, 2 * i + 1)
                a_.activation(ln_sd[0:TT, h, :], ln_mv[0:TT, h, 1:2], ACT.Sqrt, bias=eps_b[0:TT]).then_inc(sd2_ready, 1)
                a_.wait_ge(stat2_ready, 2 * i + 2)
                a_.activation(tiny[0:TT, 1:2], tiny[0:TT, 0:1], ACT.Sqrt, bias=eps_t[0:TT], scale=1.0 / (ST * ST)).then_inc(sd2_ready, 1)

            def tt_copy(i):
                a_.wait_ge(tt_psum, i + 1)
                a_.wait_ge(gate_mm, START + i)
                for b in range(2):
                    a_.activation(tt[:, 0, 4 * b:4 * b + 4, :], bank[4 + b][:, 0:4 * TT].rearrange("p (k n) -> p k n", n=TT), ACT.Copy).then_inc(tt_hi, 1)

            def mix_period(i, h, t, attend=True, first=False):
                if attend:
                    for j in range(4 * h, 4 * h + 4):
                        attend_hi(j, t + 1, PAIRS * (t + 1) + j)
                if not first:
                    tt_copy(i - 1)
                mix_sqrt(i, h)
            for j in range(PAIRS):
                attend_hi(j, 0, j)
            mix_period(0, 0, 0, first=True)
            mix_period(1, 1, 0)
            with a_.Fori(1, NT // 2 - 1) as t:
                for h in range(2):
                    mix_period(2 * t + h, h, t)
            for h in range(2):
                mix_period(NT - 2 + h, h, NT // 2 - 1, attend=False)
            tt_copy(NT - 1)
            a_.wait_ge(route_exp, 1)
            a_.activation(pe_[0:TT], pe_[0:TT], ACT.Exp).then_inc(pexp_in, 1)
            def row_hi(b, s, first=False):
                a_.wait_ge(rt_psum, b + 1)
                if not first:
                    a_.wait_ge(h_mm, b - 1)
                for q in range(2):
                    a_.activation(rowT[s][:, 0, 4 * q:4 * q + 4, :], bank[2 + 2 * s + q][:, :].rearrange("p (k n) -> p k n", n=P), ACT.Copy).then_inc(rt_hi, 1)

            def act_hi(b):
                a_.wait_ge(at_psum, b + 1)
                a_.wait_ge(y_mm, b)
                a_.activation(actT[:, 0, :, :], bank[7][:, 0:2 * P].rearrange("p (k n) -> p k n", n=P), ACT.Copy).then_inc(a_hi, 1)

            def sigmoid(b):
                a_.wait_ge(glu_ready, b + 1)
                a_.wait_ge(act_ready, b)
                a_.activation(sg, glu, ACT.Sigmoid, scale=1.702).then_inc(sg_ready, 1)

            def store_y(b, s):
                a_.wait_ge(y_ready, START + b + 1)
                a_.dma_start(y_dram[bass.ds(b * P, P), :], ysb[s]).then_inc(y_out[s], 16)
            row_hi(0, 0, first=True)
            row_hi(1, 1, first=True)
            sigmoid(0)
            row_hi(2, 0)
            act_hi(0)
            sigmoid(1)
            with a_.Fori(0, (BLOCKS - 3) // 2) as t:
                for h in range(2):
                    b = 2 * t + h + 2
                    row_hi(b + 1, 1 - h)
                    act_hi(b - 1)
                    store_y(b - 2, h)
                    sigmoid(b)
            act_hi(BLOCKS - 2)
            store_y(BLOCKS - 3, (BLOCKS - 3) % 2)
            sigmoid(BLOCKS - 1)
            act_hi(BLOCKS - 1)
            store_y(BLOCKS - 2, (BLOCKS - 2) % 2)
            store_y(BLOCKS - 1, (BLOCKS - 1) % 2)

        @block.vector
        def _(v):
            st = Steps(v, dve_step)
            v.sem_inc(xt_done, 2)
            for s in (at_f, gate_done, y_ready, acc_done):
                v.sem_inc(s, START)
            v.wait_ge(consts, 11)
            v.wait_ge(table_in, 16 * 9)
            flat = lambda a: a.rearrange("p a b -> p (a b)")
            st.done(v.tensor_scalar(flat(hi_i), flat(src_i), 7, None, ALU.logical_shift_right))
            st.done(v.tensor_copy(flat(hi_f), flat(hi_i)))
            st.done(v.tensor_scalar(flat(hi_i), flat(src_i), P - 1, None, ALU.bitwise_and))
            v.tensor_copy(flat(lo_c), flat(hi_i))
            v.tensor_scalar(flat(big), flat(hi_f), float(D // P), 16384.0, ALU.is_ge, ALU.mult)
            st.done(v.tensor_copy(flat(key_c), flat(dst_i)))
            st.done(v.scalar_tensor_tensor(flat(key_c), flat(key_c), float(D // P), flat(hi_f), ALU.mult, ALU.add))
            st.done(v.tensor_tensor(flat(key_c), flat(key_c), flat(big), ALU.add))
            for c, col in ((0, 0), (1, P - 1)):
                ins = v.tensor_scalar(ends_i[:, :, c], dst_i[:, :, col], 4, None, ALU.logical_shift_right)
            st.done(ins)
            v.tensor_scalar(w_first, ends_i[:, :, 0], float(WINDOWS - 1), None, ALU.min)
            st.done(v.tensor_scalar(w_last, ends_i[:, :, 1], float(WINDOWS - 1), None, ALU.min))
            v.scalar_tensor_tensor(n_win, w_last, 1.0, w_first, ALU.add, ALU.subtract).then_inc(table_step, 1)
            v.wait_ge(table_mm, 1)
            st.done(v.tensor_copy(first, bank[0][:, 0:3]))
            v.tensor_tensor(past, first, n_win, ALU.add)
            st.done(v.tensor_tensor(shift, w_first, first, ALU.subtract))
            for r in range(3):
                st.done(v.tensor_scalar(pick[:, r, :], step_iota, first[:, r:r + 1], None, ALU.is_ge))
                st.done(v.scalar_tensor_tensor(pick[:, r, :], step_iota, past[:, r:r + 1], pick[:, r, :], ALU.is_lt, ALU.mult))
                ins = v.scalar_tensor_tensor(win_pick[:, r, :], step_iota, shift[:, r:r + 1], pick[:, r, :], ALU.add, ALU.mult)
            ins.then_inc(table_step, 1)

            def read_table():
                v.wait_ge(table_mm, 5)
                st.done(v.tensor_copy(win_f, bank[7][:, 0:STEPS]))
                v.scalar_tensor_tensor(key16, win_f, -float(P), bank[4][:, 0:STEPS], ALU.mult, ALU.add)
                v.tensor_copy(lo16, bank[5][:, 0:STEPS])
                st.done(v.tensor_scalar(wsc, bank[6][:, 0:STEPS], SW, None, ALU.mult))
                st.done(v.tensor_copy(whi, wsc))
                v.tensor_tensor(wlo, wsc, whi, ALU.subtract)
                v.tensor_scalar(win_at, win_f, float(P), None, ALU.mult).then_inc(table_done, 1)
                v.wait_ge(table_done, 1)

            def stats(i, h, t):
                v.wait_ge(x_in[h], 32 * (t + 1))
                v.bn_stats(ln_st[0:TT, h, 0:6], xs[h][0:TT, 0:512])
                st.done(v.bn_stats(ln_st[0:TT, h, 6:12], xs[h][0:TT, 512:1024]))
                apart(v)
                v.bn_aggr(ln_mv[0:TT, h, :], ln_st[0:TT, h, :]).then_inc(stat_ready, 1)

            def norm(i, h):
                v.wait_ge(sd_ready, i + 1)
                st.done(v.reciprocal(ln_rs[0:TT, h, :], ln_sd[0:TT, h, :]))
                v.tensor_scalar(xn[h][0:TT], xs[h][0:TT], ln_mv[0:TT, h, 0:1], ln_rs[0:TT, h, :], ALU.subtract, ALU.mult).then_inc(xn_ready, 1)

            def xt_lo(i, h):
                for b in range(2):
                    v.wait_ge(xt_hi, 2 * i + b + 1)
                    ins = v.tensor_tensor(xt[:, 1, 4 * b:4 * b + 4, tok(i)], bank[2 * h + b][:, 0:4 * TT].rearrange("p (k n) -> p k n", n=TT),
                                          xt[:, 0, 4 * b:4 * b + 4, tok(i)], ALU.subtract)
                ins.then_inc(xt_done, 1)
            def wkv_lo(m, h):
                v.wait_ge(part_hi, m + 1)
                v.scalar_tensor_tensor(wkv[:, 1, bass.ds(m, 1), :].rearrange("p o c -> p (o c)"), stage[h], SW,
                                       wkv[:, 0, bass.ds(m, 1), :].rearrange("p o c -> p (o c)"), ALU.mult, ALU.subtract).then_inc(part_lo, 1)
            for h in range(2):
                stats(h, h, 0)
                norm(h, h)
            with v.Fori(1, NT // 2) as t:
                st.enter(t - 1, 4)
                for h in range(2):
                    i = 2 * t + h
                    stats(i, h, t)
                    xt_lo(i - 2, h)
                    norm(i, h)
                    wkv_lo(i - 2, h)
            st.leave(NT // 2 - 1)
            read_table()
            xt_lo(NT - 2, 0)
            xt_lo(NT - 1, 1)
            v.wait_ge(qn_in, 16)
            v.tensor_scalar(qnw, qnw, 1.0 / SW, None, ALU.mult).then_inc(qn_ready, 1)

            def make(n, s, k):
                cols = lambda a: a[:, bass.ds(n * G, G)].unsqueeze(1).to_broadcast([P, P, G])
                if k == 0:
                    v.tensor_tensor(one_hot[s][:, 0], col_iota, cols(lo16), ALU.is_equal)
                elif k == 1:
                    v.wait_ge(hot_ready, n)
                    v.tensor_tensor(key_hot, col_iota, cols(key16), ALU.is_equal).then_inc(hot_key, 1)
                elif k == 2:
                    v.wait_ge(hot_key, n + 1)
                    v.tensor_tensor(one_hot[s][:, 1], key_hot, cols(whi), ALU.mult)
                else:
                    v.tensor_tensor(one_hot[s][:, 2], key_hot, cols(wlo), ALU.mult).then_inc(hot_ready, 1)

            def accumulate(n, s):
                _, at = nc.values_load_multi_w_load_instructions(
                    win_at[0:1, bass.ds(n * G, G)], engines=(ENG.DVE,), min_val=0, max_val=(WINDOWS - 1) * P,
                    skip_runtime_bounds_check_because="the table clips windows to WINDOWS - 1")
                for j in range(G):
                    v.wait_ge(step_mm, 2 * n + j // 4 + 1)
                    v.wait_ge(acc_done, START + G * n + j)
                    v.tensor_tensor(w_acc[:, bass.ds(at[j], P)], bank[6 + j // 4][:, (j % 4) * P:(j % 4 + 1) * P],
                                    w_acc[:, bass.ds(at[j], P)], ALU.add).then_inc(acc_done, 1)
                    if j >= 4:
                        make(n + 2, s, j - 4)
            for n in range(2):
                for k in range(4):
                    make(n, n, k)

            def k_half(i, c):
                v.wait_ge(k_sq, 2 * i + c + 1)
                v.scalar_tensor_tensor(kw[0:TT], bank[c][0:TT, :], 1.0 / SW, knw[0:TT, c * 512:(c + 1) * 512], ALU.mult, ALU.mult).then_inc(kw_ready, 1)
                v.wait_ge(k_hi, 2 * i + c + 1)
                st.done(v.scalar_tensor_tensor(kt_[1][0:TT, c * 512:(c + 1) * 512], kw[0:TT], 0.0, kt_[0][0:TT, c * 512:(c + 1) * 512], ALU.max, ALU.subtract))

            def v_half(i, c):
                v.wait_ge(v_hi, 2 * i + c + 1)
                v.scalar_tensor_tensor(vt_[1][0:TT, 4 * c:4 * c + 4, 0:P], bank[2 - c][0:TT, :].rearrange("p (a b) -> p a b", b=P),
                                       tiny[0:TT, 4:5], vt_[0][0:TT, 4 * c:4 * c + 4, 0:P], ALU.mult, ALU.subtract).then_inc(v_lo, 1)

            def kv_tile(i, s):
                v.wait_ge(kv_used, START + i)
                k_half(i, 0)
                accumulate(3 * i, s % 2)
                k_half(i, 1)
                v.tensor_tensor(tiny[0:TT, 2:3], tiny[0:TT, 0:1], tiny[0:TT, 1:2], ALU.add).then_inc(k_ss, 1)
                v.wait_ge(k_sd, i + 1)
                st.done(v.reciprocal(tiny[0:TT, 4:5], tiny[0:TT, 3:4]))
                st.done(v.tensor_scalar(tiny[0:TT, 5:6], tiny[0:TT, 4:5], SX * SW, None, ALU.mult))
                st.done(v.tensor_scalar(vt_[0][0:TT, :, P], ones[0:TT, 0:PAIRS], tiny[0:TT, 5:6], None, ALU.mult))
                v.scalar_tensor_tensor(vt_[1][0:TT, :, P], ones[0:TT, 0:PAIRS], tiny[0:TT, 5:6], vt_[0][0:TT, :, P], ALU.mult, ALU.subtract).then_inc(k_rs, 1)
                v_half(i, 0)
                accumulate(3 * i + 1, (s + 1) % 2)
                v_half(i, 1)
                accumulate(3 * i + 2, (s + 2) % 2)
            v.wait_ge(acc_zero, 1)
            v.wait_ge(knw_in, 16)
            with v.Fori(0, NT // 2) as t:
                st.enter(t, 10)
                for h in range(2):
                    kv_tile(2 * t + h, 3 * h)
            st.leave(NT // 2)
            v.wait_ge(kvf_hi, 1)
            for p in range(PAIRS):
                for r0 in (0, 64):
                    c0 = (p % 3) * 130 + r0
                    v.scalar_tensor_tensor(kvb[1][r0:r0 + 64, p, r0:r0 + 64], bank[3 + p // 3][r0:r0 + 64, c0:c0 + 64], 2.0 ** -12,
                                           kvb[0][r0:r0 + 64, p, r0:r0 + 64], ALU.mult, ALU.subtract)
            for b in range(3):
                n = min(3, PAIRS - 3 * b)
                ins = v.tensor_scalar(ksf[:, 3 * b:3 * b + n], bank[3 + b][:, 0:390].rearrange("p (a b) -> p a b", b=130)[:, 0:n, P], 2.0 ** -12, None, ALU.mult)
            st.done(ins)
            for p in range(PAIRS):
                ins = v.tensor_scalar(ksb[0][:, p, :], head_mask, ksf[:, p:p + 1], None, ALU.mult)
            st.done(ins)
            for p in range(PAIRS):
                ins = v.scalar_tensor_tensor(ksb[1][:, p, :], head_mask, ksf[:, p:p + 1], ksb[0][:, p, :], ALU.mult, ALU.subtract)
            ins.then_inc(kvb_ready, 1)
            with v.Fori(0, KT // 2) as t:
                for u in range(6):
                    accumulate(KV_GROUPS + 6 * t + u, u % 2)
            for k in range(8):
                v.wait_ge(acc_hi, k + 1)
                v.tensor_tensor(acc_part[:, 1, k, :], w_acc[:, k * D:(k + 1) * D], acc_part[:, 0, k, :], ALU.subtract).then_inc(acc_lo, 1)

            def attend_unit(j, g, unit):
                o, a = bank[2 + j % 2], att[j % 2]
                v.wait_ge(at_mm, unit + 1)
                v.wait_ge(at_done, START + (max(unit - 1, 0) if isinstance(unit, int) else unit - 1))
                st.done(v.tensor_tensor(a, o[:, 256:256 + AW], eps_row[:, bass.ds(g * AW, AW)], ALU.add))
                st.done(v.reciprocal(a, a))
                v.scalar_tensor_tensor(a, o[:, 0:AW], SX, a, ALU.mult, ALU.mult).then_inc(at_f, 1)
            v.wait_ge(eps_ready, 3)
            for j in range(PAIRS):
                attend_unit(j, 0, j)

            v.wait_ge(mixc_in, 80)
            st.done(v.tensor_scalar(gate_hl[:, 0, :], gate_f, SW, None, ALU.mult))
            v.scalar_tensor_tensor(gate_hl[:, 1, :], gate_f, SW, gate_hl[:, 0, :], ALU.mult, ALU.subtract).then_inc(gate_w_ready, 1)

            def add_half(i, h, half):
                c = slice(half * 512, half * 512 + 512)
                v.wait_ge(xb_ready, i + 1)
                v.wait_ge(mix_mm, 2 * i + half + 1)
                v.scalar_tensor_tensor(xm[h][0:TT, c], bank[half][0:TT, :], 1.0 / (SX * SW), xm[h][0:TT, c], ALU.mult, ALU.add).then_inc(x1_half, 1)

            def mix_norm(i, t, h):
                v.wait_ge(x1_half, 2 * i + 2)
                v.bn_stats(ln_st[0:TT, h, 0:6], xm[h][0:TT, 0:512])
                st.done(v.bn_stats(ln_st[0:TT, h, 6:12], xm[h][0:TT, 512:1024]))
                apart(v)
                v.bn_aggr(ln_mv[0:TT, h, :], ln_st[0:TT, h, :]).then_inc(stat2_ready, 1)
                v.wait_ge(sd2_ready, 2 * i + 1)
                st.done(v.reciprocal(ln_rs[0:TT, h, :], ln_sd[0:TT, h, :]))
                v.tensor_scalar(tiny[0:TT, 0:1], ln_mv[0:TT, h, 1:2], ln_rs[0:TT, h, :], ln_rs[0:TT, h, :], ALU.mult, ALU.mult).then_inc(stat2_ready, 1)
                v.wait_ge(base_ready, i)
                v.tensor_scalar(xn2[0:TT], xm[h][0:TT], ln_mv[0:TT, h, 0:1], ln_rs[0:TT, h, :], ALU.subtract, ALU.mult).then_inc(xn2_ready, 1)
                v.wait_ge(sd2_ready, 2 * i + 2)
                st.done(v.reciprocal(tiny[0:TT, 2:3], tiny[0:TT, 1:2]))
                v.wait_ge(t_out[h], 32 * t)
                v.wait_ge(xn2_ready, i + 1)
                v.scalar_tensor_tensor(tm[h][0:TT], xn2[0:TT], tiny[0:TT, 2:3], scale_b[0:TT], ALU.mult, ALU.mult).then_inc(t_ready, 1)

            def tt_lo(i):
                for b in range(2):
                    v.wait_ge(tt_hi, 2 * i + b + 1)
                    ins = v.tensor_tensor(tt[:, 1, 4 * b:4 * b + 4, :], bank[4 + b][:, 0:4 * TT].rearrange("p (k n) -> p k n", n=TT),
                                          tt[:, 0, 4 * b:4 * b + 4, :], ALU.subtract)
                ins.then_inc(tt_done, 1)

            def gate(i):
                v.wait_ge(gate_mm, START + i + 1)
                v.scalar_tensor_tensor(logits[0:TT, bass.ds(i, 1), :].rearrange("p a b -> p (a b)"), bank[6][0:TT, 0:E], 1.0 / (ST * SW), gate_bias[0:TT],
                                       ALU.mult, ALU.add).then_inc(gate_done, 1)
            def mix_period(i, t, h, attend=True):
                for half in range(2):
                    for j in (4 * h + 2 * half, 4 * h + 2 * half + 1):
                        if j % 2 == 1:
                            add_half(i, h, half)
                        if attend:
                            attend_unit(j, t + 1, PAIRS * (t + 1) + j)
                if not isinstance(i, int) or i >= 2:
                    gate(i - 2)
                if not isinstance(i, int) or i >= 1:
                    tt_lo(i - 1)
                mix_norm(i, t, h)
            mix_period(0, 0, 0)
            mix_period(1, 0, 1)
            with v.Fori(1, NT // 2 - 1) as t:
                st.enter(t - 1, 22)
                for h in range(2):
                    mix_period(2 * t + h, t, h)
            st.leave(NT // 2 - 2)
            for h in range(2):
                mix_period(NT - 2 + h, NT // 2 - 1, h, attend=False)
            gate(NT - 2)
            tt_lo(NT - 1)
            gate(NT - 1)

            v.wait_ge(gate_done, START + NT)
            v.wait_ge(route_iota, 4)
            for i in range(NT):
                ins = v.max(top_v[0:TT, i, :], logits[0:TT, i, :])
            st.done(ins)
            for i in range(NT):
                ins = v.max_index(top_i[0:TT, i, :], top_v[0:TT, i, :], logits[0:TT, i, :])
            st.done(ins)
            v.tensor_tensor(pe_[0:TT], top_v[0:TT, :, 1], top_v[0:TT, :, 0], ALU.subtract).then_inc(route_exp, 1)
            st.done(v.tensor_copy(flat(idx_f[0:TT]), flat(top_i[0:TT])))
            for c in range(2):
                ins = v.tensor_tensor(oh[c][0:TT], e_iota[0:TT], idx_f[0:TT, :, c:c + 1].to_broadcast([TT, NT, E]), ALU.is_equal)
            st.done(ins)
            v.tensor_tensor(flat(both[0:TT]), flat(oh[0][0:TT]), flat(oh[1][0:TT]), ALU.add).then_inc(route_mm, 1)
            v.wait_ge(route_mm, 2)
            v.memset(pre[:, 0, :], 0.0)
            st.done(v.tensor_copy(flat(tot), bank[1][:, 0:NT * E]))
            for i in range(1, NT):
                st.done(v.tensor_tensor(pre[:, i, :], pre[:, i - 1, :], tot[:, i - 1, :], ALU.add))
            st.done(v.tensor_tensor(cnt, pre[:, NT - 1, :], tot[:, NT - 1, :], ALU.add))
            st.done(v.tensor_scalar(cnt_i, cnt, float(P - 1), None, ALU.add))
            st.done(v.tensor_scalar(cnt_i, cnt_i, 7, None, ALU.logical_shift_right))
            v.memset(cum[:, 0:1], 0.0)
            st.done(v.tensor_scalar(nblk, cnt_i, 1.0, None, ALU.max))
            for e in range(E):
                st.done(v.tensor_tensor(cum[:, e + 1:e + 2], cum[:, e:e + 1], nblk[:, e:e + 1], ALU.add))
            v.tensor_copy(base_i, cum)
            v.memset(expf, 0.0)
            st.done(v.memset(offf, float(slot_off[0] // 2)))
            for e in range(E - 1):
                move = (slot_off[(e + 1) % 3] - slot_off[e % 3]) // 2
                st.done(v.tensor_scalar(ge, b_iota, cum[:, e + 1:e + 2], None, ALU.is_ge))
                v.tensor_tensor(expf, expf, ge, ALU.add)
                st.done(v.scalar_tensor_tensor(offf, ge, float(move), offf, ALU.mult, ALU.add))
            v.tensor_copy(exp_i, expf)
            v.tensor_copy(blk_i, offf).then_inc(count_in, 1)
            st.done(v.tensor_tensor(flat(rank[0:TT]), bank[0][0:TT, 0:NT * E], flat(pre[0:TT]), ALU.add))
            st.done(v.scalar_tensor_tensor(rank[0:TT], cum[0:TT, 0:E].unsqueeze(1).to_broadcast([TT, NT, E]), float(P), rank[0:TT], ALU.mult, ALU.add))
            for c in range(2):
                st.done(v.tensor_tensor(flat(oh[c][0:TT]), flat(oh[c][0:TT]), flat(rank[0:TT]), ALU.mult))
                st.done(v.tensor_reduce(slot_f[0:TT, c, :], oh[c][0:TT], AX.X, ALU.add))
                ins = v.tensor_copy(slot_i[c][0:TT], slot_f[0:TT, c, :])
            ins.then_inc(slots_ready, 1)
            v.wait_ge(pexp_in, 1)
            st.done(v.tensor_scalar(pden[0:TT], pe_[0:TT], 1.0, None, ALU.add))
            st.done(v.reciprocal(prob[0:TT, 0, :], pden[0:TT]))
            st.done(v.tensor_tensor(prob[0:TT, 1, :], pe_[0:TT], prob[0:TT, 0, :], ALU.mult))

            def row_lo(b, s):
                for q in range(2):
                    v.wait_ge(rt_hi, 2 * b + q + 1)
                    ins = v.tensor_tensor(rowT[s][:, 1, 4 * q:4 * q + 4, :], bank[2 + 2 * s + q][:, :].rearrange("p (k n) -> p k n", n=P),
                                          rowT[s][:, 0, 4 * q:4 * q + 4, :], ALU.subtract)
                ins.then_inc(rt_done, 1)

            def swiglu(b):
                e = v.value_load(exp_i[0:1, bass.ds(b, 1)], min_val=0, max_val=E - 1)
                v.wait_ge(h_mm, b + 1)
                v.scalar_tensor_tensor(hb, bank[6][:, :], 1.0 / (ST * SW), b1_b[:, bass.ds(e * (2 * HID), 2 * HID)], ALU.mult, ALU.add).then_inc(h_evac, 1)
                v.wait_ge(h_evac, b + 1)
                pairs = hb.rearrange("p (j c) -> p j c", c=2)
                v.tensor_scalar(glu, pairs[:, :, 0], 7.0, None, ALU.min).then_inc(glu_ready, 1)
                st.done(v.tensor_scalar(lin, pairs[:, :, 1], -7.0, 7.0, ALU.max, ALU.min))
                st.done(v.scalar_tensor_tensor(lin, lin, 1.0, glu, ALU.add, ALU.mult))
                v.wait_ge(sg_ready, b + 1)
                v.wait_ge(at_psum, b)
                v.scalar_tensor_tensor(act, lin, SX, sg, ALU.mult, ALU.mult).then_inc(act_ready, 1)

            def act_lo(b):
                v.wait_ge(a_hi, b + 1)
                v.tensor_tensor(actT[:, 1, :, :], bank[7][:, 0:2 * P].rearrange("p (k n) -> p k n", n=P), actT[:, 0, :, :], ALU.subtract).then_inc(a_done, 1)

            def evac_y(b, s, q):
                e = v.value_load(exp_i[0:1, bass.ds(b, 1)], min_val=0, max_val=E - 1)
                v.wait_ge(y_mm, b + 1)
                v.wait_ge(y_out[s], START + 16 * q)
                for half in range(2):
                    ins = v.scalar_tensor_tensor(ysb[s][:, half * 512:half * 512 + 512], bank[half][:, :], 1.0 / (SX * SW),
                                                 b2_b[:, bass.ds(e * D + half * 512, 512)], ALU.mult, ALU.add)
                ins.then_inc(y_ready, 1)
            v.wait_ge(bias_in, 32)
            row_lo(0, 0)
            row_lo(1, 1)
            swiglu(0)
            with v.Fori(0, (BLOCKS - 3) // 2) as t:
                st.enter(t, 4)
                for h in range(2):
                    b = 2 * t + h + 1
                    row_lo(b + 1, h)
                    act_lo(b - 1)
                    swiglu(b)
                    evac_y(b - 1, h, t)
            st.leave((BLOCKS - 3) // 2)
            for b in range(BLOCKS - 2, BLOCKS):
                if b + 1 < BLOCKS:
                    row_lo(b + 1, (b + 1) % 2)
                act_lo(b - 1)
                swiglu(b)
                evac_y(b - 1, (b - 1) % 2, (b - 1) // 2)
            act_lo(BLOCKS - 1)
            evac_y(BLOCKS - 1, (BLOCKS - 1) % 2, (BLOCKS - 1) // 2)
            for i in range(NT):
                v.wait_ge(c_in[i % 2], 32 * (i // 2 + 1))
                v.wait_ge(c_base_in[i % 2], 32 * (i // 2 + 1))
                o = cb[i % 2][0:TT]
                st.done(v.scalar_tensor_tensor(o, cy[i % 2][0][0:TT], prob[0:TT, 0, i:i + 1], o, ALU.mult, ALU.add))
                v.scalar_tensor_tensor(o, cy[i % 2][1][0:TT], prob[0:TT, 1, i:i + 1], o, ALU.mult, ALU.add).then_inc(c_done, 1)


_OUT = (N, D)


def kernel(**inputs):
    import numpy as np
    import concourse.bacc as bacc
    from concourse.bass_utils import run_bass_kernel_spmd

    a = {k: np.ascontiguousarray(v) for k, v in inputs.items()}
    w_qkv = a["L0_mix_W_qkv"]
    wq = w_qkv[:, 0:D].reshape(KT, P, KT, P).transpose(2, 1, 0, 3)
    wq = wq.reshape(KT // 2, 2, P, D).transpose(0, 2, 1, 3).reshape(N_PIECE_Q, P, PIECE)
    wo = a["L0_mix_W_out"].reshape(N_PIECE_O, 2, P, D).transpose(0, 2, 1, 3).reshape(N_PIECE_O, P, PIECE)
    w1 = a["L0_ffn_mlp1_w"].reshape(E, 2, 4, P, 2 * HID).transpose(0, 1, 3, 2, 4).reshape(N_PIECE_1, P, PIECE)
    w2 = a["L0_ffn_mlp2_w"].reshape(E, 2, P, D).transpose(0, 2, 1, 3).reshape(N_PIECE_2, P, PIECE)
    arrays = {
        "x": a["x"], "src": a["src"], "dst": a["dst"], "edge_weight": a["edge_weight"],
        "gnn_bias": a["L0_gnn_bias"], "w_qkv": w_qkv,
        "qn_w": np.ascontiguousarray(a["L0_mix_qn_w"].reshape(KT, P).T), "kn_w": a["L0_mix_kn_w"],
        "w_flat": np.ascontiguousarray(np.concatenate([wq, wo, w1, w2])), "b_out": a["L0_mix_b_out"],
        "norm_scale": a["L0_ffn_norm_scale"],
        "gate_w": np.ascontiguousarray(a["L0_ffn_gate_w"].reshape(KT, P, E).transpose(1, 0, 2).reshape(P, KT * E)),
        "gate_b": a["L0_ffn_gate_b"], "mlp1_b": a["L0_ffn_mlp1_b"].reshape(-1), "mlp2_b": a["L0_ffn_mlp2_b"].reshape(-1),
    }
    nc = bacc.Bacc("TRN2", target_bir_lowering=False, num_devices=1)
    args = {k: nc.dram_tensor(f"in_{k}", v.shape, mybir.dt.from_np(v.dtype), kind="ExternalInput").ap() for k, v in arrays.items()}
    out = nc.dram_tensor("out_x", _OUT, F32, kind="ExternalOutput").ap()
    build_gps_layer(nc, **args, out=out)
    r = run_bass_kernel_spmd(nc, [{f"in_{k}": v for k, v in arrays.items()}], core_ids=[0])
    return r.results[0]["out_x"]
```

```python
from contextlib import ExitStack

import concourse.bass as bass
from concourse import mybir

F32 = mybir.dt.float32
F16 = mybir.dt.float16
I32 = mybir.dt.int32
U32 = mybir.dt.uint32
ALU = mybir.AluOpType
ACT = mybir.ActivationFunctionType
AX = mybir.AxisListType
ENG = mybir.EngineType

P = 128
N, D = 1250, 1024
TT = 125
NT = N // TT
KT = D // P
HEADS = 16
PAIRS = HEADS // 2
AT_UNITS = PAIRS * NT // 2
E, HID = 8, 256
BIAS = 2 * HID + D
NE = 41250
CHUNKS = -(-NE // P)
LAST_ROWS = CHUNKS - 2 * P
WIN = 16
WINDOWS = D // WIN
G = 8
KV_GROUPS = 3 * NT
GROUPS = -(-(CHUNKS + WINDOWS - 1) // G)
STEPS = (GROUPS + 2) * G
assert GROUPS == KV_GROUPS + 3 * (KT - 2) + 1
GRP = [(0, 418), (418, 416), (834, 416)]
GW = 418
AW = 2 * TT
PIECE = 2048
N_PIECE_Q, N_PIECE_O, N_PIECE_1, N_PIECE_2 = 4, 4, 16, 8
PIECES = 32
BLOCKS = (2 * N + E * (P - 1)) // P
SLOTS = BLOCKS * P

SX = 32.0
SW = 256.0
ST = 16.0
EPS_LN, EPS_Q, EPS_T = 1e-5, 1e-6, 1e-5

XNT_AT = 0
A_AT = 40000
B_AT = A_AT + 65536
C_AT = B_AT + 32768
S_AT = C_AT + 32768
TOP = 212800


def build_gps_layer(nc, x, src, dst, edge_weight, gnn_bias, w_qkv, qn_w, kn_w, w_flat, b_out,
                    norm_scale, gate_w, gate_b, mlp1_b, mlp2_b, out):
    scratch = lambda name, shape, dt: nc.dram_tensor(name, shape, dt, kind="Internal").ap()
    split_dram = scratch("split_dram", [2, PIECES, P, PIECE], F16)
    wg_dram = scratch("wg_dram", [2, D * D], F16)
    t_dram = scratch("t_dram", [N, D], F32)
    base_dram = scratch("base_dram", [N, D], F32)
    y_dram = scratch("y_dram", [SLOTS, D], F32)

    with ExitStack() as ctx:
        arena = ctx.enter_context(nc.sbuf_tensor("arena", [P, TOP // 4], F32))
        bank = [ctx.enter_context(nc.psum_tensor(f"bank{b}", [P, 512], F32)) for b in range(8)]
        sem = lambda name: ctx.enter_context(nc.semaphore(name))

        def view(at, shape, dt=F32):
            size = 2 if dt == F16 else 4
            n = 1
            for s in shape:
                n *= s
            assert at % 4 == 0 and at + n * size <= TOP, (at, shape)
            v = arena[:, at // 4:at // 4 + -(-n * size // 4)]
            if dt != F32:
                v = v.bitcast(dt)
            v = v[:, 0:n]
            if len(shape) == 2:
                v = v.rearrange("p (a b) -> p a b", a=shape[0])
            if len(shape) == 3:
                v = v.rearrange("p (a b c) -> p a b c", a=shape[0], b=shape[1])
            return v

        class Place:
            def __init__(self, at, end):
                self.at, self.end = at, end

            def __call__(self, shape, dt=F32):
                n = 2 if dt == F16 else 4
                for s in shape:
                    n *= s
                v = view(self.at, shape, dt)
                self.at += -(-n // 32) * 32
                assert self.at <= self.end, (self.at, self.end)
                return v

        S = Place(S_AT, TOP)
        ident = S([P])
        ones = S([P])
        upper = S([P])
        zeros = S([P], F16)
        col_iota = S([P, G], F16)
        eps_x = S([1]); eps_k = S([1]); eps_den = S([1]); eps_b = S([1]); eps_t = S([1])
        qnw = S([KT])
        logits = S([NT, E]); top_v = S([NT, E]); top_i = S([NT, E], U32)
        gate_hl = S([2, KT * E], F16)
        gate_bias = S([E])
        ln_st = S([2, 12]); ln_mv = S([2, 2]); ln_sd = S([2, 1]); ln_rs = S([2, 1]); tiny = S([8])
        table_at = S.at
        key16 = S([STEPS], F16); lo16 = S([STEPS], F16); whi = S([STEPS], F16); wlo = S([STEPS], F16)
        win_at = S([STEPS], I32)
        one_hot = [S([3, P, G], F16) for _ in range(2)]
        key_hot = S([P, G], F16)
        stage = [S([PIECE]) for _ in range(2)]

        xt = view(XNT_AT, [2, KT, N], F16)
        wkv = view(A_AT, [2, KT, 2048], F16)
        ut = view(A_AT, [2, KT, N], F16)
        tail = Place(A_AT + 40000, A_AT + 65536)
        kvb = [tail([PAIRS, P], F16) for _ in range(2)]
        ksb = [tail([PAIRS, P], F16) for _ in range(2)]
        after_q = tail.at
        wq = [tail([2, KT, P], F16) for _ in range(2)]
        tail.at = after_q
        eps_row = tail([N])
        att = [tail([AW]) for _ in range(2)]
        w_acc = view(C_AT, [WINDOWS * P])

        C = Place(C_AT, S_AT)
        src_i = C([3, P], I32); dst_i = C([3, P], I32)
        ew = C([3, P])
        key_c = C([3, P]); lo_c = C([3, P]); hi_i = C([3, P], I32)
        hi_f = C([3, P]); big = C([3, P])
        w_first = C([3]); w_last = C([3]); ends_i = C([3, 2], I32); n_win = C([3]); first = C([3])
        past = C([3]); shift = C([3])
        pick = C([3, STEPS])
        step_iota = C([STEPS])
        win_pick = C([3, STEPS])
        win_f = C([STEPS])
        wsc = C([STEPS])

        B = Place(B_AT, C_AT)
        part = [B([2, PIECE], F16) for _ in range(2)]
        wide = stage + [p.rearrange("p a b -> p (a b)").bitcast(F32) for p in part]
        b_work = B.at
        xs = [B([D]) for _ in range(4)]
        B.at = b_work
        knw = B([D])
        kw = B([512])
        kt_ = [B([D], F16) for _ in range(2)]
        vt_ = [B([PAIRS, 130], F16) for _ in range(2)]
        junk = B([512], F16)
        B.at = b_work
        u32 = [B([GW]) for _ in range(2)]
        usq = [B([GW]) for _ in range(2)]
        qss = B([3, GW])
        ksf = B([PAIRS])
        head_mask = B([P])
        wo = view(B_AT, [2, KT, D], F16)

        acc_part = view(table_at, [2, WINDOWS // 8, 8 * P], F16)

        T = Place(table_at, TOP)
        xm = [T([D]) for _ in range(2)]
        xn2 = T([D])
        tm = [T([D]) for _ in range(2)]
        tt = T([2, KT, TT], F16)
        bias_b = T([D]); scale_b = T([D])
        gate_f = T([KT * E])
        zero_row = T([D // 2])
        wg = view(C_AT, [2, KT, D], F16)

        slot_off = [A_AT + 40000, XNT_AT, B_AT]
        eslot = [(view(o, [2, KT * 512], F16), view(o + 16384, [2, 2 * D], F16)) for o in slot_off]
        arena16 = arena[:, :].bitcast(F16)
        C = Place(C_AT, S_AT)
        bias = C([3 * BIAS])
        T = C
        hb = T([2 * HID]); glu = T([HID]); lin = T([HID]); sg = T([HID]); act = T([HID])
        actT = T([2, 2, P], F16)
        blk_i = T([BLOCKS], I32); bias_i = T([BLOCKS], I32); exp_i = T([BLOCKS], I32); base_i = T([E + 1], I32)
        cb = [view(A_AT + i * 4 * D, [D]) for i in range(NT - 1)] + [C([D])]
        T2 = Place(table_at, TOP)
        rows = [T2([D]) for _ in range(2)]
        row_idx = [T2([1], I32) for _ in range(2)]
        rowT = [T2([2, KT, P], F16) for _ in range(2)]
        ysb = [T2([D]) for _ in range(2)]
        R = Place(24576, A_AT)
        oh = [R([NT, E]) for _ in range(2)]
        both = R([NT, E]); rank = R([NT, E]); tot = R([NT, E]); pre = R([NT, E])
        cnt = R([E]); cnt_i = R([E], I32); nblk = R([E]); cum = R([E + 1])
        ge = R([BLOCKS, E - 1]); moved = R([BLOCKS, E - 1]); moves = R([2, E - 1])
        e_iota = R([NT, E]); b_iota = R([BLOCKS]); expf = R([BLOCKS]); expf2 = R([BLOCKS]); offf = R([2, BLOCKS])
        slot_f = R([2 * NT]); slot_i = R([2 * NT], I32); tok_of = R([BLOCKS], I32)
        slot_p = R([2, 2 * NT], I32); slot_pf = R([2, 2 * NT])
        slot_first = R([NT], I32); slot_second = R([NT], I32); p_first = R([NT]); p_second = R([NT])
        is_first = R([2, NT]); swap = R([2, NT]); stores_i = R([2], I32)
        place_iota = R([P]); token_f = R([NT])
        place_hot = R([2 * NT, P], F16); block_token = R([2 * NT, BLOCKS], F16); block_hot = R([2 * NT, BLOCKS])
        prob = R([2, NT]); pe_ = R([NT]); pden = R([NT]); idx_f = R([NT, E])
        T3 = Place(table_at, TOP)
        cy = [T3([D]) for _ in range(8)]
        first_at = [B_AT + i * 4 * D for i in range(8)] + [A_AT + 40000 + i * 4 * D for i in range(2)]
        first_rows = [view(at, [D]) for at in first_at]

        passed = sem("passed"); edges_in = sem("edges_in"); table_in = sem("table_in"); consts = sem("consts")
        x_in = [sem(f"x_in{b}") for b in range(4)]
        xn_ready = sem("xn_ready"); stat_ready = sem("stat_ready"); sd_ready = sem("sd_ready")
        xt_psum = sem("xt_psum"); xt_hi = sem("xt_hi"); xt_done = sem("xt_done")
        stage_in = [sem(f"stage_in{b}") for b in range(4)]
        part_hi = sem("part_hi"); part_lo = [sem(f"part_lo{h}") for h in range(2)]; wkv_scaled = sem("wkv_scaled"); piece_scaled = sem("piece_scaled"); piece_done = sem("piece_done"); last_done = sem("last_done")
        part_out = [sem(f"part_out{h}") for h in range(2)]
        table_mm = sem("table_mm"); table_step = sem("table_step"); table_done = sem("table_done")
        knw_in = sem("knw_in"); qn_in = sem("qn_in"); qn_ready = sem("qn_ready"); acc_zero = sem("acc_zero")
        gate_w_ready = sem("gate_w_ready"); t_whole = sem("t_whole"); 
        kv_mm = sem("kv_mm"); k_sq = sem("k_sq"); kw_ready = sem("kw_ready"); k_hi = sem("k_hi")
        k_ss = sem("k_ss"); k_sd = sem("k_sd"); k_rs = sem("k_rs"); v_hi = sem("v_hi")
        v_lo = sem("v_lo"); kv_used = sem("kv_used")
        hot_ready = sem("hot_ready"); hot_key = sem("hot_key"); step_mm = sem("step_mm"); acc_done = sem("acc_done")
        dve_step = sem("dve_step"); act_step = sem("act_step"); pool_step = sem("pool_step")
        kvb_zero = sem("kvb_zero"); kvb_ready = sem("kvb_ready"); kvf_hi = sem("kvf_hi")
        wq_in = [sem(f"wq_in{h}") for h in range(2)]
        q_mm = sem("q_mm"); q_evac = sem("q_evac"); q_split = sem("q_split")
        eps_mm = sem("eps_mm"); eps_ready = sem("eps_ready")
        at_mm = sem("at_mm"); at_f = sem("at_f"); at_hi = sem("at_hi"); at_done = sem("at_done")
        acc_hi = sem("acc_hi"); acc_lo = sem("acc_lo")
        acc_out = sem("acc_out")
        wg_in = [sem(f"wg_in{h}") for h in range(2)]; wo_in = [sem(f"wo_in{h}") for h in range(2)]; mixc_in = sem("mixc_in"); mixc_ready = sem("mixc_ready")
        xm_in = [sem(f"xm_in{h}") for h in range(2)]
        xb_ready = sem("xb_ready"); mix_mm = sem("mix_mm"); x1_half = sem("x1_half")
        xn2_ready = sem("xn2_ready"); base_ready = sem("base_ready")
        base_out = [sem(f"base_out{h}") for h in range(2)]
        sd2_ready = sem("sd2_ready"); stat2_ready = sem("stat2_ready")
        t_ready = sem("t_ready")
        t_out = [sem(f"t_out{h}") for h in range(2)]
        tt_psum = sem("tt_psum"); tt_hi = sem("tt_hi"); tt_done = sem("tt_done")
        gate_mm = sem("gate_mm"); gate_done = sem("gate_done")
        route_iota = sem("route_iota"); route_mm = sem("route_mm")
        count_in = sem("count_in"); route_exp = sem("route_exp"); pexp_in = sem("pexp_in")
        slots_ready = sem("slots_ready"); token_mm = sem("token_mm"); tokens_ready = sem("tokens_ready")
        w_slot_in = sem("w_slot_in"); expert_ready = sem("expert_ready")
        row_in = [sem(f"row_in{h}") for h in range(2)]; idx_ready = sem("idx_ready")
        rt_psum = sem("rt_psum"); rt_hi = sem("rt_hi"); rt_done = sem("rt_done")
        h_mm = sem("h_mm"); h_evac = sem("h_evac"); glu_ready = sem("glu_ready"); sg_ready = sem("sg_ready")
        act_ready = sem("act_ready"); at_psum = sem("at_psum"); a_hi = sem("a_hi"); a_done = sem("a_done")
        y_mm = sem("y_mm"); y_ready = sem("y_ready")
        y_out = [sem(f"y_out{h}") for h in range(2)]
        c_in = [sem(f"c_in{h}") for h in range(8)]
        c_base_in = sem("c_base_in"); first_in = sem("first_in"); zero_ready = sem("zero_ready"); y_zero = sem("y_zero")
        c_done = sem("c_done"); stored = [sem(f"stored{h}") for h in range(2)]

        START = 1

        class Steps:
            def __init__(self, eng, s):
                self.eng, self.s, self.base, self.n = eng, s, 0, 0

            def done(self, ins):
                self.n += 1
                ins.then_inc(self.s, 1)
                self.eng.wait_ge(self.s, self.base + self.n)

            def enter(self, i, per):
                self.start = self.base + self.n if not hasattr(self, "start") else self.start
                self.base, self.n, self.per = self.start + i * per, 0, per

            def leave(self, iters):
                assert self.n == self.per, (self.n, self.per)
                self.base, self.n = self.start + iters * self.per, 0
                del self.start

        def apart(eng):
            eng.sem_inc(passed, 1)

        def tok(i, n=TT):
            return bass.ds(i * TT, n)

        x_rows = x.rearrange("(i p) d -> i p d", p=TT)
        out_rows = out.rearrange("(i p) d -> i p d", p=TT)
        t_rows = t_dram.rearrange("(i p) d -> i p d", p=TT)
        base_rows = base_dram.rearrange("(i p) d -> i p d", p=TT)
        wkv_rows = w_qkv.rearrange("(k p) c -> k p c", p=P)

        def tile_dma(eng, to, frm, s):
            for a, b in ((0, 112), (112, TT)):
                eng.dma_start(to[a:b], frm[a:b]).then_inc(s, 16)

        def row_of(rows3, i):
            return rows3[bass.ds(i, 1)].rearrange("o p d -> (o p) d")

        block = ctx.enter_context(nc.Block())

        @block.sync
        def _(sp):
            for i in range(2):
                tile_dma(sp, xs[i], x_rows[i], x_in[i])
            sp.wait_ge(edges_in, 1)
            for t_i, a in ((src_i, src), (dst_i, dst), (ew, edge_weight)):
                full = (CHUNKS - 1) * P
                sp.dma_start(t_i[:, 0:2, :], a[0:2 * P * P].rearrange("(r c e) -> c r e", r=2, e=P)).then_inc(table_in, 16)
                sp.dma_start(t_i[0:LAST_ROWS - 1, 2, :], a[2 * P * P:full].rearrange("(c e) -> c e", e=P)).then_inc(table_in, 16)
                sp.dma_start(t_i[LAST_ROWS - 1:LAST_ROWS, 2, 0:NE - full],
                             a[full:NE].rearrange("(c e) -> c e", c=1)).then_inc(table_in, 16)

            def load_wkv(m):
                if m >= 4:
                    sp.wait_ge(part_lo[m % 2], (m - 2) // 2)
                sp.dma_start(wide[m % 4], wkv_rows[m, :, D:3 * D]).then_inc(stage_in[m % 4], 16)
            load_wkv(0)
            load_wkv(1)
            for i in range(2, NT):
                if i >= 4:
                    sp.wait_ge(xt_psum, i - 3)
                tile_dma(sp, xs[i % 4], x_rows[i], x_in[i % 4])
                if i < KT:
                    load_wkv(i)
            sp.dma_start(qnw, qn_w).then_inc(qn_in, 16)
            def ask(m, h):
                if isinstance(m, int) and m < 2:
                    sp.wait_ge(part_lo[m], KT // 2 - 1)
                else:
                    sp.wait_ge(piece_done, m - 1)
                sp.dma_start(stage[h], w_flat[bass.ds(m, 1)].rearrange("o p c -> (o p) c")).then_inc(stage_in[h], 16)

            def store(m, h, last=False):
                sp.wait_ge(*((last_done, h + 1) if last else (piece_done, m + 1)))
                for hl in range(2):
                    sp.dma_start(split_dram[hl, bass.ds(m, 1)].rearrange("o p c -> (o p) c"), part[h][:, hl, :]).then_inc(part_out[h], 16)
            ask(0, 0)
            sp.wait_ge(xt_done, 2 + NT)
            sp.dma_start(knw, kn_w.partition_broadcast(P)).then_inc(knw_in, 16)
            ask(1, 1)
            with sp.Fori(0, N_PIECE_Q // 2 - 1) as t:
                for h in range(2):
                    store(2 * t + h, h)
                    ask(2 * t + h + 2, h)
            m0 = N_PIECE_Q - 2
            with sp.Fori(0, NT - 1) as t:
                for h in range(2):
                    store(m0 + 2 * t + h, h)
                    ask(m0 + 2 * t + h + 2, h)
            m1 = m0 + 2 * NT
            for h in range(2):
                sp.wait_ge(part_out[h], 32 * N_PIECE_Q // 2)

            def load_wq(t, h):
                for hl in range(2):
                    sp.dma_start(wq[h][:, hl, :, :], split_dram[hl, bass.ds(t, 1), :, h * D:(h + 1) * D].rearrange("o p (k c) -> (o p) k c", c=P)).then_inc(wq_in[h], 16)
            sp.wait_ge(kv_mm, 4 * NT)
            for h in range(2):
                load_wq(0, h)
            for h in range(2):
                store(m1 - 2 + h, h)
                ask(m1 + h, h)
            with sp.Fori(0, KT // 2 - 1) as t:
                for h in range(2):
                    store(m1 + 2 * t + h, h)
                    ask(m1 + 2 * t + h + 2, h)
                for h in range(2):
                    sp.wait_ge(q_mm, 6 * t + 3 * h + 3)
                    load_wq(t + 1, h)
            for h in range(2):
                store(PIECES - 4 + h, h)
                ask(PIECES - 2 + h, h)
            for h in range(2):
                store(PIECES - 2 + h, h, last=True)
            def load_wo(half):
                for hl in range(2):
                    for m in range(N_PIECE_O):
                        sp.dma_start(wo[:, hl, 2 * m:2 * m + 2, half * 512:half * 512 + 512],
                                     split_dram[hl, N_PIECE_Q + m].rearrange("p (k c) -> p k c", c=D)[:, :, half * 512:half * 512 + 512]).then_inc(wo_in[half], 16)
            wg_win = wg_dram.rearrange("l (w m c) -> l m w c", m=P, c=P)
            for k in range(KT):
                sp.wait_ge(acc_lo, k + 1)
                for hl in range(2):
                    sp.dma_start(wg_win[hl, :, 8 * k:8 * k + 8, :], acc_part[:, hl, k, :].rearrange("p (w c) -> p w c", c=P)).then_inc(acc_out, 16)
            sp.wait_ge(acc_out, 16 * 2 * KT)
            for half in range(2):
                if half == 1:
                    sp.wait_ge(eps_mm, 3)
                    for h in range(2):
                        sp.wait_ge(part_out[h], 32 * PIECES // 2)
                    load_wo(0)
                for hl in range(2):
                    sp.dma_start(wg[:, hl, :, half * 512:half * 512 + 512],
                                 wg_dram[hl].rearrange("(k p c) -> p k c", p=P, c=D)[:, :, half * 512:half * 512 + 512]).then_inc(wg_in[half], 16)
            load_wo(1)
            sp.dma_start(bias_b, gnn_bias.partition_broadcast(P)).then_inc(mixc_in, 16)
            sp.dma_start(tm[1], b_out.partition_broadcast(P)).then_inc(mixc_in, 16)
            sp.dma_start(scale_b, norm_scale.partition_broadcast(P)).then_inc(mixc_in, 16)
            sp.dma_start(gate_bias, gate_b.partition_broadcast(P)).then_inc(mixc_in, 16)
            sp.dma_start(gate_f, gate_w).then_inc(mixc_in, 16)

            def load_expert(e, s):
                w1, w2 = eslot[e % 3]
                for hl in range(2):
                    for m in range(2):
                        sp.dma_start(w1[:, hl, m * PIECE:(m + 1) * PIECE], split_dram[hl, N_PIECE_Q + N_PIECE_O + 2 * e + m]).then_inc(s, 16)
                    sp.dma_start(w2[:, hl, :], split_dram[hl, N_PIECE_Q + N_PIECE_O + N_PIECE_1 + e]).then_inc(s, 16)
            tile_dma(sp, xm[0], x_rows[0], xm_in[0])
            tile_dma(sp, xm[1], x_rows[1], xm_in[1])

            sp.wait_ge(zero_ready, 1)
            y_parts = y_dram.rearrange("(p b) (k c) -> p (b k) c", p=P, c=D // 2)

            def zero_part(i):
                n = 2 * BLOCKS // (NT - 1)
                sp.dma_start(y_parts[:, bass.ds(i * n, n), :], zero_row.unsqueeze(1).to_broadcast([P, n, D // 2])).then_inc(y_zero, 16)

            def store_mixed(i, h):
                sp.wait_ge(t_ready, i + 1)
                tile_dma(sp, row_of(t_rows, i), tm[h], t_out[h])
                sp.wait_ge(base_ready, i + 1)
                tile_dma(sp, row_of(base_rows, i), xm[h], base_out[h])
            with sp.Fori(0, NT // 2 - 1) as t:
                for h in range(2):
                    store_mixed(2 * t + h, h)
                    sp.wait_ge(base_out[h], 32 * (t + 1))
                    tile_dma(sp, xm[h], row_of(x_rows, 2 * t + h + 2), xm_in[h])
                    zero_part(2 * t + h)
            zero_part(NT - 2)
            sp.wait_ge(at_done, START + AT_UNITS)
            load_expert(0, w_slot_in)
            for h in range(2):
                store_mixed(NT - 2 + h, h)
            def load_bias(e, s):
                at = e % 3 * BIAS
                sp.dma_start(bias[:, at:at + 2 * HID], mlp1_b[e * 2 * HID:(e + 1) * 2 * HID].partition_broadcast(P)).then_inc(s, 16)
                sp.dma_start(bias[:, at + 2 * HID:at + BIAS], mlp2_b[e * D:(e + 1) * D].partition_broadcast(P)).then_inc(s, 16)
            sp.wait_ge(mix_mm, 2 * NT)
            load_bias(0, w_slot_in)
            sp.wait_ge(w_slot_in, 128)
            sp.sem_inc(expert_ready, 1)
            for h in range(2):
                sp.wait_ge(base_out[h], 16 * NT)
                sp.wait_ge(t_out[h], 16 * NT)
            sp.wait_ge(y_zero, 16 * (NT - 1))
            sp.sem_inc(t_whole, 1)
            sp.wait_ge(gate_done, START + NT)
            sp.wait_ge(row_in[1], 16)
            for e in (1, 2):
                load_expert(e, w_slot_in)
                load_bias(e, w_slot_in)
                sp.wait_ge(w_slot_in, 128 * (e + 1))
                sp.sem_inc(expert_ready, 1)
            for i in range(NT):
                tile_dma(sp, cb[i], base_rows[i], c_base_in)
            sp.wait_ge(count_in, 1)
            for e in range(3, E):
                done = sp.value_load(base_i[0:1, e - 2:e - 1], min_val=1, max_val=BLOCKS)
                sp.wait_ge(y_ready, START + done)
                load_expert(e, w_slot_in)
                load_bias(e, w_slot_in)
                sp.wait_ge(w_slot_in, 128 * (e + 1))
                sp.sem_inc(expert_ready, 1)
            for i in range(NT):
                sp.wait_ge(c_done, i + 1)
                tile_dma(sp, out_rows[i], cb[i], stored[i % 2])
            for h in range(2):
                sp.wait_ge(stored[h], 16 * NT)

        @block.gpsimd
        def _(pool):
            st = Steps(pool, pool_step)
            for s in (q_split, at_done):
                pool.sem_inc(s, START)
            pool.memset(dst_i[:, 2, :], 2047).then_inc(pool_step, 1)
            pool.memset(src_i[:, 2, :], 0).then_inc(pool_step, 1)
            pool.memset(ew[:, 2, :], 0.0).then_inc(pool_step, 1)
            st.n = 3
            pool.wait_ge(pool_step, 3)
            pool.sem_inc(edges_in, 1)
            st.done(pool.memset(ident, 0.0))
            pool.affine_select(out=ident, in_=ident, pattern=[[-1, P]], compare_op=ALU.not_equal, fill=1.0,
                               base=0, channel_multiplier=1).then_inc(consts, 1)
            pool.memset(ones, 1.0).then_inc(consts, 1)
            st.done(pool.memset(upper, 1.0))
            pool.affine_select(out=upper, in_=upper, pattern=[[1, P]], compare_op=ALU.is_gt, fill=0.0,
                               base=0, channel_multiplier=-1).then_inc(consts, 1)
            pool.iota(step_iota, [[1, STEPS]], base=0, channel_multiplier=0,
                      allow_small_or_imprecise_dtypes=True).then_inc(consts, 1)
            pool.iota(col_iota, [[1, P], [0, G]], base=0, channel_multiplier=0,
                      allow_small_or_imprecise_dtypes=True).then_inc(consts, 1)
            pool.memset(zeros, 0.0).then_inc(consts, 1)
            for tile_, v in ((eps_x, EPS_LN / (SX * SX)), (eps_k, EPS_Q * 65536.0), (eps_den, 64e-12 * EPS_Q),
                             (eps_b, EPS_LN), (eps_t, EPS_T / (ST * ST))):
                pool.memset(tile_, v).then_inc(consts, 1)

            pool.wait_ge(consts, 11)
            with pool.Fori(0, KT // 4) as t:
                for b in (1, 3):
                    m = 4 * t + b
                    pool.wait_ge(part_hi, m + 1)
                    pool.tensor_tensor(wkv[:, 1, bass.ds(m, 1), :].rearrange("p o c -> p (o c)"), wide[b],
                                       wkv[:, 0, bass.ds(m, 1), :].rearrange("p o c -> p (o c)"), ALU.subtract).then_inc(part_lo[1], 1)
            pool.wait_ge(table_done, 1)
            pool.memset(w_acc, 0.0).then_inc(acc_zero, 1)

            def piece_lo(t, h, a=0, b=PIECE):
                if a == 0:
                    pool.wait_ge(part_hi, KT + 2 * t + h + 1)
                ins = pool.tensor_tensor(part[h][:, 1, a:b], stage[h][:, a:b], part[h][:, 0, a:b], ALU.subtract)
                if b == PIECE:
                    ins.then_inc(piece_done, 1)
            for h in range(2):
                piece_lo(0, h)
            with pool.Fori(0, NT) as t:
                for h in range(2):
                    piece_lo(1 + t, h)
            pool.wait_ge(kv_mm, 4 * NT)
            for t_ in kvb:
                pool.memset(t_, 0.0).then_inc(kvb_zero, 1)
            pool.wait_ge(kv_used, START + NT)
            st.done(pool.memset(head_mask, 0.0))
            for a in (0, 64):
                pool.memset(head_mask[a:a + 64, a:a + 64], 1.0).then_inc(kvb_zero, 1)
            pool.wait_ge(kvb_zero, 4)
            st.done(pool.memset(qss, 0.0))
            for h in range(2):
                piece_lo(NT + 1, h)
            def q_lo(t, pieces=True):
                for u in range(6):
                    h, g = divmod(u, 3)
                    a, n = GRP[g]
                    pool.wait_ge(q_evac, START + 6 * t + u + 1)
                    pool.tensor_tensor(ut[:, 1, bass.ds(2 * t + h, 1), a:a + n].rearrange("p o n -> p (o n)"),
                                       u32[u % 2][:, 0:n],
                                       ut[:, 0, bass.ds(2 * t + h, 1), a:a + n].rearrange("p o n -> p (o n)"),
                                       ALU.subtract).then_inc(q_split, 1)
                    pool.tensor_tensor(qss[:, g, 0:n], qss[:, g, 0:n], usq[u % 2][:, 0:n], ALU.add).then_inc(q_split, 1)
                    pool.wait_ge(q_split, START + 2 * (6 * t + u) + 2)
                    if pieces and g > 0:
                        piece_lo(12 + t, h, (g - 1) * PIECE // 2, g * PIECE // 2)
            with pool.Fori(0, KT // 2 - 1) as t:
                q_lo(t)
            q_lo(KT // 2 - 1, pieces=False)

            def attend_lo(j, g, unit):
                pool.wait_ge(at_hi, unit + 1)
                pool.tensor_tensor(ut[:, 1, j, bass.ds(g * AW, AW)], att[j % 2], ut[:, 0, j, bass.ds(g * AW, AW)],
                                   ALU.subtract).then_inc(at_done, 1)
            for j in range(PAIRS):
                attend_lo(j, 0, j)

            pool.wait_ge(mixc_in, 80)
            pool.tensor_tensor(bias_b, bias_b, tm[1], ALU.add).then_inc(mixc_ready, 1)
            pool.wait_ge(mixc_ready, 1)
            pool.memset(zero_row, 0.0).then_inc(zero_ready, 1)

            def mix_in(i, h, t):
                pool.wait_ge(xm_in[h], 32 * (t + 1))
                pool.tensor_tensor(xm[h][0:TT], xm[h][0:TT], bias_b[0:TT], ALU.add).then_inc(xb_ready, 1)

            def mix_out(i, h):
                pool.wait_ge(xn2_ready, i + 1)
                pool.tensor_tensor(xm[h][0:TT], xm[h][0:TT], xn2[0:TT], ALU.add).then_inc(base_ready, 1)
            mix_in(0, 0, 0)
            mix_in(1, 1, 0)
            with pool.Fori(0, NT // 2 - 1) as t:
                for h in range(2):
                    for j in range(4 * h, 4 * h + 4):
                        attend_lo(j, t + 1, PAIRS * (t + 1) + j)
                    mix_out(2 * t + h, h)
                    mix_in(2 * t + h + 2, h, t + 1)
            mix_out(NT - 2, 0)
            mix_out(NT - 1, 1)

            pool.wait_ge(mix_mm, 2 * NT)
            for tile_, pattern, mult in ((e_iota, [[0, NT], [1, E]], 0), (b_iota, [[1, BLOCKS]], 0),
                                         (place_iota, [[1, P]], 0), (token_f, [[TT, NT]], 1)):
                pool.iota(tile_, pattern, base=0, channel_multiplier=mult,
                          allow_small_or_imprecise_dtypes=True).then_inc(route_iota, 1)
            for e in range(E - 1):
                for c, at in enumerate(([o // 2 for o in slot_off], [0, BIAS, 2 * BIAS])):
                    pool.memset(moves[:, c, e:e + 1], float(at[(e + 1) % 3] - at[e % 3])).then_inc(route_iota, 1)
            pool.wait_ge(tokens_ready, 1)
            pool.wait_ge(t_whole, 1)

            def gather(b, s):
                pool.tensor_copy(row_idx[s], tok_of[:, bass.ds(b, 1)]).then_inc(idx_ready, 1)
                pool.wait_ge(idx_ready, b + 1)
                apart(pool)
                pool.indirect_dma_start(out=rows[s], out_offset=None, in_=t_dram,
                                        in_offset=bass.IndirectOffsetOnAxis(ap=row_idx[s], axis=0)).then_inc(row_in[s], 16)
            gather(0, 0)
            gather(1, 1)
            with pool.Fori(0, (BLOCKS - 3) // 2) as t:
                for h in range(2):
                    pool.wait_ge(rt_psum, 2 * t + h + 1)
                    gather(2 * t + h + 2, h)
            pool.wait_ge(rt_psum, BLOCKS - 2)
            gather(BLOCKS - 1, (BLOCKS - 1) % 2)
            need = [pool.value_load(stores_i[0:1, h:h + 1], min_val=1, max_val=16 * BLOCKS) for h in range(2)]
            for h in range(2):
                pool.wait_ge(y_out[h], START + need[h])
            apart(pool)
            for i in range(NT):
                pool.indirect_dma_start(
                    out=first_rows[i][0:TT], out_offset=None, in_=y_dram,
                    in_offset=bass.IndirectOffsetOnAxis(ap=slot_first[0:TT, i:i + 1], axis=0)).then_inc(first_in, 16)
            for h in range(2):
                pool.wait_ge(y_out[h], START + 16 * ((BLOCKS + 1 - h) // 2))
            pool.wait_ge(y_ready, START + BLOCKS)
            for i in range(NT):
                if i >= 8:
                    pool.wait_ge(c_done, i - 7)
                pool.indirect_dma_start(
                    out=cy[i % 8][0:TT], out_offset=None, in_=y_dram,
                    in_offset=bass.IndirectOffsetOnAxis(ap=slot_second[0:TT, i:i + 1], axis=0)).then_inc(c_in[i % 8], 16)

        @block.tensor
        def _(pe):
            for s in (kv_used, gate_mm):
                pe.sem_inc(s, START)
            pe.wait_ge(consts, 11)
            pe.wait_ge(table_step, 1)
            rows_of = [P, P, LAST_ROWS]
            for r in range(3):
                for q in range(r):
                    pe.matmul(bank[0][:, r:r + 1], ones[0:rows_of[q], :], n_win[0:rows_of[q], q:q + 1], start=(q == 0), stop=False)
                mm = pe.matmul(bank[0][:, r:r + 1], upper[0:rows_of[r], :], n_win[0:rows_of[r], r:r + 1], start=(r == 0), stop=True)
            mm.then_inc(table_mm, 1)
            pe.wait_ge(table_step, 2)

            def table_column(c):
                for r in range(3):
                    n = rows_of[r]
                    lhs, rhs = (ones[0:n, :], win_pick) if c == 3 else ((key_c, lo_c, ew)[c][0:n, r, :], pick)
                    mm = pe.matmul(bank[4 + c][:, 0:STEPS], lhs, rhs[0:n, r, :], start=(r == 0), stop=(r == 2))
                mm.then_inc(table_mm, 1)

            def xt_tile(i, h, x):
                pe.wait_ge(xn_ready, i + 1)
                pe.wait_ge(xt_done, i + 1)
                for k in range(KT):
                    mm = pe.transpose(bank[2 * h + k // 4][:, (k % 4) * TT:(k % 4 + 1) * TT], x[0:TT, k * P:(k + 1) * P], ident[0:TT, 0:TT])
                mm.then_inc(xt_psum, 1)
            table_column(0)
            xt_tile(0, 0, xs[0])
            table_column(1)
            xt_tile(1, 1, xs[1])
            table_column(2)
            table_column(3)
            with pe.Fori(0, (NT - 2) // 4) as t:
                for k in range(4):
                    xt_tile(4 * t + 2 + k, k % 2, xs[(2 + k) % 4])
            pe.wait_ge(table_done, 1)
            pe.wait_ge(xt_done, 2 + NT)
            for h in range(2):
                pe.wait_ge(part_lo[h], KT // 2)
            for b in range(3):
                pe.matmul(bank[3 + b][:, :], zeros, wkv[:, 0, 0, 0:512], start=True, stop=False, skip_group_check=True)

            def kv_unit(i, b, c0):
                for k in range(KT):
                    for n, (l, r) in enumerate(((0, 0), (0, 1), (1, 0))):
                        mm = pe.matmul(bank[b][0:TT, :], xt[:, l, k, tok(i)], wkv[:, r, k, c0:c0 + 512],
                                       start=(k == 0 and n == 0), stop=(k == KT - 1 and n == 2))
                mm.then_inc(kv_mm, 1)

            def kv_sums():
                for p in range(PAIRS):
                    for l, r in ((0, 0), (0, 1), (1, 0)):
                        mm = pe.matmul(bank[3 + p // 3][:, (p % 3) * 130:(p % 3) * 130 + 129], kt_[l][0:TT, p * P:(p + 1) * P],
                                       vt_[r][0:TT, p, 0:129], start=False, stop=False, skip_group_check=True)
                mm.then_inc(kv_used, 1)

            def steps(n, h):
                pe.wait_ge(hot_ready, n + 1)
                pe.wait_ge(acc_done, START + G * n)
                for j in range(G):
                    o = bank[6 + j // 4][:, (j % 4) * P:(j % 4 + 1) * P]
                    pe.matmul(o, one_hot[h][:, 1, :, j], one_hot[h][:, 0, :, j], start=True, stop=False)
                    mm = pe.matmul(o, one_hot[h][:, 2, :, j], one_hot[h][:, 0, :, j], start=False, stop=True)
                    if j % 4 == 3:
                        mm.then_inc(step_mm, 1)

            def kv_tile(i, s, first=False):
                kv_unit(i, 0, 0)
                if not first:
                    pe.wait_ge(v_lo, 2 * i)
                    kv_sums()
                steps(3 * i, s % 2)
                kv_unit(i, 1, 512)
                kv_unit(i, 2, 1024)
                steps(3 * i + 1, (s + 1) % 2)
                pe.wait_ge(kw_ready, 2 * i + 2)
                kv_unit(i, 1, 1536)
                steps(3 * i + 2, (s + 2) % 2)
            kv_tile(0, 0, True)
            kv_tile(1, 3)
            with pe.Fori(1, NT // 2) as t:
                for h in range(2):
                    kv_tile(2 * t + h, 3 * h)
            pe.wait_ge(v_lo, 2 * NT)
            kv_sums()

            def q_units(t, groups):
                for u in range(6):
                    h, g = divmod(u, 3)
                    a, n = GRP[g]
                    if g == 0:
                        pe.wait_ge(wq_in[h], 32 * (t + 1))
                    pe.wait_ge(q_evac, START + 6 * t + max(u - 2, 0))
                    for k in range(KT):
                        for c, (l, r) in enumerate(((0, 0), (1, 0), (0, 1))):
                            mm = pe.matmul(bank[u % 3][:, 0:n], wq[h][:, l, k, :], xt[:, r, k, a:a + n],
                                           start=(k == 0 and c == 0), stop=(k == KT - 1 and c == 2))
                    mm.then_inc(q_mm, 1)
                    if u < groups:
                        steps(KV_GROUPS + 6 * t + u, u % 2)
            with pe.Fori(0, KT // 2 - 1) as t:
                q_units(t, 6)
            q_units(KT // 2 - 1, 1)
            pe.wait_ge(q_split, START + 6 * KT)
            pe.wait_ge(q_evac, START + 3 * KT)
            pe.wait_ge(kvb_ready, 1)
            for g in range(3):
                pe.matmul(bank[g][:, 0:GRP[g][1]], ones, qss[:, g, 0:GRP[g][1]], start=True, stop=True).then_inc(eps_mm, 1)
            def attend_unit(j, g, unit):
                o = bank[2 + j % 2]
                pe.wait_ge(at_f, START + (max(unit - 1, 0) if isinstance(unit, int) else unit - 1))
                for at, w in ((0, kvb), (256, ksb)):
                    for c, (l, r) in enumerate(((0, 0), (1, 0), (0, 1))):
                        mm = pe.matmul(o[:, at:at + AW], w[l][:, j, :], ut[:, r, j, bass.ds(g * AW, AW)], start=(c == 0), stop=(c == 2))
                mm.then_inc(at_mm, 1)
            pe.wait_ge(eps_ready, 3)
            for j in range(PAIRS):
                attend_unit(j, 0, j)


            def mix_tile(i, h, t, attend=True):
                if h == 0:
                    pe.wait_ge(at_done, START + PAIRS * (t + 1))
                for half in range(2):
                    c0 = half * 512
                    if not (isinstance(i, int) and i == 0):
                        pe.wait_ge(x1_half, 2 * i - 1 + half)
                    for m, (a_, w_) in enumerate(((ut, wo), (xt, wg))):
                        if isinstance(i, int) and i == 0:
                            pe.wait_ge((wo_in, wg_in)[m][half], (16 * 2 * N_PIECE_O, 32)[m])
                        if attend:
                            j = 4 * h + 2 * half + m
                            attend_unit(j, t + 1, PAIRS * (t + 1) + j)
                        for k in range(KT):
                            for c, (l, r) in enumerate(((0, 0), (0, 1), (1, 0))):
                                mm = pe.matmul(bank[half][0:TT, :], a_[:, l, k, tok(i)], w_[:, r, k, c0:c0 + 512],
                                               start=(m == 0 and k == 0 and c == 0), stop=(m == 1 and k == KT - 1 and c == 2))
                        if m == 1:
                            mm.then_inc(mix_mm, 1)

            def gate_tile(i, h):
                pe.wait_ge(t_ready, i + 1)
                for k in range(KT):
                    mm = pe.transpose(bank[4 + k // 4][:, (k % 4) * TT:(k % 4 + 1) * TT], tm[h][0:TT, k * P:(k + 1) * P], ident[0:TT, 0:TT])
                mm.then_inc(tt_psum, 1)

            def gate_logits(i):
                pe.wait_ge(tt_done, i + 1)
                pe.wait_ge(gate_done, START + i)
                for k in range(KT):
                    for c, (l, r) in enumerate(((0, 0), (0, 1), (1, 0))):
                        mm = pe.matmul(bank[6][0:TT, 0:E], tt[:, l, k, :], gate_hl[:, r, k * E:(k + 1) * E],
                                       start=(k == 0 and c == 0), stop=(k == KT - 1 and c == 2))
                mm.then_inc(gate_mm, 1)
            mix_tile(0, 0, 0)
            mix_tile(1, 1, 0)
            gate_tile(0, 0)
            pe.wait_ge(gate_w_ready, 1)
            with pe.Fori(1, NT // 2 - 1) as t:
                for h in range(2):
                    i = 2 * t + h
                    mix_tile(i, h, t)
                    gate_logits(i - 2)
                    gate_tile(i - 1, 1 - h)
            for h in range(2):
                i = NT - 2 + h
                mix_tile(i, h, NT // 2 - 1, attend=False)
                gate_logits(i - 2)
                gate_tile(i - 1, 1 - h)
            gate_logits(NT - 2)
            gate_tile(NT - 1, 1)
            gate_logits(NT - 1)
            pe.wait_ge(route_mm, 1)
            pe.matmul(bank[0][0:TT, 0:NT * E], upper[0:TT, 0:TT], both[0:TT].rearrange("p a b -> p (a b)"), start=True, stop=True)
            pe.matmul(bank[1][:, 0:NT * E], ones[0:TT, :], both[0:TT].rearrange("p a b -> p (a b)"), start=True, stop=True).then_inc(route_mm, 1)
            pe.wait_ge(slots_ready, 1)
            for u in range(2 * NT):
                mm = pe.matmul(bank[4][:, 0:BLOCKS], place_hot[0:TT, u, :], block_token[0:TT, u, :], start=(u == 0), stop=(u == 2 * NT - 1))
            mm.then_inc(token_mm, 1)
            def row_T(b, s, q):
                pe.wait_ge(row_in[s], 16 * (q + 1))
                for k in range(KT):
                    mm = pe.transpose(bank[2 + 2 * s + k // 4][:, (k % 4) * P:(k % 4 + 1) * P], rows[s][:, k * P:(k + 1) * P], ident)
                mm.then_inc(rt_psum, 1)

            def up(b, s, off, half):
                if half == 0:
                    pe.wait_ge(rt_done, b + 1)
                    pe.wait_ge(h_evac, b)
                for k in range(4 * half, 4 * half + 4):
                    for c, (l, r) in enumerate(((0, 0), (0, 1), (1, 0))):
                        mm = pe.matmul(bank[6][:, :], rowT[s][:, l, k, :], arena16[:, bass.ds(off + (r * KT + k) * 512, 512)],
                                       start=(k == 0 and c == 0), stop=(k == KT - 1 and c == 2))
                if half == 1:
                    mm.then_inc(h_mm, 1)

            def act_T(b):
                pe.wait_ge(act_ready, b + 1)
                for k in range(2):
                    mm = pe.transpose(bank[7][:, k * P:(k + 1) * P], act[:, k * P:(k + 1) * P], ident)
                mm.then_inc(at_psum, 1)

            def down(b):
                off = pe.value_load(blk_i[0:1, bass.ds(b, 1)], min_val=0, max_val=TOP // 2 - 12288)
                pe.wait_ge(a_done, b + 1)
                pe.wait_ge(y_ready, START + b)
                for half in range(2):
                    for k in range(2):
                        for c, (l, r) in enumerate(((0, 0), (0, 1), (1, 0))):
                            mm = pe.matmul(bank[half][:, :], actT[:, l, k, :], arena16[:, bass.ds(off + 8192 + r * 2048 + k * D + half * 512, 512)],
                                           start=(k == 0 and c == 0), stop=(k == 1 and c == 2))
                mm.then_inc(y_mm, 1)

            def expert_block(b, s, q, first=False, last=False):
                off = pe.value_load(blk_i[0:1, bass.ds(b, 1)], min_val=0, max_val=TOP // 2 - 12288)
                need = pe.value_load(exp_i[0:1, bass.ds(b, 1)], min_val=0, max_val=E)
                if not last:
                    row_T(b + 1, 1 - s, q + s)
                pe.wait_ge(expert_ready, need + 1)
                up(b, s, off, 0)
                if not first:
                    act_T(b - 1)
                up(b, s, off, 1)
                if not first:
                    down(b - 1)
            pe.wait_ge(count_in, 1)
            row_T(0, 0, 0)
            expert_block(0, 0, 0, first=True)
            with pe.Fori(0, (BLOCKS - 3) // 2) as t:
                expert_block(2 * t + 1, 1, t)
                expert_block(2 * t + 2, 0, t + 1)
            expert_block(BLOCKS - 2, 1, (BLOCKS - 2) // 2)
            expert_block(BLOCKS - 1, 0, (BLOCKS - 1) // 2, last=True)
            act_T(BLOCKS - 1)
            down(BLOCKS - 1)

        @block.scalar
        def _(act_e):
            a_ = act_e
            st = Steps(a_, act_step)
            for s in (q_evac, y_out[0], y_out[1]):
                a_.sem_inc(s, START)
            a_.wait_ge(consts, 11)

            def xt_copy(i, h):
                a_.wait_ge(xt_psum, i + 1)
                apart(a_)
                for b in range(2):
                    a_.activation(xt[:, 0, 4 * b:4 * b + 4, tok(i)], bank[2 * h + b][:, 0:4 * TT].rearrange("p (k n) -> p k n", n=TT), ACT.Copy).then_inc(xt_hi, 1)

            def ln_sqrt(i, h):
                a_.wait_ge(stat_ready, i + 1)
                a_.activation(ln_sd[0:TT, h, :], ln_mv[0:TT, h, 1:2], ACT.Sqrt, bias=eps_x[0:TT], scale=1.0 / (SX * SX)).then_inc(sd_ready, 1)
            def wkv_hi(m, b, t):
                to = wkv[:, 0, bass.ds(m, 1), :].rearrange("p o c -> p (o c)")
                a_.wait_ge(stage_in[b], 16 * (t + 1))
                if b % 2 == 1:
                    a_.activation(wide[b], wide[b], ACT.Copy, scale=SW).then_inc(wkv_scaled, 1)
                    a_.wait_ge(wkv_scaled, 2 * t + b // 2 + 1)
                apart(a_)
                a_.activation(to, wide[b], ACT.Copy, scale=1.0 if b % 2 == 1 else SW).then_inc(part_hi, 1)
            ln_sqrt(0, 0)
            ln_sqrt(1, 1)
            with a_.Fori(0, (NT - 2) // 4) as t:
                for k in range(4):
                    i, h = 4 * t + 2 + k, k % 2
                    xt_copy(i - 2, h)
                    ln_sqrt(i, h)
                    wkv_hi(i - 2, k, t)
            xt_copy(NT - 2, 0)
            xt_copy(NT - 1, 1)

            def piece_hi(t, h):
                a_.wait_ge(stage_in[h], 16 * (KT // 4 + t + 1))
                a_.activation(stage[h], stage[h], ACT.Copy, scale=SW).then_inc(piece_scaled, 1)
                a_.wait_ge(piece_scaled, 2 * t + h + 1)
                if not (isinstance(t, int) and t == 0):
                    a_.wait_ge(part_out[h], 32 * t)
                a_.activation(part[h][:, 0, :], stage[h], ACT.Copy).then_inc(part_hi, 1)
            for h in range(2):
                a_.wait_ge(part_lo[h], KT // 2)
            for h in range(2):
                piece_hi(0, h)

            def k_half(i, c):
                a_.wait_ge(kv_mm, 4 * i + c + 1)
                a_.activation(junk[0:TT], bank[c][0:TT, :], ACT.Square, accum_out=tiny[0:TT, c:c + 1]).then_inc(k_sq, 1)
                a_.wait_ge(kw_ready, 2 * i + c + 1)
                a_.activation(kt_[0][0:TT, c * 512:(c + 1) * 512], kw[0:TT], ACT.Relu).then_inc(k_hi, 1)

            def v_half(i, c):
                a_.wait_ge(kv_mm, 4 * i + 3 + c)
                a_.activation(vt_[0][0:TT, 4 * c:4 * c + 4, 0:P], bank[2 - c][0:TT, :].rearrange("p (a b) -> p a b", b=P),
                              ACT.Copy, scale=tiny[0:TT, 4:5]).then_inc(v_hi, 1)

            def kv_tile(i, t, h):
                k_half(i, 0)
                piece_hi(1 + 2 * t + h, 0)
                k_half(i, 1)
                a_.wait_ge(k_ss, i + 1)
                a_.activation(tiny[0:TT, 3:4], tiny[0:TT, 2:3], ACT.Sqrt, bias=eps_k[0:TT], scale=2.0 ** -20).then_inc(k_sd, 1)
                a_.wait_ge(k_rs, i + 1)
                v_half(i, 0)
                piece_hi(1 + 2 * t + h, 1)
                v_half(i, 1)
            with a_.Fori(0, NT // 2) as t:
                for h in range(2):
                    kv_tile(2 * t + h, t, h)
            a_.wait_ge(kv_used, START + NT)
            a_.wait_ge(kvb_zero, 4)
            for p in range(PAIRS):
                for r0 in (0, 64):
                    c0 = (p % 3) * 130 + r0
                    ins = a_.activation(kvb[0][r0:r0 + 64, p, r0:r0 + 64], bank[3 + p // 3][r0:r0 + 64, c0:c0 + 64], ACT.Copy, scale=2.0 ** -12)
            ins.then_inc(kvf_hi, 1)
            for h in range(2):
                piece_hi(NT + 1, h)

            a_.wait_ge(qn_ready, 1)
            def acc_part_hi(k):
                a_.activation(acc_part[:, 0, k, :], w_acc[:, k * D:(k + 1) * D], ACT.Copy).then_inc(acc_hi, 1)

            def q_turn(t, last=False):
                for u in range(6):
                    h, g = divmod(u, 3)
                    a, n = GRP[g]
                    a_.wait_ge(q_mm, 6 * t + u + 1)
                    a_.wait_ge(q_split, START + 2 * (6 * t + max(u - 1, 0)))
                    a_.activation(usq[u % 2][:, 0:n], bank[u % 3][:, 0:n], ACT.Square, scale=1.0 / (SX * SW)).then_inc(act_step, 1)
                    a_.activation(ut[:, 0, bass.ds(2 * t + h, 1), a:a + n].rearrange("p o n -> p (o n)"), bank[u % 3][:, 0:n], ACT.Relu,
                                  scale=qnw[:, bass.ds(2 * t + h, 1)])
                    a_.activation(u32[u % 2][:, 0:n], bank[u % 3][:, 0:n], ACT.Relu, scale=qnw[:, bass.ds(2 * t + h, 1)]).then_inc(q_evac, 1)
                    if not last and g == 0:
                        piece_hi(12 + t, h)
                    if last and u < 2:
                        piece_hi(12 + t, u)
                    if last and u >= 2:
                        if u == 2:
                            a_.wait_ge(hot_ready, GROUPS + 2)
                        acc_part_hi(2 * u - 4)
                        acc_part_hi(2 * u - 3)
            with a_.Fori(0, KT // 2 - 1) as t:
                q_turn(t)
            q_turn(KT // 2 - 1, last=True)
            for g in range(3):
                a_.wait_ge(eps_mm, g + 1)
                a_.activation(eps_row[:, GRP[g][0]:sum(GRP[g])], bank[g][:, 0:GRP[g][1]], ACT.Sqrt, bias=eps_den, scale=64e-12 / D).then_inc(eps_ready, 1)
            def attend_hi(j, g, unit):
                a_.wait_ge(at_f, START + unit + 1)
                apart(a_)
                a_.activation(ut[:, 0, j, bass.ds(g * AW, AW)], att[j % 2], ACT.Copy).then_inc(at_hi, 1)

            def mix_sqrt(i, h):
                a_.wait_ge(stat2_ready, 2 * i + 1)
                a_.activation(ln_sd[0:TT, h, :], ln_mv[0:TT, h, 1:2], ACT.Sqrt, bias=eps_b[0:TT]).then_inc(sd2_ready, 1)
                a_.wait_ge(stat2_ready, 2 * i + 2)
                a_.activation(tiny[0:TT, 1:2], tiny[0:TT, 0:1], ACT.Sqrt, bias=eps_t[0:TT], scale=1.0 / (ST * ST)).then_inc(sd2_ready, 1)

            def tt_copy(i):
                a_.wait_ge(tt_psum, i + 1)
                a_.wait_ge(gate_mm, START + i)
                for b in range(2):
                    a_.activation(tt[:, 0, 4 * b:4 * b + 4, :], bank[4 + b][:, 0:4 * TT].rearrange("p (k n) -> p k n", n=TT), ACT.Copy).then_inc(tt_hi, 1)

            def mix_period(i, h, t, attend=True, first=False, last=False):
                if attend:
                    for j in range(4 * h, 4 * h + 4):
                        attend_hi(j, t + 1, PAIRS * (t + 1) + j)
                if last:
                    mix_sqrt(i, h)
                if not first:
                    tt_copy(i - 1)
                if not last:
                    mix_sqrt(i, h)
            for j in range(PAIRS):
                attend_hi(j, 0, j)
            mix_period(0, 0, 0, first=True)
            mix_period(1, 1, 0)
            with a_.Fori(1, NT // 2 - 1) as t:
                for h in range(2):
                    mix_period(2 * t + h, h, t)
            for h in range(2):
                mix_period(NT - 2 + h, h, NT // 2 - 1, attend=False, last=(h == 1))
            tt_copy(NT - 1)
            a_.wait_ge(route_exp, 1)
            a_.activation(pe_[0:TT], pe_[0:TT], ACT.Exp).then_inc(pexp_in, 1)
            def row_hi(b, s, first=False):
                a_.wait_ge(rt_psum, b + 1)
                if not first:
                    a_.wait_ge(h_mm, b - 1)
                for q in range(2):
                    a_.activation(rowT[s][:, 0, 4 * q:4 * q + 4, :], bank[2 + 2 * s + q][:, :].rearrange("p (k n) -> p k n", n=P), ACT.Copy).then_inc(rt_hi, 1)

            def act_hi(b):
                a_.wait_ge(at_psum, b + 1)
                a_.wait_ge(y_mm, b)
                a_.activation(actT[:, 0, :, :], bank[7][:, 0:2 * P].rearrange("p (k n) -> p k n", n=P), ACT.Copy).then_inc(a_hi, 1)

            def sigmoid(b):
                a_.wait_ge(glu_ready, b + 1)
                a_.wait_ge(act_ready, b)
                a_.activation(sg, glu, ACT.Sigmoid, scale=1.702).then_inc(sg_ready, 1)

            def store_y(b, s):
                a_.wait_ge(y_ready, START + b + 1)
                a_.dma_start(y_dram[bass.ds(b * P, P), :], ysb[s]).then_inc(y_out[s], 16)
            a_.wait_ge(y_zero, 16 * (NT - 1))
            row_hi(0, 0, first=True)
            row_hi(1, 1, first=True)
            sigmoid(0)
            row_hi(2, 0)
            act_hi(0)
            sigmoid(1)
            with a_.Fori(0, (BLOCKS - 3) // 2) as t:
                for h in range(2):
                    b = 2 * t + h + 2
                    row_hi(b + 1, 1 - h)
                    act_hi(b - 1)
                    store_y(b - 2, h)
                    sigmoid(b)
            act_hi(BLOCKS - 2)
            store_y(BLOCKS - 3, (BLOCKS - 3) % 2)
            sigmoid(BLOCKS - 1)
            act_hi(BLOCKS - 1)
            store_y(BLOCKS - 2, (BLOCKS - 2) % 2)
            store_y(BLOCKS - 1, (BLOCKS - 1) % 2)

        @block.vector
        def _(v):
            st = Steps(v, dve_step)
            v.sem_inc(xt_done, 2)
            for s in (at_f, gate_done, y_ready, acc_done):
                v.sem_inc(s, START)
            v.wait_ge(consts, 11)
            v.wait_ge(table_in, 16 * 9)
            flat = lambda a: a.rearrange("p a b -> p (a b)")
            st.done(v.tensor_scalar(flat(hi_i), flat(src_i), 7, None, ALU.logical_shift_right))
            st.done(v.tensor_copy(flat(hi_f), flat(hi_i)))
            st.done(v.tensor_scalar(flat(hi_i), flat(src_i), P - 1, None, ALU.bitwise_and))
            v.tensor_copy(flat(lo_c), flat(hi_i))
            v.tensor_scalar(flat(big), flat(hi_f), float(D // P), 16384.0, ALU.is_ge, ALU.mult)
            st.done(v.tensor_copy(flat(key_c), flat(dst_i)))
            st.done(v.scalar_tensor_tensor(flat(key_c), flat(key_c), float(D // P), flat(hi_f), ALU.mult, ALU.add))
            st.done(v.tensor_tensor(flat(key_c), flat(key_c), flat(big), ALU.add))
            for c, col in ((0, 0), (1, P - 1)):
                ins = v.tensor_scalar(ends_i[:, :, c], dst_i[:, :, col], 4, None, ALU.logical_shift_right)
            st.done(ins)
            v.tensor_scalar(w_first, ends_i[:, :, 0], float(WINDOWS - 1), None, ALU.min)
            st.done(v.tensor_scalar(w_last, ends_i[:, :, 1], float(WINDOWS - 1), None, ALU.min))
            v.scalar_tensor_tensor(n_win, w_last, 1.0, w_first, ALU.add, ALU.subtract).then_inc(table_step, 1)
            v.wait_ge(table_mm, 1)
            st.done(v.tensor_copy(first, bank[0][:, 0:3]))
            v.tensor_tensor(past, first, n_win, ALU.add)
            st.done(v.tensor_tensor(shift, w_first, first, ALU.subtract))
            for r in range(3):
                st.done(v.tensor_scalar(pick[:, r, :], step_iota, first[:, r:r + 1], None, ALU.is_ge))
                st.done(v.scalar_tensor_tensor(pick[:, r, :], step_iota, past[:, r:r + 1], pick[:, r, :], ALU.is_lt, ALU.mult))
                ins = v.scalar_tensor_tensor(win_pick[:, r, :], step_iota, shift[:, r:r + 1], pick[:, r, :], ALU.add, ALU.mult)
            ins.then_inc(table_step, 1)

            def read_table():
                v.wait_ge(table_mm, 5)
                st.done(v.tensor_copy(win_f, bank[7][:, 0:STEPS]))
                v.scalar_tensor_tensor(key16, win_f, -float(P), bank[4][:, 0:STEPS], ALU.mult, ALU.add)
                v.tensor_copy(lo16, bank[5][:, 0:STEPS])
                st.done(v.tensor_scalar(wsc, bank[6][:, 0:STEPS], SW, None, ALU.mult))
                st.done(v.tensor_copy(whi, wsc))
                v.tensor_tensor(wlo, wsc, whi, ALU.subtract)
                v.tensor_scalar(win_at, win_f, float(P), None, ALU.mult).then_inc(table_done, 1)
                v.wait_ge(table_done, 1)

            def stats(b, h, uses):
                v.wait_ge(x_in[b], 32 * uses)
                v.bn_stats(ln_st[0:TT, h, 0:6], xs[b][0:TT, 0:512])
                st.done(v.bn_stats(ln_st[0:TT, h, 6:12], xs[b][0:TT, 512:1024]))
                apart(v)
                v.bn_aggr(ln_mv[0:TT, h, :], ln_st[0:TT, h, :]).then_inc(stat_ready, 1)

            def norm(i, h, b):
                v.wait_ge(sd_ready, i + 1)
                st.done(v.reciprocal(ln_rs[0:TT, h, :], ln_sd[0:TT, h, :]))
                v.tensor_scalar(xs[b][0:TT], xs[b][0:TT], ln_mv[0:TT, h, 0:1], ln_rs[0:TT, h, :], ALU.subtract, ALU.mult).then_inc(xn_ready, 1)

            def xt_lo(i, h):
                for b in range(2):
                    v.wait_ge(xt_hi, 2 * i + b + 1)
                    ins = v.tensor_tensor(xt[:, 1, 4 * b:4 * b + 4, tok(i)], bank[2 * h + b][:, 0:4 * TT].rearrange("p (k n) -> p k n", n=TT),
                                          xt[:, 0, 4 * b:4 * b + 4, tok(i)], ALU.subtract)
                ins.then_inc(xt_done, 1)
            def wkv_lo(m, b):
                v.wait_ge(part_hi, m + 1)
                v.scalar_tensor_tensor(wkv[:, 1, bass.ds(m, 1), :].rearrange("p o c -> p (o c)"), wide[b], SW,
                                       wkv[:, 0, bass.ds(m, 1), :].rearrange("p o c -> p (o c)"), ALU.mult, ALU.subtract).then_inc(part_lo[0], 1)
            for h in range(2):
                stats(h, h, 1)
                norm(h, h, h)
            with v.Fori(0, (NT - 2) // 4) as t:
                st.enter(t, 8)
                for k in range(4):
                    i, h, b = 4 * t + 2 + k, k % 2, (2 + k) % 4
                    stats(b, h, t + 1 + k // 2)
                    xt_lo(i - 2, h)
                    norm(i, h, b)
                    if h == 0:
                        wkv_lo(i - 2, k)
            st.leave((NT - 2) // 4)
            xt_lo(NT - 2, 0)
            xt_lo(NT - 1, 1)
            read_table()
            v.wait_ge(qn_in, 16)
            v.tensor_scalar(qnw, qnw, 1.0 / SW, None, ALU.mult).then_inc(qn_ready, 1)

            def make(n, s, k):
                cols = lambda a: a[:, bass.ds(n * G, G)].unsqueeze(1).to_broadcast([P, P, G])
                if k == 0:
                    v.tensor_tensor(one_hot[s][:, 0], col_iota, cols(lo16), ALU.is_equal)
                elif k == 1:
                    v.wait_ge(hot_ready, n)
                    v.tensor_tensor(key_hot, col_iota, cols(key16), ALU.is_equal).then_inc(hot_key, 1)
                elif k == 2:
                    v.wait_ge(hot_key, n + 1)
                    v.tensor_tensor(one_hot[s][:, 1], key_hot, cols(whi), ALU.mult)
                else:
                    v.tensor_tensor(one_hot[s][:, 2], key_hot, cols(wlo), ALU.mult).then_inc(hot_ready, 1)

            def accumulate(n, s):
                _, at = nc.values_load_multi_w_load_instructions(
                    win_at[0:1, bass.ds(n * G, G)], engines=(ENG.DVE,), min_val=0, max_val=(WINDOWS - 1) * P,
                    skip_runtime_bounds_check_because="the table clips windows to WINDOWS - 1")
                for j in range(G):
                    v.wait_ge(step_mm, 2 * n + j // 4 + 1)
                    v.wait_ge(acc_done, START + G * n + j)
                    v.tensor_tensor(w_acc[:, bass.ds(at[j], P)], bank[6 + j // 4][:, (j % 4) * P:(j % 4 + 1) * P],
                                    w_acc[:, bass.ds(at[j], P)], ALU.add).then_inc(acc_done, 1)
                    if j in (4, 5):
                        make(n + 2, s, j - 4)
                for k in (2, 3):
                    make(n + 2, s, k)
            for n in range(2):
                for k in range(4):
                    make(n, n, k)

            def k_half(i, c):
                v.wait_ge(k_sq, 2 * i + c + 1)
                v.scalar_tensor_tensor(kw[0:TT], bank[c][0:TT, :], 1.0 / SW, knw[0:TT, c * 512:(c + 1) * 512], ALU.mult, ALU.mult).then_inc(kw_ready, 1)
                v.wait_ge(k_hi, 2 * i + c + 1)
                st.done(v.scalar_tensor_tensor(kt_[1][0:TT, c * 512:(c + 1) * 512], kw[0:TT], 0.0, kt_[0][0:TT, c * 512:(c + 1) * 512], ALU.max, ALU.subtract))

            def v_half(i, c):
                v.wait_ge(v_hi, 2 * i + c + 1)
                v.scalar_tensor_tensor(vt_[1][0:TT, 4 * c:4 * c + 4, 0:P], bank[2 - c][0:TT, :].rearrange("p (a b) -> p a b", b=P),
                                       tiny[0:TT, 4:5], vt_[0][0:TT, 4 * c:4 * c + 4, 0:P], ALU.mult, ALU.subtract).then_inc(v_lo, 1)

            def kv_tile(i, s):
                v.wait_ge(kv_used, START + i)
                k_half(i, 0)
                accumulate(3 * i, s % 2)
                k_half(i, 1)
                v.tensor_tensor(tiny[0:TT, 2:3], tiny[0:TT, 0:1], tiny[0:TT, 1:2], ALU.add).then_inc(k_ss, 1)
                v.wait_ge(k_sd, i + 1)
                st.done(v.reciprocal(tiny[0:TT, 4:5], tiny[0:TT, 3:4]))
                st.done(v.tensor_scalar(tiny[0:TT, 5:6], tiny[0:TT, 4:5], SX * SW, None, ALU.mult))
                st.done(v.tensor_scalar(vt_[0][0:TT, :, P], ones[0:TT, 0:PAIRS], tiny[0:TT, 5:6], None, ALU.mult))
                v.scalar_tensor_tensor(vt_[1][0:TT, :, P], ones[0:TT, 0:PAIRS], tiny[0:TT, 5:6], vt_[0][0:TT, :, P], ALU.mult, ALU.subtract).then_inc(k_rs, 1)
                v_half(i, 0)
                accumulate(3 * i + 1, (s + 1) % 2)
                v_half(i, 1)
                accumulate(3 * i + 2, (s + 2) % 2)
            v.wait_ge(acc_zero, 1)
            v.wait_ge(knw_in, 16)
            with v.Fori(0, NT // 2) as t:
                st.enter(t, 10)
                for h in range(2):
                    kv_tile(2 * t + h, 3 * h)
            st.leave(NT // 2)
            with v.Fori(0, KT // 2 - 1) as t:
                for u in range(6):
                    accumulate(KV_GROUPS + 6 * t + u, u % 2)
            accumulate(GROUPS - 1, 0)
            for h in range(2):
                v.wait_ge(part_hi, KT + PIECES - 1 + h)
                v.tensor_tensor(part[h][:, 1, :], stage[h], part[h][:, 0, :], ALU.subtract).then_inc(last_done, 1)
            v.wait_ge(piece_done, PIECES - 2)
            v.wait_ge(last_done, 2)
            for k in range(8):
                v.wait_ge(acc_hi, k + 1)
                v.tensor_tensor(acc_part[:, 1, k, :], w_acc[:, k * D:(k + 1) * D], acc_part[:, 0, k, :], ALU.subtract).then_inc(acc_lo, 1)
            v.wait_ge(kvf_hi, 1)
            for p in range(PAIRS):
                for r0 in (0, 64):
                    c0 = (p % 3) * 130 + r0
                    v.scalar_tensor_tensor(kvb[1][r0:r0 + 64, p, r0:r0 + 64], bank[3 + p // 3][r0:r0 + 64, c0:c0 + 64], 2.0 ** -12,
                                           kvb[0][r0:r0 + 64, p, r0:r0 + 64], ALU.mult, ALU.subtract)
            for b in range(3):
                n = min(3, PAIRS - 3 * b)
                ins = v.tensor_scalar(ksf[:, 3 * b:3 * b + n], bank[3 + b][:, 0:390].rearrange("p (a b) -> p a b", b=130)[:, 0:n, P], 2.0 ** -12, None, ALU.mult)
            st.done(ins)
            for p in range(PAIRS):
                ins = v.tensor_scalar(ksb[0][:, p, :], head_mask, ksf[:, p:p + 1], None, ALU.mult)
            st.done(ins)
            for p in range(PAIRS):
                ins = v.scalar_tensor_tensor(ksb[1][:, p, :], head_mask, ksf[:, p:p + 1], ksb[0][:, p, :], ALU.mult, ALU.subtract)
            ins.then_inc(kvb_ready, 1)

            def attend_unit(j, g, unit):
                o, a = bank[2 + j % 2], att[j % 2]
                v.wait_ge(at_mm, unit + 1)
                v.wait_ge(at_done, START + (max(unit - 1, 0) if isinstance(unit, int) else unit - 1))
                st.done(v.tensor_tensor(a, o[:, 256:256 + AW], eps_row[:, bass.ds(g * AW, AW)], ALU.add))
                st.done(v.reciprocal(a, a))
                v.scalar_tensor_tensor(a, o[:, 0:AW], SX, a, ALU.mult, ALU.mult).then_inc(at_f, 1)
            v.wait_ge(eps_ready, 3)
            for j in range(PAIRS):
                attend_unit(j, 0, j)

            v.wait_ge(mixc_in, 80)
            st.done(v.tensor_scalar(gate_hl[:, 0, :], gate_f, SW, None, ALU.mult))
            v.scalar_tensor_tensor(gate_hl[:, 1, :], gate_f, SW, gate_hl[:, 0, :], ALU.mult, ALU.subtract).then_inc(gate_w_ready, 1)

            def add_half(i, h, half):
                c = slice(half * 512, half * 512 + 512)
                v.wait_ge(xb_ready, i + 1)
                v.wait_ge(mix_mm, 2 * i + half + 1)
                v.scalar_tensor_tensor(xm[h][0:TT, c], bank[half][0:TT, :], 1.0 / (SX * SW), xm[h][0:TT, c], ALU.mult, ALU.add).then_inc(x1_half, 1)

            def mix_norm(i, t, h):
                v.wait_ge(x1_half, 2 * i + 2)
                v.bn_stats(ln_st[0:TT, h, 0:6], xm[h][0:TT, 0:512])
                st.done(v.bn_stats(ln_st[0:TT, h, 6:12], xm[h][0:TT, 512:1024]))
                apart(v)
                v.bn_aggr(ln_mv[0:TT, h, :], ln_st[0:TT, h, :]).then_inc(stat2_ready, 1)
                v.wait_ge(sd2_ready, 2 * i + 1)
                st.done(v.reciprocal(ln_rs[0:TT, h, :], ln_sd[0:TT, h, :]))
                v.tensor_scalar(tiny[0:TT, 0:1], ln_mv[0:TT, h, 1:2], ln_rs[0:TT, h, :], ln_rs[0:TT, h, :], ALU.mult, ALU.mult).then_inc(stat2_ready, 1)
                v.wait_ge(base_ready, i)
                v.tensor_scalar(xn2[0:TT], xm[h][0:TT], ln_mv[0:TT, h, 0:1], ln_rs[0:TT, h, :], ALU.subtract, ALU.mult).then_inc(xn2_ready, 1)
                v.wait_ge(sd2_ready, 2 * i + 2)
                st.done(v.reciprocal(tiny[0:TT, 2:3], tiny[0:TT, 1:2]))
                v.wait_ge(t_out[h], 32 * t)
                v.wait_ge(xn2_ready, i + 1)
                v.scalar_tensor_tensor(tm[h][0:TT], xn2[0:TT], tiny[0:TT, 2:3], scale_b[0:TT], ALU.mult, ALU.mult).then_inc(t_ready, 1)

            def tt_lo(i):
                for b in range(2):
                    v.wait_ge(tt_hi, 2 * i + b + 1)
                    ins = v.tensor_tensor(tt[:, 1, 4 * b:4 * b + 4, :], bank[4 + b][:, 0:4 * TT].rearrange("p (k n) -> p k n", n=TT),
                                          tt[:, 0, 4 * b:4 * b + 4, :], ALU.subtract)
                ins.then_inc(tt_done, 1)

            def gate(i):
                v.wait_ge(gate_mm, START + i + 1)
                v.scalar_tensor_tensor(logits[0:TT, bass.ds(i, 1), :].rearrange("p a b -> p (a b)"), bank[6][0:TT, 0:E], 1.0 / (ST * SW), gate_bias[0:TT],
                                       ALU.mult, ALU.add).then_inc(gate_done, 1)
            def mix_period(i, t, h, attend=True, last=False):
                for half in range(2):
                    if attend:
                        for j in (4 * h + 2 * half, 4 * h + 2 * half + 1):
                            attend_unit(j, t + 1, PAIRS * (t + 1) + j)
                    add_half(i, h, half)
                if last:
                    mix_norm(i, t, h)
                if not isinstance(i, int) or i >= 2:
                    gate(i - 2)
                if not isinstance(i, int) or i >= 1:
                    tt_lo(i - 1)
                if not last:
                    mix_norm(i, t, h)
            mix_period(0, 0, 0)
            mix_period(1, 0, 1)
            with v.Fori(1, NT // 2 - 1) as t:
                st.enter(t - 1, 22)
                for h in range(2):
                    mix_period(2 * t + h, t, h)
            st.leave(NT // 2 - 2)
            for h in range(2):
                mix_period(NT - 2 + h, NT // 2 - 1, h, attend=False, last=(h == 1))
            gate(NT - 2)
            tt_lo(NT - 1)
            gate(NT - 1)

            v.wait_ge(gate_done, START + NT)
            v.wait_ge(route_iota, 4 + 2 * (E - 1))
            for i in range(NT):
                ins = v.max(top_v[0:TT, i, :], logits[0:TT, i, :])
            st.done(ins)
            for i in range(NT):
                ins = v.max_index(top_i[0:TT, i, :], top_v[0:TT, i, :], logits[0:TT, i, :])
            st.done(ins)
            v.tensor_tensor(pe_[0:TT], top_v[0:TT, :, 1], top_v[0:TT, :, 0], ALU.subtract).then_inc(route_exp, 1)
            st.done(v.tensor_copy(flat(idx_f[0:TT]), flat(top_i[0:TT])))
            for c in range(2):
                ins = v.tensor_tensor(oh[c][0:TT], e_iota[0:TT], idx_f[0:TT, :, c:c + 1].to_broadcast([TT, NT, E]), ALU.is_equal)
            st.done(ins)
            v.tensor_tensor(flat(both[0:TT]), flat(oh[0][0:TT]), flat(oh[1][0:TT]), ALU.add).then_inc(route_mm, 1)
            v.wait_ge(route_mm, 2)
            v.memset(pre[:, 0, :], 0.0)
            st.done(v.tensor_copy(flat(tot), bank[1][:, 0:NT * E]))
            for i in range(1, NT):
                st.done(v.tensor_tensor(pre[:, i, :], pre[:, i - 1, :], tot[:, i - 1, :], ALU.add))
            st.done(v.tensor_tensor(cnt, pre[:, NT - 1, :], tot[:, NT - 1, :], ALU.add))
            st.done(v.tensor_scalar(cnt_i, cnt, float(P - 1), None, ALU.add))
            st.done(v.tensor_scalar(cnt_i, cnt_i, 7, None, ALU.logical_shift_right))
            v.memset(cum[:, 0:1], 0.0)
            st.done(v.tensor_scalar(nblk, cnt_i, 1.0, None, ALU.max))
            for e in range(E):
                st.done(v.tensor_tensor(cum[:, e + 1:e + 2], cum[:, e:e + 1], nblk[:, e:e + 1], ALU.add))
            v.tensor_copy(base_i, cum)
            v.memset(offf[:, 1, :], 0.0)
            v.memset(offf[:, 0, :], float(slot_off[0] // 2))
            st.done(v.tensor_tensor(ge, b_iota.unsqueeze(2).to_broadcast([P, BLOCKS, E - 1]),
                                    cum[:, 1:E].unsqueeze(1).to_broadcast([P, BLOCKS, E - 1]), ALU.is_ge))
            st.done(v.tensor_reduce(expf, ge, AX.X, ALU.add))
            for c, to in enumerate((blk_i, bias_i)):
                st.done(v.tensor_tensor(moved, ge, moves[:, c:c + 1, :].to_broadcast([P, BLOCKS, E - 1]), ALU.mult))
                st.done(v.tensor_reduce(expf2, moved, AX.X, ALU.add))
                v.tensor_tensor(to, expf2, offf[:, c, :], ALU.add)
            st.done(v.tensor_copy(exp_i, expf))
            v.sem_inc(count_in, 1)
            for h in range(2):
                st.done(v.tensor_scalar(stores_i[:, h:h + 1], base_i[:, E - 1:E], float(1 - h), None, ALU.add))
            for k, (op, by) in enumerate(((ALU.logical_shift_right, 1), (ALU.logical_shift_left, 4))):
                st.done(v.tensor_scalar(stores_i, stores_i, by, None, op))
            st.done(v.tensor_tensor(flat(rank[0:TT]), bank[0][0:TT, 0:NT * E], flat(pre[0:TT]), ALU.add))
            st.done(v.scalar_tensor_tensor(rank[0:TT], cum[0:TT, 0:E].unsqueeze(1).to_broadcast([TT, NT, E]), float(P), rank[0:TT], ALU.mult, ALU.add))
            for c in range(2):
                st.done(v.tensor_tensor(flat(oh[c][0:TT]), flat(oh[c][0:TT]), flat(rank[0:TT]), ALU.mult))
                ins = v.tensor_reduce(slot_f[0:TT, c * NT:(c + 1) * NT], oh[c][0:TT], AX.X, ALU.add)
            st.done(ins)
            st.done(v.tensor_copy(slot_i[0:TT], slot_f[0:TT]))
            v.tensor_scalar(slot_p[0:TT, 0, :], slot_i[0:TT], P - 1, None, ALU.bitwise_and)
            st.done(v.tensor_scalar(slot_p[0:TT, 1, :], slot_i[0:TT], 7, None, ALU.logical_shift_right))
            st.done(v.tensor_copy(flat(slot_pf[0:TT]), flat(slot_p[0:TT])))
            v.tensor_tensor(place_hot[0:TT], place_iota[0:TT].unsqueeze(1).to_broadcast([TT, 2 * NT, P]),
                            slot_pf[0:TT, 0, :].unsqueeze(2).to_broadcast([TT, 2 * NT, P]), ALU.is_equal)
            st.done(v.tensor_tensor(block_hot[0:TT], b_iota[0:TT].unsqueeze(1).to_broadcast([TT, 2 * NT, BLOCKS]),
                                    slot_pf[0:TT, 1, :].unsqueeze(2).to_broadcast([TT, 2 * NT, BLOCKS]), ALU.is_equal))
            for c in range(2):
                ins = v.tensor_tensor(block_token[0:TT, c * NT:(c + 1) * NT], block_hot[0:TT, c * NT:(c + 1) * NT],
                                      token_f[0:TT].unsqueeze(2).to_broadcast([TT, NT, BLOCKS]), ALU.mult)
            ins.then_inc(slots_ready, 1)
            v.wait_ge(token_mm, 1)
            v.tensor_copy(tok_of, bank[4][:, 0:BLOCKS]).then_inc(tokens_ready, 1)
            v.wait_ge(pexp_in, 1)
            st.done(v.tensor_scalar(pden[0:TT], pe_[0:TT], 1.0, None, ALU.add))
            st.done(v.reciprocal(prob[0:TT, 0, :], pden[0:TT]))
            st.done(v.tensor_tensor(prob[0:TT, 1, :], pe_[0:TT], prob[0:TT, 0, :], ALU.mult))
            s0, s1 = slot_f[0:TT, 0:NT], slot_f[0:TT, NT:2 * NT]
            v.tensor_tensor(slot_first[0:TT], s0, s1, ALU.min)
            v.tensor_tensor(slot_second[0:TT], s0, s1, ALU.max)
            v.tensor_tensor(is_first[0:TT, 0, :], s0, s1, ALU.is_lt)
            st.done(v.tensor_tensor(is_first[0:TT, 1, :], s0, s1, ALU.is_gt))
            for to, c in ((p_first, 0), (p_second, 1)):
                for k in range(2):
                    ins = v.tensor_tensor(swap[0:TT, k, :], prob[0:TT, k, :], is_first[0:TT, (k + c) % 2, :], ALU.mult)
                st.done(ins)
                st.done(v.tensor_tensor(to[0:TT], swap[0:TT, 0, :], swap[0:TT, 1, :], ALU.add))

            def row_lo(b, s):
                for q in range(2):
                    v.wait_ge(rt_hi, 2 * b + q + 1)
                    ins = v.tensor_tensor(rowT[s][:, 1, 4 * q:4 * q + 4, :], bank[2 + 2 * s + q][:, :].rearrange("p (k n) -> p k n", n=P),
                                          rowT[s][:, 0, 4 * q:4 * q + 4, :], ALU.subtract)
                ins.then_inc(rt_done, 1)

            def swiglu(b):
                at = v.value_load(bias_i[0:1, bass.ds(b, 1)], min_val=0, max_val=2 * BIAS)
                v.wait_ge(h_mm, b + 1)
                v.scalar_tensor_tensor(hb, bank[6][:, :], 1.0 / (ST * SW), bias[:, bass.ds(at, 2 * HID)], ALU.mult, ALU.add).then_inc(h_evac, 1)
                v.wait_ge(h_evac, b + 1)
                pairs = hb.rearrange("p (j c) -> p j c", c=2)
                v.tensor_scalar(glu, pairs[:, :, 0], 7.0, None, ALU.min).then_inc(glu_ready, 1)
                st.done(v.tensor_scalar(lin, pairs[:, :, 1], -7.0, 7.0, ALU.max, ALU.min))
                st.done(v.scalar_tensor_tensor(lin, lin, 1.0, glu, ALU.add, ALU.mult))
                v.wait_ge(sg_ready, b + 1)
                v.wait_ge(at_psum, b)
                v.scalar_tensor_tensor(act, lin, SX, sg, ALU.mult, ALU.mult).then_inc(act_ready, 1)

            def act_lo(b):
                v.wait_ge(a_hi, b + 1)
                v.tensor_tensor(actT[:, 1, :, :], bank[7][:, 0:2 * P].rearrange("p (k n) -> p k n", n=P), actT[:, 0, :, :], ALU.subtract).then_inc(a_done, 1)

            def evac_y(b, s, q):
                at = v.value_load(bias_i[0:1, bass.ds(b, 1)], min_val=0, max_val=2 * BIAS)
                v.wait_ge(y_mm, b + 1)
                v.wait_ge(y_out[s], START + 16 * q)
                for half in range(2):
                    ins = v.scalar_tensor_tensor(ysb[s][:, half * 512:half * 512 + 512], bank[half][:, :], 1.0 / (SX * SW),
                                                 bias[:, bass.ds(at + 2 * HID + half * 512, 512)], ALU.mult, ALU.add)
                ins.then_inc(y_ready, 1)
            row_lo(0, 0)
            row_lo(1, 1)
            swiglu(0)
            with v.Fori(0, (BLOCKS - 3) // 2) as t:
                st.enter(t, 4)
                for h in range(2):
                    b = 2 * t + h + 1
                    row_lo(b + 1, h)
                    act_lo(b - 1)
                    swiglu(b)
                    evac_y(b - 1, h, t)
            st.leave((BLOCKS - 3) // 2)
            for b in range(BLOCKS - 2, BLOCKS):
                if b + 1 < BLOCKS:
                    row_lo(b + 1, (b + 1) % 2)
                act_lo(b - 1)
                swiglu(b)
                evac_y(b - 1, (b - 1) % 2, (b - 1) // 2)
            act_lo(BLOCKS - 1)
            evac_y(BLOCKS - 1, (BLOCKS - 1) % 2, (BLOCKS - 1) // 2)
            v.wait_ge(c_base_in, 32 * NT)
            v.wait_ge(first_in, 16 * NT)

            def add_first(i):
                o = cb[i][0:TT]
                st.done(v.scalar_tensor_tensor(o, first_rows[i][0:TT], p_first[0:TT, i:i + 1], o, ALU.mult, ALU.add))
            ahead = 6
            for i in range(ahead):
                add_first(i)
            for i in range(NT):
                v.wait_ge(c_in[i % 8], 16 * (i // 8 + 1))
                o = cb[i][0:TT]
                v.scalar_tensor_tensor(o, cy[i % 8][0:TT], p_second[0:TT, i:i + 1], o, ALU.mult, ALU.add).then_inc(c_done, 1)
                if i + ahead < NT:
                    add_first(i + ahead)


_OUT = (N, D)


def kernel(**inputs):
    import numpy as np
    import concourse.bacc as bacc
    from concourse.bass_utils import run_bass_kernel_spmd

    a = {k: np.ascontiguousarray(v) for k, v in inputs.items()}
    w_qkv = a["L0_mix_W_qkv"]
    wq = w_qkv[:, 0:D].reshape(KT, P, KT, P).transpose(2, 1, 0, 3)
    wq = wq.reshape(KT // 2, 2, P, D).transpose(0, 2, 1, 3).reshape(N_PIECE_Q, P, PIECE)
    wo = a["L0_mix_W_out"].reshape(N_PIECE_O, 2, P, D).transpose(0, 2, 1, 3).reshape(N_PIECE_O, P, PIECE)
    w1 = a["L0_ffn_mlp1_w"].reshape(E, 2, 4, P, 2 * HID).transpose(0, 1, 3, 2, 4).reshape(N_PIECE_1, P, PIECE)
    w2 = a["L0_ffn_mlp2_w"].reshape(E, 2, P, D).transpose(0, 2, 1, 3).reshape(N_PIECE_2, P, PIECE)
    arrays = {
        "x": a["x"], "src": a["src"], "dst": a["dst"], "edge_weight": a["edge_weight"],
        "gnn_bias": a["L0_gnn_bias"], "w_qkv": w_qkv,
        "qn_w": np.ascontiguousarray(a["L0_mix_qn_w"].reshape(KT, P).T), "kn_w": a["L0_mix_kn_w"],
        "w_flat": np.ascontiguousarray(np.concatenate([wq, wo, w1, w2])), "b_out": a["L0_mix_b_out"],
        "norm_scale": a["L0_ffn_norm_scale"],
        "gate_w": np.ascontiguousarray(a["L0_ffn_gate_w"].reshape(KT, P, E).transpose(1, 0, 2).reshape(P, KT * E)),
        "gate_b": a["L0_ffn_gate_b"], "mlp1_b": a["L0_ffn_mlp1_b"].reshape(-1), "mlp2_b": a["L0_ffn_mlp2_b"].reshape(-1),
    }
    nc = bacc.Bacc("TRN2", target_bir_lowering=False, num_devices=1)
    args = {k: nc.dram_tensor(f"in_{k}", v.shape, mybir.dt.from_np(v.dtype), kind="ExternalInput").ap() for k, v in arrays.items()}
    out = nc.dram_tensor("out_x", _OUT, F32, kind="ExternalOutput").ap()
    build_gps_layer(nc, **args, out=out)
    r = run_bass_kernel_spmd(nc, [{f"in_{k}": v for k, v in arrays.items()}], core_ids=[0])
    return r.results[0]["out_x"]
```
